# Optimizing a Trainium2 kernel written in Bass

```python
import numpy as np
import jax
import jax.numpy as jnp

def _softmax(x, axis=-1):
    return jax.nn.softmax(x, axis=axis)

def _gelu(x):
    return jax.nn.gelu(x, approximate=True)

def _silu(x):
    return jax.nn.silu(x)

def _sigmoid(x):
    return jax.nn.sigmoid(x)

def _layernorm(x, axis=-1, eps=1e-05):
    m = jnp.mean(x, axis=axis, keepdims=True)
    v = jnp.var(x, axis=axis, keepdims=True)
    return (x - m) / jnp.sqrt(v + eps)

def _scatter_add(tgt, idx, src, axis=0):
    return tgt.at[idx].add(src)

def _segment_sum(src, seg, n):
    return jax.ops.segment_sum(src, seg, n)
kernel_name = 'mk_decoder_preln_d2_seqx_r8_f06bf8'

def setup_inputs(seed: int=0):
    np.random.seed(seed)
    _w = jnp.asarray

    def _rec_inputs():
        import jax
        import jax.numpy as jnp
        _rk = jax.random.key(seed)
        x = -0.0003929 + 0.9999 * jax.random.normal(jax.random.fold_in(_rk, 1), (4, 256, 128), jnp.float32)
        _lenS = 256 - jax.random.randint(jax.random.fold_in(_rk, 7), (4,), 0, max(1, 256 // 4) + 1, jnp.int32)
        _lenS2 = 256 - jax.random.randint(jax.random.fold_in(_rk, 8), (4,), 0, max(1, 256 // 4) + 1, jnp.int32)
        _ctx_1024P = jax.random.normal(jax.random.fold_in(_rk, 11), (4, 16, 128), jnp.float32)
        _ctx_1024c = jax.random.dirichlet(jax.random.fold_in(_rk, 511), 0.3 * jnp.ones((16,), jnp.float32), (4, 256))
        _ctx_1024t = jnp.einsum('bsk,bkd->bsd', _ctx_1024c, _ctx_1024P)
        _ctx_1024t = _ctx_1024t * jax.lax.rsqrt(jnp.mean(jnp.square(_ctx_1024t)) + 1e-12) * 0.953939
        ctx_1024 = 2.81802e-05 + 1.00001 * (_ctx_1024t + 0.3 * jax.random.normal(jax.random.fold_in(_rk, 611), (4, 256, 128), jnp.float32))
        fside_BxSx4_0 = jax.random.uniform(jax.random.fold_in(_rk, 12), (4, 256, 4), jnp.float32, 0.0, 0.999884)
        return (x, ctx_1024, fside_BxSx4_0)
    x, ctx_1024, fside_BxSx4_0 = _rec_inputs()

    def _L0_attn_setup():
        import jax, jax.numpy as jnp
        import numpy as np
        from jax import lax
        D_MODEL = 128
        STATE_DIM = 128

        def _reference_tuple_inner(x, A, Bm, W_imp, W_ctx):
            B, S, D = x.shape
            xB = jnp.einsum('bsd,dn->bsn', x, Bm)

            def step(h, u_t):
                h = h @ A + u_t
                return (h, h)
            h0 = jnp.zeros((B, STATE_DIM), dtype=x.dtype)
            h_final, states = lax.scan(step, h0, jnp.swapaxes(xB, 0, 1))
            states = jnp.swapaxes(states, 0, 1)
            h_proj = h_final @ W_imp.T
            importance = jax.nn.softmax(jnp.einsum('bsd,bd->bs', x, h_proj), axis=-1)
            context = jnp.einsum('bsn,dn->bsd', states, W_ctx)
            return (importance, context)
        key = jax.random.key(seed)
        k_x, k_a, k_b, k_i, k_c = jax.random.split(key, 5)
        B, S = (4, 512)
        x = jax.random.normal(k_x, (B, S, D_MODEL), dtype=jnp.float32)
        A = jax.random.normal(k_a, (STATE_DIM, STATE_DIM), dtype=jnp.float32) * 0.01
        Bm = jax.random.normal(k_b, (D_MODEL, STATE_DIM), dtype=jnp.float32) * 0.01
        bound = 1.0 / np.sqrt(STATE_DIM)
        W_imp = jax.random.uniform(k_i, (D_MODEL, STATE_DIM), dtype=jnp.float32, minval=-bound, maxval=bound)
        W_ctx = jax.random.uniform(k_c, (D_MODEL, STATE_DIM), dtype=jnp.float32, minval=-bound, maxval=bound)
        return {'x': x, 'A': A, 'Bm': Bm, 'W_imp': W_imp, 'W_ctx': W_ctx}
    _L0_attn_all = _L0_attn_setup()
    _L0_attn_in = {k: v for k, v in _L0_attn_all.items() if k in ('A', 'Bm', 'W_imp', 'W_ctx')}
    del _L0_attn_all

    def _L0_xattn_setup():
        import jax, jax.numpy as jnp
        import numpy as np
        import math
        E = 128
        H = 16
        BS = 128
        G = 1
        D = E // H

        def _block_sparse_attn(Q, K, V):
            B, Hn, S, Dh = Q.shape
            nb = S // BS
            scale = 1.0 / math.sqrt(Dh)
            Qb = Q.reshape(B, Hn, nb, BS, Dh)
            Kb = K.reshape(B, Hn, nb, BS, Dh)
            Vb = V.reshape(B, Hn, nb, BS, Dh)
            loc_s = jnp.einsum('bhnqd,bhnkd->bhnqk', Qb, Kb) * scale
            loc_p = jax.nn.softmax(loc_s, axis=-1)
            out = jnp.einsum('bhnqk,bhnkd->bhnqd', loc_p, Vb)
            offs = jnp.arange(-G, G + 1)
            win = jnp.arange(nb)[:, None] + offs[None, :]
            valid = (win >= 0) & (win < nb)
            winc = jnp.clip(win, 0, nb - 1)
            W = 2 * G + 1
            Kw = Kb[:, :, winc].reshape(B, Hn, nb, W * BS, Dh)
            Vw = Vb[:, :, winc].reshape(B, Hn, nb, W * BS, Dh)
            cross_s = jnp.einsum('bhnqd,bhnkd->bhnqk', Qb, Kw) * scale
            kmask = jnp.repeat(valid, BS, axis=-1)
            cross_s = jnp.where(kmask[None, None, :, None, :], cross_s, -jnp.inf)
            cross_p = jax.nn.softmax(cross_s, axis=-1)
            out = out + jnp.einsum('bhnqk,bhnkd->bhnqd', cross_p, Vw)
            return out.reshape(B, Hn, S, Dh)
        key = jax.random.key(seed)
        ks = jax.random.split(key, 12)
        s = 1.0 / math.sqrt(E)
        inp = {'q': jax.random.normal(ks[0], (4, 512, E), jnp.float32), 'k': jax.random.normal(ks[1], (4, 512, E), jnp.float32), 'v': jax.random.normal(ks[2], (4, 512, E), jnp.float32), 'Wq': jax.random.uniform(ks[3], (E, E), jnp.float32, -s, s), 'bq': jax.random.uniform(ks[4], (E,), jnp.float32, -s, s), 'Wk': jax.random.uniform(ks[5], (E, E), jnp.float32, -s, s), 'bk': jax.random.uniform(ks[6], (E,), jnp.float32, -s, s), 'Wv': jax.random.uniform(ks[7], (E, E), jnp.float32, -s, s), 'bv': jax.random.uniform(ks[8], (E,), jnp.float32, -s, s), 'Wo': jax.random.uniform(ks[9], (E, E), jnp.float32, -s, s), 'bo': jax.random.uniform(ks[10], (E,), jnp.float32, -s, s)}
        return inp
    _L0_xattn_all = _L0_xattn_setup()
    _L0_xattn_in = {k: v for k, v in _L0_xattn_all.items() if k in ('Wq', 'bq', 'Wk', 'bk', 'Wv', 'bv', 'Wo', 'bo')}
    del _L0_xattn_all

    def _L0_ffn_setup():
        import jax, jax.numpy as jnp
        import numpy as np
        TOP_K = 2
        key = jax.random.key(seed)
        k1, k2, k3, k4 = jax.random.split(key, 4)
        B, N, D, E, F = (4, 256, 128, 8, 512)
        x = jax.random.normal(k1, (B, N, D), dtype=jnp.float32)
        gate_w = jax.random.normal(k2, (D, E), dtype=jnp.float32) * D ** (-0.5)
        w1 = jax.random.normal(k3, (E, D, F), dtype=jnp.float32) * D ** (-0.5)
        w2 = jax.random.normal(k4, (E, F, D), dtype=jnp.float32) * F ** (-0.5)
        return {'x': x, 'gate_w': gate_w, 'w1': w1, 'w2': w2}
    _L0_ffn_all = _L0_ffn_setup()
    _L0_ffn_in = {k: v for k, v in _L0_ffn_all.items() if k in ('gate_w', 'w1', 'w2')}
    del _L0_ffn_all

    def _L1_attn_setup():
        import jax, jax.numpy as jnp
        import numpy as np
        B, S, E, H = (2, 256, 128, 16)
        HD = E // H

        def _rope_tables(seq_len, head_dim, dtype=jnp.float32):
            i = jnp.arange(head_dim // 2, dtype=dtype)
            angles = jnp.power(jnp.asarray(10000.0, dtype), 2.0 * i / head_dim)
            theta = jnp.arange(seq_len, dtype=dtype)[:, None] * angles[None, :]
            cos = jnp.cos(theta)[None, :, None, :]
            sin = jnp.sin(theta)[None, :, None, :]
            return (cos, sin)

        def _apply_rope(t, cos, sin):
            tr, ti = (t[..., 0::2], t[..., 1::2])
            out_r = tr * cos - ti * sin
            out_i = tr * sin + ti * cos
            return jnp.stack([out_r, out_i], axis=-1).reshape(t.shape)
        key = jax.random.key(seed)
        ks = jax.random.split(key, 5)
        x = jax.random.normal(ks[0], (B, S, E), dtype=jnp.float32)
        w_q = jax.random.normal(ks[1], (H * HD, E), dtype=jnp.float32) * 0.02
        w_k = jax.random.normal(ks[2], (H * HD, E), dtype=jnp.float32) * 0.02
        w_v = jax.random.normal(ks[3], (H * HD, E), dtype=jnp.float32) * 0.02
        w_o = jax.random.normal(ks[4], (E, H * HD), dtype=jnp.float32) * 0.02
        return {'x': x, 'w_q': w_q, 'w_k': w_k, 'w_v': w_v, 'w_o': w_o}
    _L1_attn_all = _L1_attn_setup()
    _L1_attn_in = {k: v for k, v in _L1_attn_all.items() if k in ('w_q', 'w_k', 'w_v', 'w_o')}
    del _L1_attn_all

    def _L1_xattn_setup():
        import jax, jax.numpy as jnp
        import numpy as np
        D_MODEL = 128
        H = 16
        D_K = 64
        D_V = 64
        D_G = D_MODEL // H
        WAVE_LEN = 1000.0
        B = 8
        N = 64

        def box_relational_embedding(boxes, dim_g=D_G):
            x_min, y_min, x_max, y_max = jnp.split(boxes, 4, axis=-1)
            cx = (x_min + x_max) * 0.5
            cy = (y_min + y_max) * 0.5
            w = x_max - x_min + 1.0
            h = y_max - y_min + 1.0
            delta_x = jnp.log(jnp.clip(jnp.abs((cx - jnp.swapaxes(cx, 1, 2)) / w), 0.001, None))
            delta_y = jnp.log(jnp.clip(jnp.abs((cy - jnp.swapaxes(cy, 1, 2)) / h), 0.001, None))
            delta_w = jnp.log(w / jnp.swapaxes(w, 1, 2))
            delta_h = jnp.log(h / jnp.swapaxes(h, 1, 2))
            pos = jnp.stack([delta_x, delta_y, delta_w, delta_h], axis=-1)
            n_freq = dim_g // 8
            feat_range = jnp.arange(n_freq, dtype=jnp.float32)
            dim_mat = 1.0 / WAVE_LEN ** (feat_range / n_freq)
            mul = (100.0 * pos)[..., None] * dim_mat
            b, n = (pos.shape[0], pos.shape[1])
            mul = mul.reshape(b, n, n, 4 * n_freq)
            return jnp.concatenate([jnp.sin(mul), jnp.cos(mul)], axis=-1)
        key = jax.random.key(seed)
        ks = jax.random.split(key, 12)
        s = 0.02
        inp = {'queries': jax.random.normal(ks[0], (B, N, D_MODEL), jnp.float32), 'keys': jax.random.normal(ks[1], (B, N, D_MODEL), jnp.float32), 'values': jax.random.normal(ks[2], (B, N, D_MODEL), jnp.float32), 'boxes': jax.random.uniform(ks[3], (B, N, 4), jnp.float32), 'Wq': jax.random.normal(ks[4], (H * D_K, D_MODEL), jnp.float32) * s, 'bq': jnp.zeros((H * D_K,), jnp.float32), 'Wk': jax.random.normal(ks[5], (H * D_K, D_MODEL), jnp.float32) * s, 'bk': jnp.zeros((H * D_K,), jnp.float32), 'Wv': jax.random.normal(ks[6], (H * D_V, D_MODEL), jnp.float32) * s, 'bv': jnp.zeros((H * D_V,), jnp.float32), 'Wo': jax.random.normal(ks[7], (D_MODEL, H * D_V), jnp.float32) * s, 'bo': jnp.zeros((D_MODEL,), jnp.float32), 'Wg': jax.random.normal(ks[8], (H, D_G), jnp.float32) * s, 'bg': jnp.zeros((H,), jnp.float32)}
        return inp
    _L1_xattn_all = _L1_xattn_setup()
    _L1_xattn_in = {k: v for k, v in _L1_xattn_all.items() if k in ('Wq', 'bq', 'Wk', 'bk', 'Wv', 'bv', 'Wo', 'bo', 'Wg', 'bg')}
    del _L1_xattn_all

    def _L1_ffn_setup():
        import jax, jax.numpy as jnp
        import numpy as np
        D_MODEL = 128
        key = jax.random.key(seed)
        k_x, k_w, k_a1, k_a2 = jax.random.split(key, 4)
        x = jax.random.normal(k_x, (4, 256, D_MODEL), dtype=jnp.float32)
        weight = jax.random.normal(k_w, (D_MODEL, D_MODEL), dtype=jnp.float32) * 0.02
        aux_weight1 = jax.random.normal(k_a1, (D_MODEL, D_MODEL), dtype=jnp.float32) * 0.02
        aux_weight2 = jax.random.normal(k_a2, (D_MODEL, D_MODEL), dtype=jnp.float32) * 0.02
        bias = jnp.zeros((D_MODEL,), dtype=jnp.float32)
        return {'x': x, 'weight': weight, 'aux_weight1': aux_weight1, 'aux_weight2': aux_weight2, 'bias': bias}
    _L1_ffn_all = _L1_ffn_setup()
    _L1_ffn_in = {k: v for k, v in _L1_ffn_all.items() if k in ('weight', 'aux_weight1', 'aux_weight2', 'bias')}
    del _L1_ffn_all
    return {'x': x, 'ctx_1024': ctx_1024, 'fside_BxSx4_0': fside_BxSx4_0, 'L0_attn_A': _L0_attn_in['A'], 'L0_attn_Bm': _L0_attn_in['Bm'], 'L0_attn_W_imp': _L0_attn_in['W_imp'], 'L0_attn_W_ctx': _L0_attn_in['W_ctx'], 'L0_xattn_Wq': _L0_xattn_in['Wq'], 'L0_xattn_bq': _L0_xattn_in['bq'], 'L0_xattn_Wk': _L0_xattn_in['Wk'], 'L0_xattn_bk': _L0_xattn_in['bk'], 'L0_xattn_Wv': _L0_xattn_in['Wv'], 'L0_xattn_bv': _L0_xattn_in['bv'], 'L0_xattn_Wo': _L0_xattn_in['Wo'], 'L0_xattn_bo': _L0_xattn_in['bo'], 'L0_ffn_gate_w': _L0_ffn_in['gate_w'], 'L0_ffn_w1': _L0_ffn_in['w1'], 'L0_ffn_w2': _L0_ffn_in['w2'], 'L1_attn_w_q': _L1_attn_in['w_q'], 'L1_attn_w_k': _L1_attn_in['w_k'], 'L1_attn_w_v': _L1_attn_in['w_v'], 'L1_attn_w_o': _L1_attn_in['w_o'], 'L1_xattn_Wq': _L1_xattn_in['Wq'], 'L1_xattn_bq': _L1_xattn_in['bq'], 'L1_xattn_Wk': _L1_xattn_in['Wk'], 'L1_xattn_bk': _L1_xattn_in['bk'], 'L1_xattn_Wv': _L1_xattn_in['Wv'], 'L1_xattn_bv': _L1_xattn_in['bv'], 'L1_xattn_Wo': _L1_xattn_in['Wo'], 'L1_xattn_bo': _L1_xattn_in['bo'], 'L1_xattn_Wg': _L1_xattn_in['Wg'], 'L1_xattn_bg': _L1_xattn_in['bg'], 'L1_ffn_weight': _L1_ffn_in['weight'], 'L1_ffn_aux_weight1': _L1_ffn_in['aux_weight1'], 'L1_ffn_aux_weight2': _L1_ffn_in['aux_weight2'], 'L1_ffn_bias': _L1_ffn_in['bias']}

def reference(x, ctx_1024, fside_BxSx4_0, L0_attn_A, L0_attn_Bm, L0_attn_W_imp, L0_attn_W_ctx, L0_xattn_Wq, L0_xattn_bq, L0_xattn_Wk, L0_xattn_bk, L0_xattn_Wv, L0_xattn_bv, L0_xattn_Wo, L0_xattn_bo, L0_ffn_gate_w, L0_ffn_w1, L0_ffn_w2, L1_attn_w_q, L1_attn_w_k, L1_attn_w_v, L1_attn_w_o, L1_xattn_Wq, L1_xattn_bq, L1_xattn_Wk, L1_xattn_bk, L1_xattn_Wv, L1_xattn_bv, L1_xattn_Wo, L1_xattn_bo, L1_xattn_Wg, L1_xattn_bg, L1_ffn_weight, L1_ffn_aux_weight1, L1_ffn_aux_weight2, L1_ffn_bias):
    import jax
    import jax.numpy as jnp

    def _L0_attn_ref(x, A, Bm, W_imp, W_ctx):
        import jax, jax.numpy as jnp
        import numpy as np
        from jax import lax
        D_MODEL = 128
        STATE_DIM = 128

        def _reference_tuple_inner(x, A, Bm, W_imp, W_ctx):
            B, S, D = x.shape
            xB = jnp.einsum('bsd,dn->bsn', x, Bm)

            def step(h, u_t):
                h = h @ A + u_t
                return (h, h)
            h0 = jnp.zeros((B, STATE_DIM), dtype=x.dtype)
            h_final, states = lax.scan(step, h0, jnp.swapaxes(xB, 0, 1))
            states = jnp.swapaxes(states, 0, 1)
            h_proj = h_final @ W_imp.T
            importance = jax.nn.softmax(jnp.einsum('bsd,bd->bs', x, h_proj), axis=-1)
            context = jnp.einsum('bsn,dn->bsd', states, W_ctx)
            return (importance, context)
        return _reference_tuple_inner(x, A, Bm, W_imp, W_ctx)[1]

    def _L0_xattn_ref(q, k, v, Wq, bq, Wk, bk, Wv, bv, Wo, bo):
        import jax, jax.numpy as jnp
        import numpy as np
        import math
        E = 128
        H = 16
        BS = 128
        G = 1
        D = E // H

        def _block_sparse_attn(Q, K, V):
            B, Hn, S, Dh = Q.shape
            nb = S // BS
            scale = 1.0 / math.sqrt(Dh)
            Qb = Q.reshape(B, Hn, nb, BS, Dh)
            Kb = K.reshape(B, Hn, nb, BS, Dh)
            Vb = V.reshape(B, Hn, nb, BS, Dh)
            loc_s = jnp.einsum('bhnqd,bhnkd->bhnqk', Qb, Kb) * scale
            loc_p = jax.nn.softmax(loc_s, axis=-1)
            out = jnp.einsum('bhnqk,bhnkd->bhnqd', loc_p, Vb)
            offs = jnp.arange(-G, G + 1)
            win = jnp.arange(nb)[:, None] + offs[None, :]
            valid = (win >= 0) & (win < nb)
            winc = jnp.clip(win, 0, nb - 1)
            W = 2 * G + 1
            Kw = Kb[:, :, winc].reshape(B, Hn, nb, W * BS, Dh)
            Vw = Vb[:, :, winc].reshape(B, Hn, nb, W * BS, Dh)
            cross_s = jnp.einsum('bhnqd,bhnkd->bhnqk', Qb, Kw) * scale
            kmask = jnp.repeat(valid, BS, axis=-1)
            cross_s = jnp.where(kmask[None, None, :, None, :], cross_s, -jnp.inf)
            cross_p = jax.nn.softmax(cross_s, axis=-1)
            out = out + jnp.einsum('bhnqk,bhnkd->bhnqd', cross_p, Vw)
            return out.reshape(B, Hn, S, Dh)
        B, S, _ = q.shape

        def proj(x, Wm, bm):
            y = jnp.einsum('bse,fe->bsf', x, Wm) + bm
            return y.reshape(B, S, H, D).transpose(0, 2, 1, 3)
        Q = proj(q, Wq, bq)
        K = proj(k, Wk, bk)
        V = proj(v, Wv, bv)
        attn = _block_sparse_attn(Q, K, V)
        attn = attn.transpose(0, 2, 1, 3).reshape(B, S, E)
        return jnp.einsum('bse,fe->bsf', attn, Wo) + bo

    def _L0_ffn_ref(x, gate_w, w1, w2):
        import jax, jax.numpy as jnp
        import numpy as np
        TOP_K = 2
        E = gate_w.shape[-1]
        gate_logits = jnp.einsum('bnd,de->bne', x, gate_w)
        gate_probs = jax.nn.softmax(gate_logits, axis=-1)
        top_k_probs, top_k_idx = jax.lax.top_k(gate_probs, TOP_K)
        top_k_weights = top_k_probs / jnp.sum(top_k_probs, axis=-1, keepdims=True)
        comb = jnp.sum(jax.nn.one_hot(top_k_idx, E, dtype=x.dtype) * top_k_weights[..., None], axis=2)
        h = jax.nn.gelu(jnp.einsum('bnd,edf->benf', x, w1))
        expert_out = jnp.einsum('benf,efd->bend', h, w2)
        output = jnp.einsum('bne,bend->bnd', comb, expert_out)
        return output

    def _L1_attn_ref(x, w_q, w_k, w_v, w_o):
        import jax, jax.numpy as jnp
        import numpy as np
        B, S, E, H = (2, 256, 128, 16)
        HD = E // H

        def _rope_tables(seq_len, head_dim, dtype=jnp.float32):
            i = jnp.arange(head_dim // 2, dtype=dtype)
            angles = jnp.power(jnp.asarray(10000.0, dtype), 2.0 * i / head_dim)
            theta = jnp.arange(seq_len, dtype=dtype)[:, None] * angles[None, :]
            cos = jnp.cos(theta)[None, :, None, :]
            sin = jnp.sin(theta)[None, :, None, :]
            return (cos, sin)

        def _apply_rope(t, cos, sin):
            tr, ti = (t[..., 0::2], t[..., 1::2])
            out_r = tr * cos - ti * sin
            out_i = tr * sin + ti * cos
            return jnp.stack([out_r, out_i], axis=-1).reshape(t.shape)
        b, s, _ = x.shape
        q = (x @ w_q.T).reshape(b, s, H, HD)
        k = (x @ w_k.T).reshape(b, s, H, HD)
        v = (x @ w_v.T).reshape(b, s, H, HD)
        cos, sin = _rope_tables(s, HD, x.dtype)
        q = _apply_rope(q, cos, sin)
        k = _apply_rope(k, cos, sin)
        att = jnp.einsum('bqhd,bkhd->bhqk', q, k) / jnp.sqrt(jnp.asarray(HD, x.dtype))
        att = jax.nn.softmax(att, axis=-1)
        y = jnp.einsum('bhqk,bkhd->bqhd', att, v).reshape(b, s, H * HD)
        return y @ w_o.T

    def _L1_xattn_ref(queries, keys, values, boxes, Wq, bq, Wk, bk, Wv, bv, Wo, bo, Wg, bg):
        import jax, jax.numpy as jnp
        import numpy as np
        D_MODEL = 128
        H = 16
        D_K = 64
        D_V = 64
        D_G = D_MODEL // H
        WAVE_LEN = 1000.0
        B = 8
        N = 64

        def box_relational_embedding(boxes, dim_g=D_G):
            x_min, y_min, x_max, y_max = jnp.split(boxes, 4, axis=-1)
            cx = (x_min + x_max) * 0.5
            cy = (y_min + y_max) * 0.5
            w = x_max - x_min + 1.0
            h = y_max - y_min + 1.0
            delta_x = jnp.log(jnp.clip(jnp.abs((cx - jnp.swapaxes(cx, 1, 2)) / w), 0.001, None))
            delta_y = jnp.log(jnp.clip(jnp.abs((cy - jnp.swapaxes(cy, 1, 2)) / h), 0.001, None))
            delta_w = jnp.log(w / jnp.swapaxes(w, 1, 2))
            delta_h = jnp.log(h / jnp.swapaxes(h, 1, 2))
            pos = jnp.stack([delta_x, delta_y, delta_w, delta_h], axis=-1)
            n_freq = dim_g // 8
            feat_range = jnp.arange(n_freq, dtype=jnp.float32)
            dim_mat = 1.0 / WAVE_LEN ** (feat_range / n_freq)
            mul = (100.0 * pos)[..., None] * dim_mat
            b, n = (pos.shape[0], pos.shape[1])
            mul = mul.reshape(b, n, n, 4 * n_freq)
            return jnp.concatenate([jnp.sin(mul), jnp.cos(mul)], axis=-1)
        b, nq, _ = queries.shape
        nk = keys.shape[1]
        emb = box_relational_embedding(boxes)
        g = jax.nn.relu(jnp.einsum('bnmd,hd->bhnm', emb, Wg) + bg[None, :, None, None])
        q = (queries @ Wq.T + bq).reshape(b, nq, H, D_K).transpose(0, 2, 1, 3)
        k = (keys @ Wk.T + bk).reshape(b, nk, H, D_K).transpose(0, 2, 1, 3)
        v = (values @ Wv.T + bv).reshape(b, nk, H, D_V).transpose(0, 2, 1, 3)
        a = jnp.einsum('bhqd,bhkd->bhqk', q, k) / jnp.sqrt(jnp.float32(D_K))
        mn = jax.nn.softmax(jnp.log(jnp.clip(g, 1e-06, None)) + a, axis=-1)
        out = jnp.einsum('bhqk,bhkd->bqhd', mn, v).reshape(b, nq, H * D_V)
        return out @ Wo.T + bo

    def _L1_ffn_ref(x, weight, aux_weight1, aux_weight2, bias):
        import jax, jax.numpy as jnp
        import numpy as np
        D_MODEL = 128
        h = jnp.einsum('btc,cd->btd', x, weight)
        h = jnp.einsum('btc,cd->btd', h, aux_weight1)
        h = jnp.einsum('btc,cd->btd', h, aux_weight2)
        return jnp.tanh(h + bias)
    x = x + _L0_attn_ref(_layernorm(x, axis=-1), L0_attn_A, L0_attn_Bm, L0_attn_W_imp, L0_attn_W_ctx)
    x = x + _L0_xattn_ref(_layernorm(x, axis=-1), ctx_1024, ctx_1024, L0_xattn_Wq, L0_xattn_bq, L0_xattn_Wk, L0_xattn_bk, L0_xattn_Wv, L0_xattn_bv, L0_xattn_Wo, L0_xattn_bo)
    x = x + _L0_ffn_ref(_layernorm(x, axis=-1), L0_ffn_gate_w, L0_ffn_w1, L0_ffn_w2)
    x = x + _L1_attn_ref(_layernorm(x, axis=-1), L1_attn_w_q, L1_attn_w_k, L1_attn_w_v, L1_attn_w_o)
    x = x + _L1_xattn_ref(_layernorm(x, axis=-1), ctx_1024, ctx_1024, fside_BxSx4_0, L1_xattn_Wq, L1_xattn_bq, L1_xattn_Wk, L1_xattn_bk, L1_xattn_Wv, L1_xattn_bv, L1_xattn_Wo, L1_xattn_bo, L1_xattn_Wg, L1_xattn_bg)
    x = x + _L1_ffn_ref(_layernorm(x, axis=-1), L1_ffn_weight, L1_ffn_aux_weight1, L1_ffn_aux_weight2, L1_ffn_bias)
    return x

_drawn_inputs = setup_inputs


def setup_inputs(seed=0):
    import zlib

    import numpy as np

    out = dict(_drawn_inputs(seed))
    spreads = {'L1_xattn_bq': (0.0, 0.8),
     'L1_xattn_bk': (0.0, 0.8),
     'L1_xattn_bv': (0.0, 0.1),
     'L1_xattn_bo': (0.0, 0.1),
     'L1_xattn_bg': (0.0, 0.1),
     'L1_ffn_bias': (0.0, 0.1)}
    factors = {'L0_xattn_bq': 3.025,
     'L0_xattn_bk': 8.0,
     'L1_attn_w_q': 8.0,
     'L1_attn_w_k': 8.0,
     'L1_attn_w_v': 4.997,
     'L1_attn_w_o': 4.934,
     'L1_xattn_Wq': 8.0,
     'L1_xattn_Wk': 8.0,
     'L1_ffn_weight': 5.808,
     'L1_ffn_aux_weight1': 5.723,
     'L1_ffn_aux_weight2': 5.858}
    for name, (base, spread) in spreads.items():
        noise = np.random.default_rng([zlib.crc32(name.encode()), seed]).standard_normal(out[name].shape)
        drawn = base * np.exp(spread * noise) if base else spread * noise
        out[name] = jnp.asarray(drawn.astype(out[name].dtype))
    for name, factor in factors.items():
        out[name] = (out[name] * factor).astype(out[name].dtype)
    return out
```

```python
from contextlib import ExitStack

import concourse.bass as bass
import numpy as np
from concourse import mybir

F32 = mybir.dt.float32
BF16 = mybir.dt.bfloat16
I32 = mybir.dt.int32
ALU = mybir.AluOpType
ACT = mybir.ActivationFunctionType
AX_X = mybir.AxisListType.X

B, S, D = 4, 256, 128
T = B * S
P = 128
NT = T // P
KB = S // P
H = 16
HD = D // H
G = 4
NG = H // G
HS = P // G
E, F = 8, 512
FC = F // P
DK = 64
NC = H * DK // P
EPS = 1e-5
RSQRT_GUESS = float(0x5F3759DF)

WEIGHTS = [("A", P), ("A_T", P), ("Bm", P), ("W_ctx_T", P), ("wq0", NG * P), ("wk0", NG * P),
           ("wv0", P), ("wo0", P), ("gate", E), ("wq1", P), ("wk1", P), ("wv1", P), ("wo1", P),
           ("ffn1", P), ("ffn2", P), ("ffn3", P), ("bq0", NG), ("bk0", 2 * NG), ("bq2", NC), ("bk2", NC)]
WIDE = [("wq2", H * DK), ("wk2", H * DK), ("wv2", H * DK), ("wo2", H * DK)]
ROWS = [("bv0", D), ("bo0", D), ("bo2", D), ("ffn_b", D), ("bv2", H * DK)]
CONSTS = [("ident", P), ("cos", KB * P), ("sin", KB * P), ("rank", E)]


def columns(parts):
    at, out = 0, {}
    for name, n in parts:
        out[name] = slice(at, at + n)
        at += n
    return out, at


W_AT, W_COLS = columns(WEIGHTS)
WIDE_AT, WIDE_COLS = columns(WIDE)
ROW_AT, ROW_COLS = columns(ROWS)
CONST_AT, CONST_COLS = columns(CONSTS)


class Parts:
    pass


class Link:

    def __init__(self, eng, sem):
        self.eng, self.sem, self.n = eng, sem, 0

    def __call__(self, ins):
        self.n += 1
        ins.then_inc(self.sem, 1)
        self.eng.wait_ge(self.sem, self.n)


def half(t4):
    return slice(t4 * 512, t4 * 512 + 512)


def tile(t):
    return slice(t * P, t * P + P)



def norm_sems(k, name):
    s = Parts()
    s.norm_step = k.sem(f"{name}_norm_step")
    s.z_ready = k.sem(f"{name}_z_ready")
    s.zT_in_psum = k.sem(f"{name}_zT_in_psum")
    s.zT_lo = k.sem(f"{name}_zT_lo")
    s.zT_hi = k.sem(f"{name}_zT_hi")
    return s


def norm_vector(dve, k, s):
    step = Link(dve, s.norm_step)
    for t in range(NT):
        ins = dve.bn_stats(k.stats[:, t, :], k.x[:, t, :])
    step(ins)
    for t in range(NT):
        ins = dve.bn_aggr(k.mv[:, t, :], k.stats[:, t, :])
    step(ins)
    step(dve.tensor_scalar(k.var[:, :], k.mv[:, :, 1], EPS, None, ALU.add))
    step(dve.tensor_scalar(k.rstd[:, :].bitcast(I32), k.var[:, :].bitcast(I32), -0.5, RSQRT_GUESS,
                           ALU.mult, ALU.add))
    for _ in range(3):
        step(dve.tensor_tensor(k.newton[:, :], k.rstd[:, :], k.rstd[:, :], ALU.mult))
        step(dve.scalar_tensor_tensor(out=k.newton[:, :], in0=k.newton[:, :], scalar=-0.5, in1=k.var[:, :],
                                      op0=ALU.mult, op1=ALU.mult))
        step(dve.scalar_tensor_tensor(out=k.rstd[:, :], in0=k.newton[:, :], scalar=1.5, in1=k.rstd[:, :],
                                      op0=ALU.add, op1=ALU.mult))
    for t in range(NT):
        dve.tensor_scalar(k.z[:, t, :], k.x[:, t, :], k.mv[:, t, 0:1], k.rstd[:, t:t + 1],
                          ALU.subtract, ALU.mult).then_inc(s.z_ready, 1)
    dve.wait_ge(s.zT_in_psum, NT // 2)
    dve.tensor_copy(k.zT[:, half(0)], k.ps[:, 0, :]).then_inc(s.zT_lo, 1)


def norm_tensor(pe, k, s):
    for t in range(NT):
        pe.wait_ge(s.z_ready, t + 1)
        pe.transpose(k.ps[:, t // 4, tile(t % 4)], k.z[:, t, :], k.ident).then_inc(s.zT_in_psum, 1)


def norm_scalar(act, k, s):
    act.wait_ge(s.zT_in_psum, NT)
    act.activation(k.zT[:, half(1)], k.ps[:, 1, :], ACT.Copy).then_inc(s.zT_hi, 1)


def wait_zT(eng, s):
    eng.wait_ge(s.zT_lo, 1)
    eng.wait_ge(s.zT_hi, 1)



def load_phase(nc, k, ins):
    with nc.Block() as block:
        @block.sync
        def _(sp):
            sp.dma_start(k.x[:, :, :], ins["x"].rearrange("(t p) d -> p t d", p=P)).then_inc(k.x_loaded, 16)
            sp.dma_start(k.const[:, :], ins["const"]).then_inc(k.const_loaded, 16)
            sp.dma_start(k.weights[:, :], ins["weights"]).then_inc(k.weights_loaded, 16)
            sp.dma_start(k.ctxT[:, :], ins["ctx_T"]).then_inc(k.ctx_loaded, 16)
            sp.dma_start(k.rows[:, :], ins["rows"].partition_broadcast(P)).then_inc(k.rows_loaded, 16)
            sp.dma_start(k.wide[:, :], ins["wide"]).then_inc(k.wide_loaded, 16)



LEVELS = S.bit_length() - 1


def scan_phase(nc, k):
    s = norm_sems(k, "scan")
    power_step = k.sem("scan_power_in_psum")
    power_dve = k.sem("scan_power_copied")
    power_act = k.sem("scan_power_T_copied")
    level_done = [k.sem(f"scan_level_done_{i}") for i in range(2)]
    copied = [k.sem(f"scan_copied_{i}") for i in range(2)]
    out_ready = k.sem("scan_out_ready")
    W = k.w
    with ExitStack() as ctx:
        powers = ctx.enter_context(nc.sbuf_tensor("powers", [P, LEVELS, 2, P], F32))
        hs = ctx.enter_context(nc.sbuf_tensor("scan_h", [P, T], F32))
        block = ctx.enter_context(nc.Block())

        def power(level, transposed):
            if level == 0:
                return W["A_T" if transposed else "A"]
            return powers[:, level, transposed, :]

        @block.vector
        def _(dve):
            dve.wait_ge(k.x_loaded, 16)
            norm_vector(dve, k, s)
            for level in range(1, LEVELS):
                dve.wait_ge(power_step, level)
                dve.tensor_copy(powers[:, level, 0, :], k.ps[:, 6, 0:P]).then_inc(power_dve, 1)
            for level in range(LEVELS + 1):
                dve.wait_ge(level_done[0], level + 1)
                dve.tensor_copy(hs[:, half(0)], k.ps[:, 2, :]).then_inc(copied[0], 1)
            dve.wait_ge(out_ready, 1)
            dve.tensor_tensor(k.x[:, 0:4, :], k.x[:, 0:4, :], k.ps[:, 4, :].rearrange("p (t d) -> p t d", d=D), ALU.add)
            dve.wait_ge(out_ready, 2)
            dve.tensor_tensor(k.x[:, 4:8, :], k.x[:, 4:8, :], k.ps[:, 5, :].rearrange("p (t d) -> p t d", d=D), ALU.add)

        @block.scalar
        def _(act):
            norm_scalar(act, k, s)
            for level in range(1, LEVELS):
                act.wait_ge(power_step, level)
                act.activation(powers[:, level, 1, :], k.ps[:, 7, 0:P], ACT.Copy).then_inc(power_act, 1)
            for level in range(LEVELS + 1):
                act.wait_ge(level_done[1], level + 1)
                act.activation(hs[:, half(1)], k.ps[:, 3, :], ACT.Copy).then_inc(copied[1], 1)

        @block.tensor
        def _(pe):
            pe.wait_ge(k.const_loaded, 16)
            norm_tensor(pe, k, s)
            pe.wait_ge(k.weights_loaded, 16)

            def square(level):
                if level > 1:
                    pe.wait_ge(power_dve, level - 1)
                    pe.wait_ge(power_act, level - 1)
                pe.matmul(k.ps[:, 6, 0:P], power(level - 1, 1), power(level - 1, 0), start=True, stop=True)
                pe.matmul(k.ps[:, 7, 0:P], power(level - 1, 0), power(level - 1, 1), start=True,
                          stop=True).then_inc(power_step, 1)

            for level in range(1, LEVELS):
                square(level)
            wait_zT(pe, s)
            for i in range(2):
                pe.matmul(k.ps[:, 2 + i, :], W["Bm"], k.zT[:, half(i)], start=True, stop=True,
                          skip_group_check=True).then_inc(level_done[i], 1)
            pe.wait_ge(power_dve, LEVELS - 1)
            for level in range(LEVELS):
                shift = 1 << level
                for i in range(2):
                    pe.wait_ge(copied[i], level + 1)
                    for b in range(2):
                        at = b * S
                        mm = pe.matmul(k.ps[:, 2 + i, at + shift:at + S], power(level, 0),
                                       hs[:, i * 512 + at:i * 512 + at + S - shift], start=False, stop=True,
                                       skip_group_check=True)
                    mm.then_inc(level_done[i], 1)
            for i in range(2):
                pe.wait_ge(copied[i], LEVELS + 1)
                for t in range(4):
                    mm = pe.matmul(k.ps[:, 4 + i, tile(t)], hs[:, tile(4 * i + t)], W["W_ctx_T"],
                                   start=True, stop=True)
                mm.then_inc(out_ready, 1)



def narrow_sems(k, name):
    s = norm_sems(k, name)
    s.proj_ready = k.sem(f"{name}_proj_ready")
    s.bias_added = k.sem(f"{name}_bias_added")
    s.q_copied = k.sem(f"{name}_q_copied")
    s.k_copied = k.sem(f"{name}_k_copied")
    s.v_copied = k.sem(f"{name}_v_copied")
    s.scores_ready = k.sem(f"{name}_scores_ready")
    s.max_ready = k.sem(f"{name}_max_ready")
    s.maxT_ready = k.sem(f"{name}_maxT_ready")
    s.q_shifted = k.sem(f"{name}_q_shifted")
    s.scoresT_ready = k.sem(f"{name}_scoresT_ready")
    s.exp_ready = k.sem(f"{name}_exp_ready")
    s.pv_ready = k.sem(f"{name}_pv_ready")
    s.pv_copied = k.sem(f"{name}_pv_copied")
    s.outT_ready = k.sem(f"{name}_outT_ready")
    s.mix_step = k.sem(f"{name}_mix_step")
    s.diff_ready = k.sem(f"{name}_diff_ready")
    s.mix_weights = k.sem(f"{name}_mix_weights")
    s.att_ready = k.sem(f"{name}_att_ready")
    s.attT_ready = k.sem(f"{name}_attT_ready")
    s.attT_lo = k.sem(f"{name}_attT_lo")
    s.attT_hi = k.sem(f"{name}_attT_hi")
    s.out_ready = k.sem(f"{name}_out_ready")
    s.prep = k.sem(f"{name}_prep")
    return s


def narrow_buffers(nc, ctx, sublayer):
    def sb(name, shape):
        return ctx.enter_context(nc.sbuf_tensor(f"{sublayer}_{name}", shape, F32))
    n = Parts()
    n.q = sb("q", [P, NG, T])
    n.k = sb("k", [P, NG, T])
    n.v = sb("v", [P, NT, H, HS])
    n.top = sb("top", [P, NT, NG, P])
    n.e = sb("e", [P, 2, G, 2, S])
    n.oT = sb("oT", [P, 2, NG, KB, S])
    n.att = sb("att", [P, NT, D])
    n.tmp = sb("products", [P, 2, NG, G, HD])
    n.mw = sb("block_weights", [P, NT, 2, H])
    n.mf = sb("factors", [P, 2, H])
    n.mt = sb("mix_tmp", [P, 2, H])
    n.ml = sb("mix_sum", [P, H])
    return n



def slot_heads(i):
    return [(g, gi) for g in (2 * (i % 2), 2 * (i % 2) + 1) for gi in (i // 2 % 2 * 2, i // 2 % 2 * 2 + 1)]


def first_pass_tensor(pe, k, n, s):
    def shift(t):
        pe.wait_ge(s.max_ready, NG * (t + 1))
        if t >= 2:
            pe.wait_ge(s.q_shifted, t - 1)
        for gi in range(NG):
            mm = pe.transpose(k.ps[:, 4 + t % 2, tile(gi)], n.top[:, t, gi, :], k.ident)
        mm.then_inc(s.maxT_ready, 1)

    for t in range(NT):
        b = t // KB
        for i in range(4 * t, 4 * t + 4):
            if i >= 2:
                pe.wait_ge(s.max_ready, i - 1)
            for g, gi in slot_heads(i):
                rows = slice(HS * g, HS * g + HS)
                mm = pe.matmul(k.ps[:, g, (gi % 2) * S:(gi % 2) * S + S],
                               n.q[rows, gi, tile(t)], n.k[rows, gi, b * S:b * S + S], start=True, stop=True)
            mm.then_inc(s.scores_ready, 1)
        if t >= 1:
            shift(t - 1)
    shift(NT - 1)


def first_pass_vector(dve, k, n, s, kinds):
    def shift(t):
        dve.wait_ge(s.maxT_ready, t + 1)
        dve.tensor_tensor(n.q[:, :, tile(t)], n.q[:, :, tile(t)],
                          k.ps[:, 4 + t % 2, :].rearrange("p (g c) -> p g c", c=P), ALU.subtract)\
           .then_inc(s.q_shifted, 1)

    for t in range(NT):
        for i in range(4 * t, 4 * t + 4):
            dve.wait_ge(s.scores_ready, i + 1)
            place, group = slot_heads(i)[0]
            top = n.top[:, t, group:group + 2, :].rearrange("p a (g c) -> p g a c", g=G)[
                :, place:place + 2, :, HD:HD + kinds]
            scores = k.ps[:, place:place + 2, :].rearrange("p g (a j c) -> p g a j c", a=2, j=kinds)
            dve.tensor_reduce(top, scores, AX_X, ALU.max).then_inc(s.max_ready, 1)
        if t >= 1:
            shift(t - 1)
    shift(NT - 1)


def second_pass_tensor(pe, k, n, s, kinds):
    def scores(j):
        b, kb = j // 8, j // 2 % 2
        if j >= 2:
            pe.wait_ge(s.exp_ready, j - 1)
        for g, gi in slot_heads(j // 4 * 2 + j % 2):
            rows = slice(HS * g, HS * g + HS)
            mm = pe.matmul(k.ps[:, g, (gi % 2) * S:(gi % 2) * S + S],
                           n.k[rows, gi, tile(b * KB + kb)], n.q[rows, gi, b * S:b * S + S], start=True, stop=True)
        mm.then_inc(s.scoresT_ready, 1)

    def values(r):
        b, pair, kb = r // 4, r // 2 % 2, r % 2
        pe.wait_ge(s.exp_ready, 2 * (r + 1))
        if kb == 0 and r >= 2:
            pe.wait_ge(s.pv_copied, r // 2)
        at = kb * S if kinds == 2 else 0
        for i in range(2):
            for g in range(G):
                mm = pe.matmul(k.ps[HS * g:HS * g + HS, 4 + i, at:at + S], n.v[:, b * KB + kb, G * (2 * pair + i) + g, :],
                               n.e[:, r % 2, g, i, :], start=(kb == 0 or kinds == 2), stop=(kb == 1 or kinds == 2),
                               skip_group_check=True)
        mm.then_inc(s.pv_ready, 1)

    def turn(b):
        pe.wait_ge(s.pv_copied, 2 * (b + 1))
        for i in range(KB):
            t = b * KB + i
            if t >= 1:
                pe.wait_ge(s.att_ready, t)
            for gi in range(NG):
                for kd in range(kinds):
                    mm = pe.transpose(k.ps[:, 6 + gi // 2, ((gi % 2) * 2 + kd) * P:((gi % 2) * 2 + kd) * P + P],
                                      n.oT[:, b % 2, gi, kd, tile(i)], k.ident)
            mm.then_inc(s.outT_ready, 1)

    rounds = B * 4
    pe.wait_ge(s.q_shifted, NT)
    for r in range(rounds):
        scores(2 * r)
        scores(2 * r + 1)
        if r >= 1:
            values(r - 1)
        if r >= 4 and r % 4 == 1:
            turn(r // 4 - 1)
    values(rounds - 1)
    turn(B - 1)


def second_pass_scalar(act, k, n, s, scale):
    for j in range(B * NG * KB):
        r, places = j // 2, slice(2 * (j % 2), 2 * (j % 2) + 2)
        act.wait_ge(s.scoresT_ready, j + 1)
        if r >= 2:
            act.wait_ge(s.pv_ready, r - 1)
        act.activation(n.e[:, r % 2, places, :, :], k.ps[:, places, :].rearrange("p g (a c) -> p g a c", c=S),
                       ACT.Exp, scale=scale).then_inc(s.exp_ready, 1)


def second_pass_vector(dve, k, n, s, kinds):
    step = Link(dve, s.mix_step)

    def copy(u):
        b, pair = u // 2, u % 2
        dve.wait_ge(s.pv_ready, KB * (u + 1))
        dve.tensor_copy(n.oT[:, b % 2, 2 * pair:2 * pair + 2, 0:kinds, :],
                        k.ps[:, 4:6, 0:kinds * S].rearrange("p i (a c) -> p i a c", c=S)).then_inc(s.pv_copied, 1)

    def mix(t):
        dve.wait_ge(s.outT_ready, t + 1)
        o = k.ps[:, 6:8, :].rearrange("p a (g j h c) -> p (a g) j h c", g=2, j=2, h=G)
        if kinds == 1:
            step(dve.reciprocal(n.mf[:, 0, :].rearrange("p (a h) -> p a h", h=G), o[:, :, 0, :, HD]))
            dve.tensor_tensor(n.att[:, t, :].rearrange("p (a h c) -> p a h c", h=G, c=HD), o[:, :, 0, :, 0:HD],
                              n.mf[:, 0, :].rearrange("p (a h) -> p a h", h=G).unsqueeze(3)
                              .broadcast_to([P, NG, G, HD]), ALU.mult).then_inc(s.att_ready, 1)
            return
        own = t % KB
        for kd in range(2):
            ins = dve.tensor_tensor(n.mt[:, kd, :].rearrange("p (a h) -> p a h", h=G), o[:, :, kd, :, HD],
                                    n.mw[:, t, kd, :].rearrange("p (a h) -> p a h", h=G), ALU.mult)
        step(ins)
        step(dve.tensor_tensor(n.ml[:, :], n.mt[:, 0, :], n.mt[:, 1, :], ALU.add))
        step(dve.reciprocal(n.ml[:, :], n.ml[:, :]))
        step(dve.reciprocal(n.mt[:, 0, :].rearrange("p (a h) -> p a h", h=G), o[:, :, own, :, HD]))
        step(dve.tensor_tensor(n.mf[:, :, :], n.mw[:, t, :, :], n.ml[:, :].unsqueeze(1).broadcast_to([P, 2, H]),
                               ALU.mult))
        step(dve.tensor_tensor(n.mf[:, own, :], n.mf[:, own, :], n.mt[:, 0, :], ALU.add))
        for kd in range(2):
            ins = dve.tensor_tensor(n.tmp[:, kd, :, :, :], o[:, :, kd, :, 0:HD],
                                    n.mf[:, kd, :].rearrange("p (a h) -> p a h", h=G).unsqueeze(3)
                                    .broadcast_to([P, NG, G, HD]), ALU.mult)
        step(ins)
        dve.tensor_tensor(n.att[:, t, :].rearrange("p (a h c) -> p a h c", h=G, c=HD), n.tmp[:, 0, :, :, :],
                          n.tmp[:, 1, :, :, :], ALU.add).then_inc(s.att_ready, 1)

    if kinds == 2:
        dve.wait_ge(s.mix_weights, 1)
    for u in range(B * 2):
        if u >= 2 and u % 2 == 0:
            mix(u - 2)
            mix(u - 1)
        copy(u)
    mix(NT - 2)
    mix(NT - 1)


def project_tensor(pe, k, s, att, w, ready):
    for t in range(NT):
        pe.wait_ge(ready, t + 1)
        pe.transpose(k.ps[:, t // 4, tile(t % 4)], att[:, t, :], k.ident).then_inc(s.attT_ready, 1)
    pe.wait_ge(s.attT_lo, 1)
    for t in range(NT):
        if t == 4:
            pe.wait_ge(s.attT_hi, 1)
        pe.matmul(k.ps[:, 2 + t // 4, tile(t % 4)], k.zT[:, tile(t)], w, start=True, stop=True)\
          .then_inc(s.out_ready, 1)


def project_scalar(act, k, s):
    act.wait_ge(s.attT_ready, NT)
    act.activation(k.zT[:, half(1)], k.ps[:, 1, :], ACT.Copy).then_inc(s.attT_hi, 1)


def project_vector(dve, k, s):
    dve.wait_ge(s.attT_ready, NT // 2)
    dve.tensor_copy(k.zT[:, half(0)], k.ps[:, 0, :]).then_inc(s.attT_lo, 1)
    for i in range(2):
        dve.wait_ge(s.out_ready, 4 * (i + 1))
        dve.tensor_tensor(k.x[:, 4 * i:4 * i + 4, :], k.x[:, 4 * i:4 * i + 4, :],
                          k.ps[:, 2 + i, :].rearrange("p (t d) -> p t d", d=D), ALU.add)


def row_over_tiles(k, name, tiles):
    return k.rows[:, ROW_AT[name]].unsqueeze(1).broadcast_to([P, tiles, D])


def copy_values(dve, k, n, s, bank, before, bias):
    for i in range(2):
        dve.wait_ge(s.proj_ready, before + i + 1)
        src = k.ps[:, bank + i, :].rearrange("p (t h c) -> p t h c", t=4, c=HD)
        dst = n.v[:, 4 * i:4 * i + 4, :, 0:HD]
        if bias is None:
            ins = dve.tensor_copy(dst, src)
        else:
            ins = dve.tensor_tensor(dst, src, k.rows[:, ROW_AT[bias]].rearrange("p (h c) -> p h c", c=HD)
                                    .unsqueeze(1).broadcast_to([P, 4, H, HD]), ALU.add)
        ins.then_inc(s.v_copied, 1)


def cross_phase(nc, k):
    s = narrow_sems(k, "cross")
    W = k.w
    scale = HD ** -0.5
    with ExitStack() as ctx:
        n = narrow_buffers(nc, ctx, "cross")
        block = ctx.enter_context(nc.Block())

        @block.gpsimd
        def _(pool):
            pool.memset(n.v[:, :, :, HD:HS], 0.0).then_inc(s.prep, 1)
            pool.wait_ge(s.prep, 1)
            pool.memset(n.v[:, :, :, HD:HD + 1], 1.0).then_inc(s.prep, 1)
            pool.memset(n.top[:, :, :, :], 0.0).then_inc(s.prep, 1)

        @block.vector
        def _(dve):
            dve.wait_ge(k.rows_loaded, 16)
            copy_values(dve, k, n, s, 5, 0, "bv0")
            norm_vector(dve, k, s)
            for i in range(NG * 2):
                dve.wait_ge(s.proj_ready, 2 + 2 * NG + i + 1)
                dve.tensor_scalar(n.q[:, i // 2, half(i % 2)], k.ps[:, 5 + i % 3, :],
                                  W["bq0"][:, i // 2:i // 2 + 1], None, ALU.add).then_inc(s.q_copied, 1)
            dve.wait_ge(s.prep, 3)
            first_pass_vector(dve, k, n, s, 2)
            step = Link(dve, s.diff_ready)
            m = n.top[:, :, :, :].rearrange("p t a (h c) -> p t (a h) c", h=G)
            step(dve.tensor_tensor(n.mw[:, :, 0, :], m[:, :, :, HD], m[:, :, :, HD + 1], ALU.subtract))
            step(dve.tensor_scalar(n.mw[:, :, 1, :], n.mw[:, :, 0, :], -1.0, 0.0, ALU.mult, ALU.min))
            step(dve.tensor_scalar(n.mw[:, :, 0, :], n.mw[:, :, 0, :], 0.0, None, ALU.min))
            dve.tensor_tensor(k.x[:, :, :], k.x[:, :, :], row_over_tiles(k, "bo0", NT), ALU.add).then_inc(s.bias_added, 1)
            second_pass_vector(dve, k, n, s, 2)
            dve.wait_ge(s.bias_added, 1)
            project_vector(dve, k, s)

        @block.scalar
        def _(act):
            act.wait_ge(k.weights_loaded, 16)
            for i in range(NG * 2):
                act.wait_ge(s.proj_ready, 2 + i + 1)
                for kb in range(KB):
                    src = k.ps[:, 2 + i % 3, :].rearrange("p (b c d) -> p b c d", c=KB, d=P)[:, :, kb, :]
                    dst = n.k[:, i // 2, half(i % 2)].rearrange("p (b c d) -> p b c d", c=KB, d=P)[:, :, kb, :]
                    ins = act.activation(dst, src, ACT.Identity, bias=W["bk0"][:, 2 * (i // 2) + kb:2 * (i // 2) + kb + 1])
                ins.then_inc(s.k_copied, 1)
            norm_scalar(act, k, s)
            act.wait_ge(s.diff_ready, 3)
            act.activation(n.mw[:, :, :, :], n.mw[:, :, :, :], ACT.Exp, scale=scale).then_inc(s.mix_weights, 1)
            second_pass_scalar(act, k, n, s, scale)
            project_scalar(act, k, s)

        @block.tensor
        def _(pe):
            pe.wait_ge(k.ctx_loaded, 16)
            for i in range(2):
                for t in range(4):
                    mm = pe.matmul(k.ps[:, 5 + i, tile(t)], k.ctxT[:, tile(4 * i + t)], W["wv0"], start=True, stop=True)
                mm.then_inc(s.proj_ready, 1)
            for i in range(NG * 2):
                if i >= 3:
                    pe.wait_ge(s.k_copied, i - 2)
                pe.matmul(k.ps[:, 2 + i % 3, :], W["wk0"][:, tile(i // 2)], k.ctxT[:, half(i % 2)], start=True,
                          stop=True).then_inc(s.proj_ready, 1)
            norm_tensor(pe, k, s)
            wait_zT(pe, s)
            pe.wait_ge(s.v_copied, 2)
            for i in range(NG * 2):
                if i >= 3:
                    pe.wait_ge(s.q_copied, i - 2)
                pe.matmul(k.ps[:, 5 + i % 3, :], W["wq0"][:, tile(i // 2)], k.zT[:, half(i % 2)], start=True,
                          stop=True).then_inc(s.proj_ready, 1)
            pe.wait_ge(s.q_copied, 2 * NG)
            pe.wait_ge(s.k_copied, 2 * NG)
            first_pass_tensor(pe, k, n, s)
            second_pass_tensor(pe, k, n, s, 2)
            project_tensor(pe, k, s, n.att, W["wo0"], s.att_ready)



def moe_phase(nc, k, ins):
    s = norm_sems(k, "moe")
    loaded = k.sem("moe_weights_loaded")
    logits_ready = k.sem("moe_logits_ready")
    gate_step = k.sem("moe_gate_step")
    gap_ready = k.sem("moe_gap_ready")
    gap_exp = k.sem("moe_gap_exp")
    hidden_ready = k.sem("moe_hidden_ready")
    gelu_done = k.sem("moe_gelu_done")
    expert_ready = k.sem("moe_expert_ready")
    added = k.sem("moe_added")
    with ExitStack() as ctx:
        def sb(name, shape):
            return ctx.enter_context(nc.sbuf_tensor(name, shape, F32))
        w1 = sb("w1", [P, E, F])
        w2 = sb("w2", [P, E, FC, D])
        h = sb("hidden", [P, 2, FC, T])
        lg = sb("logits", [P, NT, E])
        cand = sb("candidates", [P, NT, E])
        pick1 = sb("pick1", [P, NT, E])
        pick2 = sb("pick2", [P, NT, E])
        comb = sb("comb", [P, NT, E])
        c1, c2, c3, c4 = (sb(f"moe_c{i}", [P, NT]) for i in range(4))
        block = ctx.enter_context(nc.Block())

        @block.sync
        def _(sp):
            sp.dma_start(w1[:, :, :], ins["w1"].rearrange("e d f -> d e f")).then_inc(loaded, 16)
            sp.dma_start(w2[:, :, :, :], ins["w2"].rearrange("e (c p) d -> p e c d", p=P)).then_inc(loaded, 16)

        @block.vector
        def _(dve):
            norm_vector(dve, k, s)
            step = Link(dve, gate_step)

            def wide(a):
                return a[:, :].unsqueeze(2).broadcast_to([P, NT, E])
            rank = k.const[:, CONST_AT["rank"]].unsqueeze(1).broadcast_to([P, NT, E])
            dve.wait_ge(logits_ready, 1)
            step(dve.tensor_copy(lg[:, :, :], k.ps[:, 2, 0:NT * E].rearrange("p (t e) -> p t e", e=E)))

            def best(top, pick):
                step(dve.tensor_reduce(top[:, :], lg[:, :, :], AX_X, ALU.max))
                step(dve.tensor_tensor(cand[:, :, :], lg[:, :, :], wide(top), ALU.is_equal))
                step(dve.tensor_tensor(cand[:, :, :], cand[:, :, :], rank, ALU.mult))
                step(dve.tensor_reduce(c3[:, :], cand[:, :, :], AX_X, ALU.max))
                step(dve.tensor_tensor(pick[:, :, :], cand[:, :, :], wide(c3), ALU.is_equal))

            best(c1, pick1)
            step(dve.scalar_tensor_tensor(out=lg[:, :, :], in0=pick1[:, :, :], scalar=-3e38, in1=lg[:, :, :],
                                          op0=ALU.mult, op1=ALU.add))
            best(c2, pick2)
            dve.tensor_tensor(c3[:, :], c2[:, :], c1[:, :], ALU.subtract).then_inc(gap_ready, 1)
            dve.wait_ge(gap_exp, 1)
            step(dve.tensor_scalar(c1[:, :], c4[:, :], 1.0, None, ALU.add))
            step(dve.reciprocal(c1[:, :], c1[:, :]))
            step(dve.tensor_tensor(pick2[:, :, :], pick2[:, :, :], wide(c4), ALU.mult))
            step(dve.tensor_tensor(comb[:, :, :], pick1[:, :, :], pick2[:, :, :], ALU.add))
            step(dve.tensor_tensor(comb[:, :, :], comb[:, :, :], wide(c1), ALU.mult))
            for e in range(E):
                for t in range(NT):
                    dve.wait_ge(expert_ready, e * NT + 4 * (t // 4) + 4)
                    if e >= 1:
                        dve.wait_ge(added, (e - 1) * NT + t + 1)
                    dve.scalar_tensor_tensor(out=k.x[:, t, :], in0=k.ps[:, 2 * (e % 2) + t // 4, tile(t % 4)],
                                             scalar=comb[:, t, e:e + 1], in1=k.x[:, t, :], op0=ALU.mult,
                                             op1=ALU.add).then_inc(added, 1)

        @block.scalar
        def _(act):
            norm_scalar(act, k, s)
            act.wait_ge(gap_ready, 1)
            act.activation(c4[:, :], c3[:, :], ACT.Exp).then_inc(gap_exp, 1)
            for i in range(E * 2 * FC):
                e, c, part = i // (2 * FC), i // 2 % FC, i % 2
                act.wait_ge(hidden_ready, i + 1)
                if e >= 2:
                    act.wait_ge(expert_ready, (e - 1) * NT)
                act.activation(h[:, e % 2, c, half(part)], k.ps[:, 4 + i % 4, :], ACT.Gelu_apprx_tanh)\
                   .then_inc(gelu_done, 1)

        @block.tensor
        def _(pe):
            norm_tensor(pe, k, s)
            wait_zT(pe, s)
            for t in range(NT):
                mm = pe.matmul(k.ps[:, 2, t * E:t * E + E], k.zT[:, tile(t)], k.w["gate"], start=True, stop=True)
            mm.then_inc(logits_ready, 1)
            pe.wait_ge(loaded, 32)

            def hidden(i):
                e, c, part = i // (2 * FC), i // 2 % FC, i % 2
                if i >= 4:
                    pe.wait_ge(gelu_done, i - 3)
                pe.matmul(k.ps[:, 4 + i % 4, :], w1[:, e, tile(c)], k.zT[:, half(part)], start=True,
                          stop=True).then_inc(hidden_ready, 1)

            def expert(e, t):
                pe.wait_ge(gelu_done, (e + 1) * 2 * FC)
                if e == 1:
                    pe.wait_ge(gate_step, 1)
                if e >= 2:
                    pe.wait_ge(added, (e - 2) * NT + 4 * (t // 4) + 4)
                for c in range(FC):
                    mm = pe.matmul(k.ps[:, 2 * (e % 2) + t // 4, tile(t % 4)], h[:, e % 2, c, tile(t)],
                                   w2[:, e, c, :], start=(c == 0), stop=(c == FC - 1))
                mm.then_inc(expert_ready, 1)

            for e in range(E + 1):
                for i in range(NT):
                    if e < E:
                        hidden(e * NT + i)
                    if e >= 1:
                        expert(e - 1, i)



def rotary_phase(nc, k):
    s = narrow_sems(k, "rotary")
    rope_step = k.sem("rotary_rope_step")
    q_padded = k.sem("rotary_q_padded")
    k_padded = k.sem("rotary_k_padded")
    q_turned = k.sem("rotary_q_turned")
    k_turned = k.sem("rotary_k_turned")
    W = k.w
    with ExitStack() as ctx:
        n = narrow_buffers(nc, ctx, "rotary")
        block = ctx.enter_context(nc.Block())
        qp = n.e[:, :, :, :, :].rearrange("p a g j c -> p (a g j c)").rearrange("p (t h c) -> p t h c", t=NT, c=HS)
        kp = n.oT[:, :, :, :, :].rearrange("p a g j c -> p (a g j c)").rearrange("p (t h c) -> p t h c", t=NT, c=HS)

        @block.gpsimd
        def _(pool):
            pool.memset(n.e[:, :, :, :, :], 0.0).then_inc(s.prep, 1)
            pool.memset(n.oT[:, :, :, :, :], 0.0).then_inc(s.prep, 1)
            pool.wait_ge(s.prep, 2)
            pool.memset(kp[:, :, :, HD:HD + 1], 1.0).then_inc(s.prep, 1)
            pool.memset(n.v[:, :, :, HD:HS], 0.0).then_inc(s.prep, 1)
            pool.wait_ge(s.prep, 4)
            pool.memset(n.v[:, :, :, HD:HD + 1], 1.0).then_inc(s.prep, 1)
            pool.memset(n.top[:, :, :, :], 0.0).then_inc(s.prep, 1)

        @block.vector
        def _(dve):
            step = Link(dve, rope_step)

            def rope(bank, i, dst, ready):
                src = k.ps[:, bank, :].rearrange("p (b c) -> p b c", b=2)
                pairs = k.ps[:, bank, :].rearrange("p (b c two) -> p b c two", b=2, two=2)
                by_cos = n.att[:, 0:4, :].rearrange("p t c -> p (t c)")
                by_sin = n.att[:, 4:8, :].rearrange("p t c -> p (t c)")
                sin = k.const[:, CONST_AT["sin"]].rearrange("p (c two) -> p c two", two=2)
                dve.tensor_tensor(by_cos.rearrange("p (b c) -> p b c", b=2), src,
                                  k.const[:, CONST_AT["cos"]].unsqueeze(1).broadcast_to([P, 2, KB * P]), ALU.mult)
                for even in range(2):
                    ins = dve.tensor_tensor(by_sin.rearrange("p (b c two) -> p b c two", b=2, two=2)[:, :, :, even],
                                            pairs[:, :, :, 1 - even],
                                            sin[:, :, even].unsqueeze(1).broadcast_to([P, 2, KB * P // 2]), ALU.mult)
                step(ins)
                ins = dve.tensor_tensor(dst[:, 4 * i:4 * i + 4, :, 0:HD], by_cos.rearrange("p (t h c) -> p t h c", t=4, c=HD),
                                        by_sin.rearrange("p (t h c) -> p t h c", t=4, c=HD), ALU.add)
                ins.then_inc(ready, 1)
                dve.wait_ge(ready, i + 1)

            norm_vector(dve, k, s)
            dve.wait_ge(s.prep, 6)
            for i in range(2):
                dve.wait_ge(s.proj_ready, 1 + i)
                rope(2 + i, i, qp, q_padded)
            for i in range(2):
                dve.wait_ge(s.proj_ready, 3 + i)
                rope(4 + i, i, kp, k_padded)
            copy_values(dve, k, n, s, 6, 4, None)
            for t in range(NT):
                dve.wait_ge(q_turned, t + 1)
                dve.tensor_copy(n.q[:, :, tile(t)], k.ps[:, t % 2, :].rearrange("p (g c) -> p g c", c=P))\
                   .then_inc(s.q_copied, 1)
            first_pass_vector(dve, k, n, s, 1)
            second_pass_vector(dve, k, n, s, 1)
            project_vector(dve, k, s)

        @block.scalar
        def _(act):
            norm_scalar(act, k, s)
            for t in range(NT):
                act.wait_ge(k_turned, t + 1)
                act.activation(n.k[:, :, tile(t)], k.ps[:, 6 + t % 2, :].rearrange("p (g c) -> p g c", c=P), ACT.Copy)\
                   .then_inc(s.k_copied, 1)
            second_pass_scalar(act, k, n, s, HD ** -0.5)
            project_scalar(act, k, s)

        @block.tensor
        def _(pe):
            norm_tensor(pe, k, s)
            wait_zT(pe, s)
            for bank, w in ((2, "wq1"), (4, "wk1"), (6, "wv1")):
                for i in range(2):
                    for t in range(4):
                        mm = pe.matmul(k.ps[:, bank + i, tile(t)], k.zT[:, tile(4 * i + t)], W[w], start=True, stop=True)
                    mm.then_inc(s.proj_ready, 1)
            for t in range(NT):
                pe.wait_ge(q_padded, t // 4 + 1)
                if t >= 2:
                    pe.wait_ge(s.q_copied, t - 1)
                for gi in range(NG):
                    mm = pe.transpose(k.ps[:, t % 2, tile(gi)], qp[:, t, G * gi:G * gi + G, :], k.ident)
                mm.then_inc(q_turned, 1)
            pe.wait_ge(s.v_copied, 2)
            for t in range(NT):
                pe.wait_ge(k_padded, t // 4 + 1)
                if t >= 2:
                    pe.wait_ge(s.k_copied, t - 1)
                for gi in range(NG):
                    mm = pe.transpose(k.ps[:, 6 + t % 2, tile(gi)], kp[:, t, G * gi:G * gi + G, :], k.ident)
                mm.then_inc(k_turned, 1)
            pe.wait_ge(s.q_copied, NT)
            pe.wait_ge(s.k_copied, NT)
            first_pass_tensor(pe, k, n, s)
            second_pass_tensor(pe, k, n, s, 1)
            project_tensor(pe, k, s, n.att, W["wo1"], s.att_ready)




QG = 16
NQ = S // QG
NPAIR = 4
RPAIR = NPAIR * QG
RSUM = 5
ROUND = 1.5 * 2.0 ** 23
TWO_PI_HI = 6.28125
TWO_PI_LO = float(2.0 * np.pi - 6.28125)
BELOW_PI = 3.1415925
U = DK + 1


def box_prep_phase(nc, k, ins):
    box_in = k.sem("box_inputs")
    centre_step = k.sem("box_centre_step")
    apart = k.sem("box_apart")
    absolute = k.sem("box_absolute")
    clipped = k.sem("box_clipped")
    logged = k.sem("box_logged")
    turns_ready = k.sem("box_turns")
    angle_step = k.sem("box_angle_step")
    angle_ready = k.sem("box_angle_ready")
    sine_done = k.sem("box_sine_done")
    half_sine_step = k.sem("box_half_sine_step")
    half_sine = k.sem("box_half_sine")
    features = k.sem("box_features")
    size_step = k.sem("box_size_step")
    size_ready = k.sem("box_size_ready")
    size_log = k.sem("box_size_log")
    size_angle = k.sem("box_size_angle")
    size_sine = k.sem("box_size_sine")
    with ExitStack() as ctx:
        def sb(name, shape):
            return ctx.enter_context(nc.sbuf_tensor(name, shape, F32))
        rows = sb("box_rows", [P, 4, T])
        own = sb("box_own", [P, NT, 4])
        ckey = sb("box_centre_key", [P, 2, T])
        cown = sb("box_centre_own", [P, NT, 2])
        size = sb("box_size_own", [P, NT, 2])
        d = sb("box_distance", [P, NT, 2, S])
        turns = sb("box_turns_of", [P, NT, 2, S])
        feat = sb("box_feat", [P, NT, NPAIR, S])
        ends = sb("box_ends", [P, 2, T])
        y5 = sb("box_y5", [P, 2, T])
        t5 = sb("box_t5", [P, 2, T])
        block = ctx.enter_context(nc.Block())
        r5 = slice(RPAIR, RPAIR + RSUM)

        @block.sync
        def _(sp):
            sp.dma_start(rows[:, :, :], ins["box_rows"].partition_broadcast(P)).then_inc(box_in, 16)
            sp.dma_start(own[:, :, :], ins["boxes"].rearrange("(t p) c -> p t c", p=P)).then_inc(box_in, 16)
            sp.dma_start(ends[r5, :, :], ins["box_ends"]).then_inc(box_in, 16)
            sp.dma_start(k.box5[r5, :], ins["box5"]).then_inc(box_in, 16)
            for t in range(NT):
                b, i = t // KB, t % KB
                sp.wait_ge(sine_done, b + 1)
                sp.wait_ge(features, b + 1)
                sp.dma_start(k.pairs[b, :, i * P:i * P + P, :].rearrange("f q m -> q f m"), feat[:, t, :, :])\
                  .then_inc(k.pairs_stored, 16)
            sp.wait_ge(k.pairs_stored, 16 * NT)

        @block.vector
        def _(dve):
            step = Link(dve, centre_step)
            dve.wait_ge(box_in, 64)
            step(dve.tensor_tensor(ckey[:, :, :], rows[:, 0:2, :], rows[:, 2:4, :], ALU.add))
            step(dve.tensor_scalar(ckey[:, :, :], ckey[:, :, :], 0.5, None, ALU.mult))
            step(dve.tensor_tensor(cown[:, :, :], own[:, :, 0:2], own[:, :, 2:4], ALU.add))
            step(dve.tensor_scalar(cown[:, :, :], cown[:, :, :], 0.5, None, ALU.mult))
            step(dve.tensor_tensor(size[:, :, :], own[:, :, 2:4], own[:, :, 0:2], ALU.subtract))
            step(dve.tensor_scalar(size[:, :, :], size[:, :, :], 1.0, None, ALU.add))
            step(dve.reciprocal(size[:, :, :], size[:, :, :]))
            for b in range(B):
                for t in range(KB * b, KB * b + KB):
                    for c in range(2):
                        ins_ = dve.tensor_scalar(d[:, t, c, :], ckey[:, c, b * S:b * S + S], cown[:, t, c:c + 1],
                                                 None, ALU.subtract)
                ins_.then_inc(apart, 1)
            five = Link(dve, size_step)
            five(dve.tensor_tensor(y5[r5, 0, :], ends[r5, 0, :], ends[r5, 1, :], ALU.subtract))
            dve.tensor_scalar(y5[r5, 0, :], y5[r5, 0, :], 1.0, None, ALU.add).then_inc(size_ready, 1)
            for b in range(B):
                dve.wait_ge(absolute, b + 1)
                dve.tensor_scalar(d[:, 2 * b:2 * b + 2, :, :], d[:, 2 * b:2 * b + 2, :, :], 1e-3, None, ALU.max)\
                   .then_inc(clipped, 1)
            dve.wait_ge(size_log, 1)
            five(dve.tensor_scalar(y5[r5, 0, :], y5[r5, 0, :], 100.0, None, ALU.mult))
            for form in range(2):
                quarter, phase = k.box5[r5, 2 * form:2 * form + 1], k.box5[r5, 2 * form + 1:2 * form + 2]
                five(dve.tensor_scalar(t5[r5, form, :], y5[r5, 0, :], float(1 / (2 * np.pi)), quarter, ALU.mult, ALU.add))
                five(dve.tensor_scalar(t5[r5, form, :], t5[r5, form, :], ROUND, None, ALU.add))
                five(dve.tensor_scalar(t5[r5, form, :], t5[r5, form, :], ROUND, None, ALU.subtract))
                five(dve.scalar_tensor_tensor(out=y5[r5, 1, :], in0=t5[r5, form, :], scalar=-TWO_PI_HI,
                                              in1=y5[r5, 0, :], op0=ALU.mult, op1=ALU.add))
                five(dve.scalar_tensor_tensor(out=t5[r5, form, :], in0=t5[r5, form, :], scalar=-TWO_PI_LO,
                                              in1=y5[r5, 1, :], op0=ALU.mult, op1=ALU.add))
                five(dve.tensor_scalar(t5[r5, form, :], t5[r5, form, :], phase, BELOW_PI, ALU.add, ALU.min))
                dve.tensor_scalar(t5[r5, form, :], t5[r5, form, :], -BELOW_PI, None, ALU.max).then_inc(size_angle, 1)
            angle = Link(dve, angle_step)
            for b in range(B):
                y, n = d[:, 2 * b:2 * b + 2, :, :], turns[:, 2 * b:2 * b + 2, :, :]
                y, n = (v.rearrange("p t c m -> p (t c m)") for v in (y, n))
                dve.wait_ge(turns_ready, b + 1)
                angle(dve.scalar_tensor_tensor(out=y, in0=n, scalar=-TWO_PI_HI, in1=y, op0=ALU.mult, op1=ALU.add))
                angle(dve.scalar_tensor_tensor(out=y, in0=n, scalar=-TWO_PI_LO, in1=y, op0=ALU.mult, op1=ALU.add))
                dve.tensor_scalar(y, y, BELOW_PI, -BELOW_PI, ALU.min, ALU.max).then_inc(angle_ready, 1)
            for b in range(B):
                dve.wait_ge(half_sine, b + 1)
                dve.tensor_scalar(feat[:, 2 * b:2 * b + 2, 2:4, :], turns[:, 2 * b:2 * b + 2, :, :], -2.0, 1.0,
                                  ALU.mult, ALU.add).then_inc(features, 1)

        @block.gpsimd
        def _(pool):
            step = Link(pool, k.sem("box_pool_step"))
            for b in range(B):
                pool.wait_ge(logged, b + 1)
                y, n = d[:, 2 * b:2 * b + 2, :, :], turns[:, 2 * b:2 * b + 2, :, :]
                step(pool.tensor_scalar(y, y, 100.0, None, ALU.mult))
                step(pool.tensor_scalar(n, y, float(1 / (2 * np.pi)), ROUND, ALU.mult, ALU.add))
                pool.tensor_scalar(n, n, ROUND, None, ALU.subtract).then_inc(turns_ready, 1)

        @block.scalar
        def _(act):
            for b in range(B):
                act.wait_ge(apart, b + 1)
                for t in range(KB * b, KB * b + KB):
                    for c in range(2):
                        ins_ = act.activation(d[:, t, c, :], d[:, t, c, :], ACT.Abs, scale=size[:, t, c:c + 1])
                ins_.then_inc(absolute, 1)
            act.wait_ge(size_ready, 1)
            act.activation(y5[r5, 0, :], y5[r5, 0, :], ACT.Ln).then_inc(size_log, 1)
            for b in range(B):
                act.wait_ge(clipped, b + 1)
                act.activation(d[:, 2 * b:2 * b + 2, :, :], d[:, 2 * b:2 * b + 2, :, :], ACT.Ln).then_inc(logged, 1)
            for form in range(2):
                act.wait_ge(size_angle, form + 1)
                act.activation(k.size_waves[r5, form, :], t5[r5, form, :], ACT.Sin).then_inc(size_sine, 1)
            for b in range(B):
                angle, n = d[:, 2 * b:2 * b + 2, :, :], turns[:, 2 * b:2 * b + 2, :, :]
                act.wait_ge(angle_ready, b + 1)
                act.activation(n, angle, ACT.Sin, scale=0.5).then_inc(half_sine_step, 1)
                act.activation(feat[:, 2 * b:2 * b + 2, 0:2, :], angle, ACT.Sin).then_inc(sine_done, 1)
                act.wait_ge(half_sine_step, b + 1)
                act.activation(n, n, ACT.Square).then_inc(half_sine, 1)


def box_plan():
    plan = []
    for b in range(B + 1):
        front = ([("K", b, j) for j in range(2)] + [("Q", b, j) for j in range(2)] + [("V", b, j) for j in range(2)]
                 if b < B else [])
        late = [("G", b - 1, 1, j) for j in range(NQ // 2)] if b else []
        while front or late:
            if front:
                plan.append(front.pop(0))
            if late:
                plan.append(late.pop(0))
        sc = [("S", b, i, j) for i in range(KB) for j in range(4)] if b < B else []
        pv = []
        if b:
            for i in range(KB):
                pv += [("P", b - 1, i, j) for j in range(3)] + [("T", b - 1, i), ("O", b - 1, i)]
        while sc or pv:
            if sc:
                plan.append(sc.pop(0))
            if pv:
                plan.append(pv.pop(0))
        if b < B:
            plan.append(("M", b))
            plan += [("X", b, 0, j) for j in range(4)]
            for j in range(4):
                plan += [("X", b, 1, j), ("G", b, 0, 2 * j), ("G", b, 0, 2 * j + 1)]
    return plan


PV_HEADS = [range(0, 6), range(6, 11), range(11, 16)]
SLOT_USERS = {"K": "act", "Q": "dve", "V": "dve", "S": "dve", "M": "dve", "X": "act", "T": "act", "O": "dve"}


def box_phase(nc, k, ins):
    s = norm_sems(k, "box")
    prep = k.sem("box_prep")
    minus_loaded = k.sem("box_minus_loaded")
    consts_cast = k.sem("box_consts_cast")
    sums_loaded = k.sem("box_weights_loaded")
    pairs_loaded = [k.sem(f"box_pairs_loaded_{i}") for i in range(2)]
    sums_step = k.sem("box_sums_step")
    sums_ready = k.sem("box_sums_ready")
    slot_ready = k.sem("box_slot_ready")
    slot_freed = {"act": k.sem("box_slot_freed_act"), "dve": k.sem("box_slot_freed_dve")}
    g_ready = k.sem("box_g_ready")
    g_used = k.sem("box_g_used")
    pv_ready = k.sem("box_pv_ready")
    pv_used = k.sem("box_pv_used")
    pv_step = k.sem("box_pv_step")
    split_step = k.sem("box_split_step")
    max_split = k.sem("box_max_split")
    x_step = k.sem("box_x_step")
    plan = box_plan()
    slots = [item for item in plan if item[0] in SLOT_USERS]
    slot_at = {item: n for n, item in enumerate(slots)}
    g_at = {item: n for n, item in enumerate(i for i in plan if i[0] == "G")}
    pv_at = {item: n for n, item in enumerate(i for i in plan if i[0] == "P")}

    def freed(item):
        user = SLOT_USERS[item[0]]
        return slot_freed[user], sum(SLOT_USERS[i[0]] == user for i in slots[:slot_at[item] + 1])

    with ExitStack() as ctx:
        def sb(name, shape, dt=F32):
            return ctx.enter_context(nc.sbuf_tensor(name, shape, dt))
        q2 = sb("box_q", [P, NC, S])
        k2 = sb("box_k", [P, NC, S])
        v2 = sb("box_v", [P, 2, KB, H, U])
        top = sb("box_top", [P, NT, H])
        rest = sb("box_top_rest", [P, 2, H])
        top3 = sb("box_top3", [P, 2, 2, 64], BF16)
        top3T = sb("box_top3T", [P, S], BF16)
        minus = sb("box_minus", [P, H, P], BF16)
        identb = sb("box_identb", [P, P], BF16)
        e = sb("box_e", [P, 3, S, H])
        pairs = sb("box_pairs", [P, 2, NQ, P])
        sums = sb("box_sums", [P, S, H])
        sums2 = sb("box_sums2", [P, S, H])
        att = sb("box_att", [P, 2, H, DK])
        rden = sb("box_rden", [P, 2, 8])
        attT = sb("box_attT", [P, NC, P])
        block = ctx.enter_context(nc.Block())
        r5 = slice(RPAIR, RPAIR + RSUM)
        rows = RPAIR + RSUM

        def slot(item):
            return 2 * (slot_at[item] % 2)

        @block.sync
        def _(sp):
            sp.dma_start(e[:, 0, 0:P, :], ins["minus"]).then_inc(minus_loaded, 16)
            sp.dma_start(sums[0:RPAIR, :, :].rearrange("p (n q) h -> p n (q h)", q=QG),
                         ins["wg_rows"].unsqueeze(1).broadcast_to([RPAIR, NQ, H * QG])).then_inc(sums_loaded, 16)
            sp.wait_ge(k.pairs_stored, 16 * NT)
            for u in range(B * KB):
                b, kb = u // KB, u % KB
                if u >= 2:
                    sp.wait_ge(g_ready, (u - 1) * NQ // 2)
                for f in range(NPAIR):
                    sp.dma_start(pairs[QG * f:QG * f + QG, u % 2, :, :],
                                 k.pairs[b, f, :, kb * P:kb * P + P].rearrange("(n q) m -> q n m", q=QG))\
                      .then_inc(pairs_loaded[u % 2], 16)
                sp.dma_start(pairs[r5, u % 2, :, :], k.size_waves[r5, 0, b * S + kb * P:b * S + kb * P + P].unsqueeze(1)
                             .broadcast_to([RSUM, NQ, P])).then_inc(pairs_loaded[u % 2], 16)

        @block.gpsimd
        def _(pool):
            pool.memset(v2[:, :, :, :, DK:U], 1.0).then_inc(prep, 1)
            pool.memset(top3[:, :, :, :], 0.0).then_inc(prep, 1)
            pool.wait_ge(prep, 2)
            step = Link(pool, sums_step)
            full = [RSUM, S, H]
            for b in range(B):
                if b >= 1:
                    pool.wait_ge(sums_ready, b)
                    pool.wait_ge(g_ready, b * NQ)
                for form, dst in ((0, sums[r5, :, :]), (1, sums2[r5, :, :])):
                    step(pool.tensor_tensor(dst, k.size_waves[r5, form, b * S:b * S + S].unsqueeze(2).broadcast_to(full),
                                            k.box5[r5, 4 + H * form:4 + H * form + H].unsqueeze(1)
                                            .broadcast_to(full), ALU.mult))
                pool.tensor_tensor(sums[r5, :, :], sums[r5, :, :], sums2[r5, :, :], ALU.add).then_inc(sums_ready, 1)

        @block.tensor
        def _(pe):
            norm_tensor(pe, k, s)
            wait_zT(pe, s)
            pe.wait_ge(k.wide_loaded, 16)
            pe.wait_ge(sums_loaded, 16)
            pe.wait_ge(consts_cast, 2)
            wq, wk, wv, wo = (k.wide[:, WIDE_AT[n]] for n in ("wq2", "wk2", "wv2", "wo2"))

            def wait_freed(item):
                pe.wait_ge(*freed(item))

            for item in plan:
                kind, b = item[:2]
                if kind in SLOT_USERS:
                    bank = slot(item)
                    if slot_at[item] >= 2:
                        wait_freed(slots[slot_at[item] - 2])
                if kind in "KQ":
                    w, src = (wk, k.ctxT) if kind == "K" else (wq, k.zT)
                    for j in range(4):
                        mm = pe.matmul(k.ps[:, bank + j // 2, j % 2 * S:j % 2 * S + S], w[:, tile(4 * item[2] + j)],
                                       src[:, b * S:b * S + S], start=True, stop=True)
                elif kind == "V":
                    for j in range(2):
                        mm = pe.matmul(k.ps[:, bank + j, :], k.ctxT[:, tile(KB * b + item[2])], wv[:, half(j)],
                                       start=True, stop=True)
                elif kind == "S":
                    wait_freed(("K", b, 1))
                    wait_freed(("Q", b, 1))
                    for j in range(4):
                        h = 4 * item[3] + j
                        r = slice(DK * (h % 2), DK * (h % 2) + DK)
                        mm = pe.matmul(k.ps[:, bank + h % 2, j // 2 * S:j // 2 * S + S], q2[r, h // 2, tile(item[2])],
                                       k2[r, h // 2, :], start=True, stop=True)
                elif kind == "M":
                    pe.wait_ge(max_split, b + 1)
                    for i in range(KB):
                        mm = pe.transpose(k.ps[:, bank, :].bitcast(BF16)[:, tile(i)],
                                          top3[:, i, :, :], identb[:, :])
                elif kind == "X":
                    wait_freed(("M", b))
                    for j in range(4):
                        h = 4 * item[3] + j
                        r = slice(DK * (h % 2), DK * (h % 2) + DK)
                        at = k.ps[:, bank + h % 2, j // 2 * S:j // 2 * S + S]
                        pe.matmul(at, k2[r, h // 2, tile(item[2])], q2[r, h // 2, :], start=True, stop=False,
                                  skip_group_check=True)
                        mm = pe.matmul(at, minus[r, h, :], top3T[r, :], start=False, stop=True, skip_group_check=True)
                elif kind == "G":
                    n = g_at[item]
                    u = KB * b + item[2]
                    pe.wait_ge(pairs_loaded[u % 2], 16 * (NPAIR + 1) * (u // 2 + 1))
                    pe.wait_ge(sums_ready, b + 1)
                    if n >= 2:
                        pe.wait_ge(g_used, n - 1)
                    for j in range(2):
                        qg = 2 * item[3] + j
                        mm = pe.matmul(k.ps[:, 4 + n % 2, j * H * QG:(j + 1) * H * QG], pairs[0:rows, u % 2, qg, :],
                                       sums[0:rows, QG * qg:QG * qg + QG, :], start=True, stop=True)
                    mm.then_inc(g_ready, 1)
                elif kind == "P":
                    n = pv_at[item]
                    pe.wait_ge(g_used, (b + 1) * NQ)
                    wait_freed(("V", b, 1))
                    if n >= 2:
                        pe.wait_ge(pv_used, n - 1)
                    for j, h in enumerate(PV_HEADS[item[3]]):
                        for kb in range(KB):
                            mm = pe.matmul(k.ps[:, 6 + n % 2, j * U:j * U + U],
                                           e[:, (KB * b + kb) % 3, tile(item[2]), h],
                                           v2[:, b % 2, kb, h, :], start=(kb == 0), stop=(kb == KB - 1))
                    mm.then_inc(pv_ready, 1)
                elif kind == "T":
                    pe.wait_ge(pv_used, pv_at[("P", b, item[2], 2)] + 1)
                    for c in range(NC):
                        mm = pe.transpose(k.ps[:, bank + c // 4, tile(c % 4)], att[:, item[2], 2 * c:2 * c + 2, :],
                                          k.ident)
                elif kind == "O":
                    wait_freed(("T", b, item[2]))
                    for c in range(NC):
                        mm = pe.matmul(k.ps[:, bank, 0:D], attT[:, c, :], wo[:, tile(c)], start=(c == 0),
                                       stop=(c == NC - 1))
                if kind in SLOT_USERS:
                    mm.then_inc(slot_ready, 1)

        @block.scalar
        def _(act):
            act.activation(identb[:, :], k.ident, ACT.Copy).then_inc(consts_cast, 1)
            act.wait_ge(minus_loaded, 16)
            act.activation(minus[:, :, :].rearrange("p h m -> p (h m)"), e[:, 0, 0:P, :].rearrange("p a b -> p (a b)"),
                           ACT.Copy).then_inc(consts_cast, 1)
            norm_scalar(act, k, s)
            for item in plan:
                kind, b = item[:2]
                if SLOT_USERS.get(kind) != "act":
                    continue
                act.wait_ge(slot_ready, slot_at[item] + 1)
                bank = slot(item)
                if kind == "K":
                    for j in range(4):
                        c = 4 * item[2] + j
                        ins_ = act.activation(k2[:, c, :], k.ps[:, bank + j // 2, j % 2 * S:j % 2 * S + S], ACT.Identity,
                                              bias=k.w["bk2"][:, c:c + 1])
                elif kind == "X":
                    for par in range(2):
                        ins_ = act.activation(
                            e[:, (KB * b + item[2]) % 3, :, 4 * item[3] + par:4 * item[3] + 4:2].rearrange("p q h -> p h q"),
                            k.ps[:, bank + par, :].rearrange("p (h q) -> p h q", h=2), ACT.Exp, scale=DK ** -0.5)
                else:
                    ins_ = act.activation(attT[:, :, :].rearrange("p (a c) t -> p a (c t)", a=2),
                                          k.ps[:, bank:bank + 2, :], ACT.Copy)
                ins_.then_inc(slot_freed["act"], 1)

        @block.vector
        def _(dve):
            norm_vector(dve, k, s)
            dve.wait_ge(prep, 2)
            split = Link(dve, split_step)
            pvl = Link(dve, pv_step)
            dve.wait_ge(s.zT_hi, 1)
            dve.tensor_tensor(k.x[:, :, :], k.x[:, :, :], row_over_tiles(k, "bo2", NT), ALU.add).then_inc(x_step, 1)
            dve.wait_ge(x_step, 1)
            for item in plan:
                kind, b = item[:2]
                bank = 0
                if SLOT_USERS.get(kind) == "dve":
                    dve.wait_ge(slot_ready, slot_at[item] + 1)
                    bank = slot(item)
                if kind == "Q":
                    for j in range(4):
                        c = 4 * item[2] + j
                        ins_ = dve.tensor_scalar(q2[:, c, :], k.ps[:, bank + j // 2, j % 2 * S:j % 2 * S + S],
                                                 k.w["bq2"][:, c:c + 1], None, ALU.add)
                elif kind == "V":
                    ins_ = dve.tensor_tensor(v2[:, b % 2, item[2], :, 0:DK],
                                             k.ps[:, bank:bank + 2, :].rearrange("p a (h c) -> p (a h) c", c=DK),
                                             k.rows[:, ROW_AT["bv2"]].rearrange("p (h c) -> p h c", c=DK), ALU.add)
                elif kind == "S":
                    t = KB * b + item[2]
                    ins_ = dve.tensor_reduce(top[:, t, 4 * item[3]:4 * item[3] + 4].rearrange("p (a h) -> p h a", h=2),
                                             k.ps[:, bank:bank + 2, :].rearrange("p h (a c) -> p h a c", c=S), AX_X, ALU.max)
                elif kind == "M":
                    ins_ = dve.tensor_copy(top3T[:, :], k.ps[:, bank, :].bitcast(BF16)[:, 0:S])
                elif kind == "O":
                    t = KB * b + item[2]
                    ins_ = dve.tensor_tensor(k.x[:, t, :], k.x[:, t, :], k.ps[:, bank, 0:D], ALU.add)
                elif kind == "G":
                    n = g_at[item]
                    part = e[:, (KB * b + item[2]) % 3, 2 * QG * item[3]:2 * QG * (item[3] + 1), :].rearrange("p q h -> p (q h)")
                    dve.wait_ge(g_ready, n + 1)
                    dve.wait_ge(*freed(("X", b, item[2], 3)))
                    dve.scalar_tensor_tensor(out=part, in0=k.ps[:, 4 + n % 2, :], scalar=1e-6, in1=part, op0=ALU.max,
                                             op1=ALU.mult).then_inc(g_used, 1)
                elif kind == "P":
                    n = pv_at[item]
                    heads = PV_HEADS[item[3]]
                    m = len(heads)
                    dve.wait_ge(pv_ready, n + 1)
                    o = k.ps[:, 6 + n % 2, 0:m * U].rearrange("p (h c) -> p h c", c=U)
                    if n >= 2:
                        dve.wait_ge(pv_used, n - 1)
                    pvl(dve.reciprocal(rden[:, n % 2, 0:m], o[:, :, DK]))
                    dve.tensor_tensor(att[:, item[2], heads[0]:heads[0] + m, :], o[:, :, 0:DK],
                                      rden[:, n % 2, 0:m].unsqueeze(2).broadcast_to([P, m, DK]), ALU.mult).then_inc(pv_used, 1)
                if SLOT_USERS.get(kind) == "dve":
                    ins_.then_inc(slot_freed["dve"], 1)
                if kind == "S" and item[2:] == (KB - 1, 3):
                    dve.wait_ge(*freed(item))
                    m2 = top[:, KB * b:KB * b + KB, :]

                    def put(j, src):
                        for side in range(2):
                            i_ = dve.tensor_copy(top3[:, :, side, H * j:H * j + H], src)
                        split(i_)
                    if b >= 1:
                        dve.wait_ge(*freed(("M", b - 1)))
                    put(0, m2)
                    for j in range(2):
                        split(dve.tensor_tensor(rest[:, :, :], m2 if j == 0 else rest[:, :, :],
                                                top3[:, :, 0, H * j:H * j + H], ALU.subtract))
                        if j == 0:
                            put(1, rest[:, :, :])
                    for side in range(2):
                        i_ = dve.tensor_copy(top3[:, :, side, 2 * H:3 * H], rest[:, :, :])
                    i_.then_inc(max_split, 1)


def box_arrays(a):
    boxes = a["fside_BxSx4_0"].reshape(T, 4)
    lo_x, lo_y, hi_x, hi_y = boxes.T
    zero = np.zeros(T, np.float32)
    wg, bg = a["L1_xattn_Wg"], a["L1_xattn_bg"]
    quarters = np.array([[0.25, 0.0, 0.25, 0.0, 0.25], [0.0, -0.25, 0.0, -0.25, 0.25]], np.float32)
    box5 = np.zeros((RSUM, 4 + 2 * H), np.float32)
    for form in range(2):
        box5[:, 2 * form] = quarters[form]
        box5[:, 2 * form + 1] = quarters[form] * np.float32(2 * np.pi)
    box5[0:2, 4:4 + H], box5[2:4, 4:4 + H] = wg[:, 6], wg[:, 7]
    box5[0:2, 4 + H:], box5[2:4, 4 + H:], box5[4, 4 + H:] = wg[:, 2], wg[:, 3], bg
    wg_rows = np.zeros((NPAIR, QG, QG, H), np.float32)
    for f, col in enumerate((0, 1, 4, 5)):
        for q in range(QG):
            wg_rows[f, q, q, :] = wg[:, col]
    minus = np.zeros((2, DK, H, P), np.float32)
    for h in range(H):
        minus[:, h:3 * H:H, h, :] = -1.0
    return {
        "boxes": boxes, "box_rows": np.ascontiguousarray(boxes.T), "box5": box5,
        "box_ends": np.ascontiguousarray(np.stack([np.stack([hi_x, hi_x, hi_y, hi_y, zero]),
                                                   np.stack([lo_x, lo_x, lo_y, lo_y, zero])], 1)),
        "wg_rows": wg_rows.reshape(RPAIR, H * QG), "minus": minus.reshape(P, H, P),
    }



def chain_phase(nc, k):
    s = norm_sems(k, "chain")
    turned = [k.sem(f"chain_product_{i}") for i in range(2)]
    copied_lo = k.sem("chain_copied_lo")
    copied_hi = k.sem("chain_copied_hi")
    last_ready = k.sem("chain_last_ready")
    biased = k.sem("chain_biased")
    tanh_done = k.sem("chain_tanh_done")
    W = k.w
    with ExitStack() as ctx:
        a = ctx.enter_context(nc.sbuf_tensor("chain_a", [P, T], F32))
        b = ctx.enter_context(nc.sbuf_tensor("chain_b", [P, T], F32))
        block = ctx.enter_context(nc.Block())
        bufs = (a, b)

        @block.vector
        def _(dve):
            norm_vector(dve, k, s)
            for j in range(2):
                dve.wait_ge(turned[0], j + 1)
                dve.tensor_copy(bufs[j][:, half(0)], k.ps[:, 2 + 2 * j, :]).then_inc(copied_lo, 1)
            for i in range(2):
                dve.wait_ge(last_ready, i + 1)
                dve.tensor_tensor(k.z[:, 4 * i:4 * i + 4, :], k.ps[:, 6 + i, :].rearrange("p (t d) -> p t d", d=D),
                                  row_over_tiles(k, "ffn_b", 4), ALU.add).then_inc(biased, 1)
            for i in range(2):
                dve.wait_ge(tanh_done, i + 1)
                dve.tensor_tensor(k.x[:, 4 * i:4 * i + 4, :], k.x[:, 4 * i:4 * i + 4, :],
                                  k.z[:, 4 * i:4 * i + 4, :], ALU.add).then_inc(k.x_final, 1)

        @block.scalar
        def _(act):
            norm_scalar(act, k, s)
            for j in range(2):
                act.wait_ge(turned[1], j + 1)
                act.activation(bufs[j][:, half(1)], k.ps[:, 3 + 2 * j, :], ACT.Copy).then_inc(copied_hi, 1)
            for i in range(2):
                act.wait_ge(biased, i + 1)
                act.activation(k.z[:, 4 * i:4 * i + 4, :], k.z[:, 4 * i:4 * i + 4, :], ACT.Tanh).then_inc(tanh_done, 1)

        @block.tensor
        def _(pe):
            norm_tensor(pe, k, s)
            wait_zT(pe, s)
            for i in range(2):
                pe.matmul(k.ps[:, 2 + i, :], W["ffn1"], k.zT[:, half(i)], start=True, stop=True).then_inc(turned[i], 1)
            for i in range(2):
                pe.wait_ge((copied_lo, copied_hi)[i], 1)
                pe.matmul(k.ps[:, 4 + i, :], W["ffn2"], a[:, half(i)], start=True, stop=True).then_inc(turned[i], 1)
            for i in range(2):
                pe.wait_ge((copied_lo, copied_hi)[i], 2)
                for t in range(4):
                    mm = pe.matmul(k.ps[:, 6 + i, tile(t)], b[:, tile(4 * i + t)], W["ffn3"], start=True, stop=True)
                mm.then_inc(last_ready, 1)


def store_phase(nc, k, out):
    stored = k.sem("stored")
    with nc.Block() as block:
        @block.sync
        def _(sp):
            sp.dma_start(out.rearrange("(t p) d -> p t d", p=P), k.x[:, :, :]).then_inc(stored, 16)
            sp.wait_ge(stored, 16)


def decoder(nc, ins, out):
    with ExitStack() as ctx:
        def sb(name, shape, dt=F32):
            return ctx.enter_context(nc.sbuf_tensor(name, shape, dt))
        k = Parts()
        k.sem = lambda name: ctx.enter_context(nc.semaphore(name))
        k.ps = ctx.enter_context(nc.psum_tensor("ps", [P, 8, 512], F32))
        k.x = sb("x", [P, NT, D])
        k.z = sb("z", [P, NT, D])
        k.zT = sb("zT", [P, T])
        k.ctxT = sb("ctxT", [P, T])
        k.stats = sb("stats", [P, NT, 6])
        k.mv = sb("mv", [P, NT, 2])
        k.var = sb("var", [P, NT])
        k.rstd = sb("rstd", [P, NT])
        k.newton = sb("newton", [P, NT])
        k.const = sb("const", [P, CONST_COLS])
        k.ident = k.const[:, CONST_AT["ident"]]
        k.weights = sb("weights", [P, W_COLS])
        k.w = {n: k.weights[:, c] for n, c in W_AT.items()}
        k.wide = sb("wide", [P, WIDE_COLS])
        k.rows = sb("rows", [P, ROW_COLS])
        k.box5 = sb("box5", [P, 4 + 2 * H])
        k.size_waves = sb("size_waves", [P, 2, T])
        k.pairs = nc.dram_tensor("pair_features", (B, NPAIR, S, S), F32).ap()
        k.pairs_stored = k.sem("box_pairs_stored")
        k.x_loaded = k.sem("x_loaded")
        k.const_loaded = k.sem("const_loaded")
        k.weights_loaded = k.sem("weights_loaded")
        k.ctx_loaded = k.sem("ctx_loaded")
        k.rows_loaded = k.sem("rows_loaded")
        k.wide_loaded = k.sem("wide_loaded")
        k.x_final = k.sem("x_final")
        load_phase(nc, k, ins)
        box_prep_phase(nc, k, ins)
        scan_phase(nc, k)
        cross_phase(nc, k)
        moe_phase(nc, k, ins)
        rotary_phase(nc, k)
        box_phase(nc, k, ins)
        chain_phase(nc, k)
        store_phase(nc, k, out)





def heads_apart(w):
    out = np.zeros((w.shape[0], H, HS), np.float32)
    out[:, :, :HD] = w.reshape(-1, H, HD)
    return out.reshape(w.shape[0], H * HS)


def group_columns(bias, flags):
    out = np.zeros((NG, len(flags), G, HS), np.float32)
    out[:, :, :, :HD] = bias.reshape(NG, 1, G, HD)
    for i, rows in enumerate(flags):
        for r in rows:
            out[:, i, :, HD + r] = 1.0
    return np.ascontiguousarray(out.reshape(NG * len(flags), P).T)


def kernel(**inputs):
    import concourse.bacc as _bacc
    from concourse.bass_utils import run_bass_kernel_spmd as _run

    a = {n: np.asarray(v) for n, v in inputs.items()}
    pos = np.arange(S, dtype=np.float32)[:, None] * np.power(np.float32(10000.0), np.float32(2.0) * np.arange(
        HD // 2, dtype=np.float32) / np.float32(HD))[None, :]
    cos = np.tile(np.repeat(np.cos(pos), 2, 1), (1, H)).astype(np.float32)
    sin = np.tile(np.stack([-np.sin(pos), np.sin(pos)], -1).reshape(S, HD), (1, H)).astype(np.float32)
    parts = {
        "A": a["L0_attn_A"], "A_T": a["L0_attn_A"].T, "Bm": a["L0_attn_Bm"], "W_ctx_T": a["L0_attn_W_ctx"].T,
        "wq0": heads_apart(a["L0_xattn_Wq"].T), "wk0": heads_apart(a["L0_xattn_Wk"].T), "wv0": a["L0_xattn_Wv"].T,
        "wo0": a["L0_xattn_Wo"].T, "gate": a["L0_ffn_gate_w"], "wq1": a["L1_attn_w_q"].T, "wk1": a["L1_attn_w_k"].T,
        "wv1": a["L1_attn_w_v"].T, "wo1": a["L1_attn_w_o"].T, "ffn1": a["L1_ffn_weight"],
        "ffn2": a["L1_ffn_aux_weight1"], "ffn3": a["L1_ffn_aux_weight2"],
        "bq0": group_columns(a["L0_xattn_bq"], [()]), "bk0": group_columns(a["L0_xattn_bk"], [(0,), (1,)]),
        "bq2": a["L1_xattn_bq"].reshape(NC, P).T, "bk2": a["L1_xattn_bk"].reshape(NC, P).T,
        "wq2": a["L1_xattn_Wq"].T, "wk2": a["L1_xattn_Wk"].T, "wv2": a["L1_xattn_Wv"].T,
        "wo2": a["L1_xattn_Wo"].T.reshape(NC, P, D).transpose(1, 0, 2).reshape(P, NC * D),
        "bv0": a["L0_xattn_bv"], "bo0": a["L0_xattn_bo"], "bo2": a["L1_xattn_bo"], "ffn_b": a["L1_ffn_bias"],
        "bv2": a["L1_xattn_bv"],
        "ident": np.eye(P, dtype=np.float32), "cos": cos.reshape(KB, P, D).transpose(1, 0, 2).reshape(P, KB * D),
        "sin": sin.reshape(KB, P, D).transpose(1, 0, 2).reshape(P, KB * D),
        "rank": np.tile(np.arange(E, 0, -1, dtype=np.float32), (P, 1)),
    }

    def pack(names, axis=1):
        return np.ascontiguousarray(np.concatenate([parts[n] for n, _ in names], axis))

    arrays = {
        "x": a["x"].reshape(T, D), "ctx_T": np.ascontiguousarray(a["ctx_1024"].reshape(T, D).T),
        "const": pack(CONSTS), "weights": pack(WEIGHTS), "wide": pack(WIDE), "rows": pack(ROWS, 0),
        "w1": a["L0_ffn_w1"], "w2": a["L0_ffn_w2"],
    }
    arrays.update(box_arrays(a))
    nc = _bacc.Bacc("TRN2", target_bir_lowering=False, num_devices=1)
    ins = {n: nc.dram_tensor(f"in_{n}", v.shape, mybir.dt.from_np(v.dtype), kind="ExternalInput").ap()
           for n, v in arrays.items()}
    out = nc.dram_tensor("out", (T, D), F32, kind="ExternalOutput").ap()
    decoder(nc, ins, out)
    r = _run(nc, [{f"in_{n}": v for n, v in arrays.items()}], core_ids=[0])
    return np.asarray(r.results[0]["out"]).reshape(B, S, D)
```

```python
from contextlib import ExitStack

import concourse.bass as bass
import numpy as np
from concourse import mybir

F32 = mybir.dt.float32
BF16 = mybir.dt.bfloat16
I32 = mybir.dt.int32
ALU = mybir.AluOpType
ACT = mybir.ActivationFunctionType
AX_X = mybir.AxisListType.X

B, S, D = 4, 256, 128
T = B * S
P = 128
NT = T // P
KB = S // P
H = 16
HD = D // H
G = 4
NG = H // G
HS = P // G
E, F = 8, 512
FC = F // P
DK = 64
NC = H * DK // P
EPS = 1e-5
RSQRT_GUESS = float(0x5F3759DF)

WEIGHTS = [("A", P), ("A_T", P), ("Bm", P), ("W_ctx_T", P), ("wq0", P), ("wk0", P),
           ("wv0", P), ("wo0", P), ("gate", E), ("wq1", P), ("wk1", P), ("wv1", P), ("wo1", P),
           ("ffn1", P), ("ffn2", P), ("ffn3", P), ("bq2", NC), ("bk2", NC)]
WIDE = [("wq2", H * DK), ("wk2", H * DK), ("wv2", H * DK), ("wo2", H * DK)]
ROWS = [("bq0", D), ("bk0", D), ("bv0", D), ("bo0", D), ("bo2", D), ("ffn_b", D), ("bv2", H * DK)]
CONSTS = [("ident", P), ("cos", KB * P), ("sin", KB * P), ("rank", E), ("minus", KB * H)]


def columns(parts):
    at, out = 0, {}
    for name, n in parts:
        out[name] = slice(at, at + n)
        at += n
    return out, at


W_AT, W_COLS = columns(WEIGHTS)
WIDE_AT, WIDE_COLS = columns(WIDE)
ROW_AT, ROW_COLS = columns(ROWS)
CONST_AT, CONST_COLS = columns(CONSTS)


class Parts:
    pass


class Link:

    def __init__(self, eng, sem, before=0):
        self.eng, self.sem, self.n = eng, sem, before

    def __call__(self, ins):
        self.n += 1
        ins.then_inc(self.sem, 1)
        self.eng.wait_ge(self.sem, self.n)


def half(t4):
    return slice(t4 * 512, t4 * 512 + 512)


def tile(t):
    return slice(t * P, t * P + P)



NORM_STEPS = 13


def norm_sems(k, name):
    s = Parts()
    s.nth = k.norms
    k.norms += 1
    s.norm_step, s.z_ready, s.zT_in_psum, s.zT_lo, s.zT_hi = k.norm_sems
    return s


def norm_vector(dve, k, s):
    step = Link(dve, s.norm_step, s.nth * NORM_STEPS)
    for t in range(NT):
        ins = dve.bn_stats(k.stats[:, t, :], k.x[:, t, :])
    step(ins)
    for t in range(NT):
        ins = dve.bn_aggr(k.mv[:, t, :], k.stats[:, t, :])
    step(ins)
    step(dve.tensor_scalar(k.var[:, :], k.mv[:, :, 1], EPS, None, ALU.add))
    step(dve.tensor_scalar(k.rstd[:, :].bitcast(I32), k.var[:, :].bitcast(I32), -0.5, RSQRT_GUESS,
                           ALU.mult, ALU.add))
    for _ in range(3):
        step(dve.tensor_tensor(k.newton[:, :], k.rstd[:, :], k.rstd[:, :], ALU.mult))
        step(dve.scalar_tensor_tensor(out=k.newton[:, :], in0=k.newton[:, :], scalar=-0.5, in1=k.var[:, :],
                                      op0=ALU.mult, op1=ALU.mult))
        step(dve.scalar_tensor_tensor(out=k.rstd[:, :], in0=k.newton[:, :], scalar=1.5, in1=k.rstd[:, :],
                                      op0=ALU.add, op1=ALU.mult))
    for t in range(NT):
        dve.tensor_scalar(k.z[:, t, :], k.x[:, t, :], k.mv[:, t, 0:1], k.rstd[:, t:t + 1],
                          ALU.subtract, ALU.mult).then_inc(s.z_ready, 1)
    dve.wait_ge(s.zT_in_psum, s.nth * NT + NT // 2)
    dve.tensor_copy(k.zT[:, half(0)], k.ps[:, 0, :]).then_inc(s.zT_lo, 1)


def norm_tensor(pe, k, s):
    for t in range(NT):
        pe.wait_ge(s.z_ready, s.nth * NT + t + 1)
        pe.transpose(k.ps[:, t // 4, tile(t % 4)], k.z[:, t, :], k.ident).then_inc(s.zT_in_psum, 1)


def norm_scalar(act, k, s):
    act.wait_ge(s.zT_in_psum, s.nth * NT + NT)
    act.activation(k.zT[:, half(1)], k.ps[:, 1, :], ACT.Copy).then_inc(s.zT_hi, 1)


def wait_zT(eng, s):
    eng.wait_ge(s.zT_lo, s.nth + 1)
    eng.wait_ge(s.zT_hi, s.nth + 1)



def load_phase(nc, k, ins):
    with nc.Block() as block:
        @block.sync
        def _(sp):
            sp.dma_start(k.x[:, :, :], ins["x"].rearrange("(t p) d -> p t d", p=P)).then_inc(k.x_loaded, 16)
            sp.dma_start(k.const[:, :], ins["const"]).then_inc(k.const_loaded, 16)
            sp.dma_start(k.weights[:, :], ins["weights"]).then_inc(k.weights_loaded, 16)
            sp.dma_start(k.ctxT[:, :], ins["ctx_T"]).then_inc(k.ctx_loaded, 16)
            sp.dma_start(k.rows[:, :], ins["rows"].partition_broadcast(P)).then_inc(k.rows_loaded, 16)

        @block.scalar
        def _(act):
            act.wait_ge(k.const_loaded, 16)
            act.activation(k.identb[:, :], k.ident, ACT.Copy)
            act.activation(k.minus[:, :, :], k.const[:, CONST_AT["minus"]].unsqueeze(2).broadcast_to([P, KB * H, P]),
                           ACT.Copy)



LEVELS = S.bit_length() - 1


def scan_phase(nc, k):
    s = norm_sems(k, "scan")
    power_step = k.sem("scan_power_in_psum")
    power_dve = k.sem("scan_power_copied")
    power_act = k.sem("scan_power_T_copied")
    level_done = [k.sem(f"scan_level_done_{i}") for i in range(2)]
    copied = [k.sem(f"scan_copied_{i}") for i in range(2)]
    out_ready = k.sem("scan_out_ready")
    W = k.w
    with ExitStack() as ctx:
        powers = ctx.enter_context(nc.sbuf_tensor("powers", [P, LEVELS, 2, P], F32))
        hs = ctx.enter_context(nc.sbuf_tensor("scan_h", [P, T], F32))
        block = ctx.enter_context(nc.Block())

        def power(level, transposed):
            if level == 0:
                return W["A_T" if transposed else "A"]
            return powers[:, level, transposed, :]

        @block.vector
        def _(dve):
            dve.wait_ge(k.x_loaded, 16)
            norm_vector(dve, k, s)
            for level in range(1, LEVELS):
                dve.wait_ge(power_step, level)
                dve.tensor_copy(powers[:, level, 0, :], k.ps[:, 6, 0:P]).then_inc(power_dve, 1)
            for level in range(LEVELS + 1):
                dve.wait_ge(level_done[0], level + 1)
                dve.tensor_copy(hs[:, half(0)], k.ps[:, 2, :]).then_inc(copied[0], 1)
            dve.wait_ge(out_ready, 1)
            dve.tensor_tensor(k.x[:, 0:4, :], k.x[:, 0:4, :], k.ps[:, 4, :].rearrange("p (t d) -> p t d", d=D), ALU.add)
            dve.wait_ge(out_ready, 2)
            dve.tensor_tensor(k.x[:, 4:8, :], k.x[:, 4:8, :], k.ps[:, 5, :].rearrange("p (t d) -> p t d", d=D), ALU.add)

        @block.scalar
        def _(act):
            norm_scalar(act, k, s)
            for level in range(1, LEVELS):
                act.wait_ge(power_step, level)
                act.activation(powers[:, level, 1, :], k.ps[:, 7, 0:P], ACT.Copy).then_inc(power_act, 1)
            for level in range(LEVELS + 1):
                act.wait_ge(level_done[1], level + 1)
                act.activation(hs[:, half(1)], k.ps[:, 3, :], ACT.Copy).then_inc(copied[1], 1)

        @block.tensor
        def _(pe):
            pe.wait_ge(k.const_loaded, 16)
            norm_tensor(pe, k, s)
            pe.wait_ge(k.weights_loaded, 16)

            def square(level):
                if level > 1:
                    pe.wait_ge(power_dve, level - 1)
                    pe.wait_ge(power_act, level - 1)
                pe.matmul(k.ps[:, 6, 0:P], power(level - 1, 1), power(level - 1, 0), start=True, stop=True)
                pe.matmul(k.ps[:, 7, 0:P], power(level - 1, 0), power(level - 1, 1), start=True,
                          stop=True).then_inc(power_step, 1)

            for level in range(1, LEVELS):
                square(level)
            wait_zT(pe, s)
            for i in range(2):
                pe.matmul(k.ps[:, 2 + i, :], W["Bm"], k.zT[:, half(i)], start=True, stop=True,
                          skip_group_check=True).then_inc(level_done[i], 1)
            pe.wait_ge(power_dve, LEVELS - 1)
            for level in range(LEVELS):
                shift = 1 << level
                for i in range(2):
                    pe.wait_ge(copied[i], level + 1)
                    for b in range(2):
                        at = b * S
                        mm = pe.matmul(k.ps[:, 2 + i, at + shift:at + S], power(level, 0),
                                       hs[:, i * 512 + at:i * 512 + at + S - shift], start=False, stop=True,
                                       skip_group_check=True)
                    mm.then_inc(level_done[i], 1)
            for i in range(2):
                pe.wait_ge(copied[i], LEVELS + 1)
                for t in range(4):
                    mm = pe.matmul(k.ps[:, 4 + i, tile(t)], hs[:, tile(4 * i + t)], W["W_ctx_T"],
                                   start=True, stop=True)
                mm.then_inc(out_ready, 1)



SEG = 64
NSEG = 6
PAIRS = H // 2


class Ring:

    def __init__(self, k, name, plan, users, places):
        self.users, self.places = users, places
        self.steps = [item for item in plan if item[0] in users]
        self.at = {item: n for n, item in enumerate(self.steps)}
        self.ready = k.sem(f"{name}_ready")
        self.freed = {e: k.sem(f"{name}_freed_{e}") for e in ("act", "dve") if any(e in u for u in users.values())}

    def place(self, item):
        return self.places[self.at[item] % len(self.places)]

    def wait_free(self, pe, item):
        n = self.at[item] - len(self.places)
        if n >= 0:
            self.wait_read(pe, self.steps[n])

    def wait_read(self, eng, item, of=None):
        for user in self.users[item[0]]:
            if of in (None, user):
                count = sum(user in self.users[i[0]] for i in self.steps[:self.at[item] + 1])
                eng.wait_ge(self.freed[user], count)

    def wait_ready(self, eng, item):
        eng.wait_ge(self.ready, self.at[item] + 1)


def narrow_plan():
    def scores(b):
        return [("S", b, i, j) for i in range(KB) for j in range(PAIRS)] if b < B else []

    plan = [("A", 0, 0), ("A", 0, 1)] + scores(0) + [("A", 1, 0), ("A", 1, 1)]
    for b in range(B):
        plan.append(("M", b))
        sc = scores(b + 1)
        late = []
        for n in range(NG * KB):
            j, kb = n // KB, n % KB
            plan += [("X", b, j, kb, 0)] + sc[:1] + [("X", b, j, kb, 1)] + sc[1:2]
            sc = sc[2:]
            plan += late
            late = [("P", b, j, kb)]
            if b >= 1 and n in (1, 3):
                plan.append(("T", b - 1, n // 2))
            if b + 2 < B and n in (5, 7):
                plan.append(("A", b + 2, n // 2 - 2))
        plan += late
    return plan + [("T", B - 1, 0), ("T", B - 1, 1)]


def narrow_sems(k, name):
    s = norm_sems(k, name)
    s.bias_added = k.sem(f"{name}_bias_added")
    s.prep = k.sem(f"{name}_prep")
    s.proj_ready = k.sem(f"{name}_proj_ready")
    s.v_copied = k.sem(f"{name}_v_copied")
    s.full_ready = {"q": k.sem(f"{name}_q_full"), "k": k.sem(f"{name}_k_full")}
    s.high_ready = {"q": k.sem(f"{name}_q_high"), "k": k.sem(f"{name}_k_high")}
    s.rest_ready = {"q": k.sem(f"{name}_q_rest"), "k": k.sem(f"{name}_k_rest")}
    s.middle_ready = {"q": k.sem(f"{name}_q_middle"), "k": k.sem(f"{name}_k_middle")}
    s.split_ready = {"q": k.sem(f"{name}_q_split"), "k": k.sem(f"{name}_k_split")}
    s.top_step = k.sem(f"{name}_top_step")
    s.top_ready = k.sem(f"{name}_top_ready")
    s.gap_ready = k.sem(f"{name}_gap_ready")
    s.gap_exp = k.sem(f"{name}_gap_exp")
    s.mix_step = k.sem(f"{name}_mix_step")
    s.attT_ready = k.sem(f"{name}_attT_ready")
    s.attT_lo = k.sem(f"{name}_attT_lo")
    s.attT_hi = k.sem(f"{name}_attT_hi")
    s.out_ready = k.sem(f"{name}_out_ready")
    plan = narrow_plan()
    s.plan = plan
    s.turned = Ring(k, f"{name}_turned", plan, {"A": ("act", "dve"), "M": ("dve",), "T": ("dve",)}, [6])
    s.scores = Ring(k, f"{name}_scores", plan, {"S": ("dve",)}, [0, 1])
    s.scoresT = Ring(k, f"{name}_scoresT", plan, {"X": ("act",)}, [2, 3])
    s.pv_ready = k.sem(f"{name}_pv_ready")
    s.pv_copied = k.sem(f"{name}_pv_copied")
    return s


def narrow_buffers(nc, k, ctx, sublayer):
    def sb(name, shape, dt=F32):
        return ctx.enter_context(nc.sbuf_tensor(f"{sublayer}_{name}", shape, dt))
    n = Parts()
    n.full = {"q": sb("q_full", [P, NT, D]), "k": sb("k_full", [P, NT, D])}
    n.parts = {"q": sb("q_parts", [P, NT, H, SEG], BF16), "k": sb("k_parts", [P, NT, H, SEG], BF16)}
    n.q = sb("q", [P, H, T], BF16)
    n.k = sb("k", [P, PAIRS, T], BF16)
    n.v = sb("v", [P, NT, H, HS])
    n.top = sb("top", [P, NT, KB, H])
    n.rest = sb("top_rest", [P, KB, KB * H])
    n.top3 = sb("top3", [P, NT, P], BF16)
    n.topT = sb("topT", [P, T], BF16)
    n.e = sb("e", [P, 4, G, S])
    n.oT = sb("oT", [P, 2, NG, KB, S])
    n.att = k.z
    n.tmp = sb("products", [P, 2, NG, G, HD])
    n.mw = sb("block_weights", [P, NT, KB, H])
    n.mf = sb("factors", [P, 2, H])
    n.mt = sb("mix_tmp", [P, 2, H])
    n.ml = sb("mix_sum", [P, H])
    return n


HIGH_AT = {"q": [(0, 3, 1)], "k": [(0, 2, 3), (5, 1, 1)]}
MIDDLE_AT = {"q": [(3, 2, 1)], "k": [(1, 2, 3)]}
LOW_AT = {"q": 5, "k": 2}


def narrow_prepare(pool, n, s):
    step = Link(pool, s.prep)
    step(pool.memset(n.parts["q"][:, :, :, NSEG * HD:SEG], 0.0))
    step(pool.memset(n.parts["k"][:, :, :, NSEG * HD:SEG], 0.0))
    step(pool.memset(n.q[SEG:P, 0:H:2, :], 0.0))
    step(pool.memset(n.q[0:SEG, 1:H:2, :], 0.0))
    step(pool.memset(n.v[:, :, :, HD + 1:HS], 0.0))
    step(pool.memset(n.v[:, :, :, HD:HD + 1], 1.0))
    step(pool.memset(n.top3[:, :, :], 0.0))


PREPARED = 7


def segments(n, which, i, at):
    first, count, by = at
    v = n.parts[which][:, 4 * i:4 * i + 4, :, 0:NSEG * HD].rearrange("p t h (g c) -> p (t h) g c", c=HD)
    return v[:, :, first:first + (count - 1) * by + 1:by, :]


def heads_of(a, i):
    return a[:, 4 * i:4 * i + 4, :].rearrange("p t (h c) -> p (t h) c", c=HD)


def split_scalar(act, n, s, which, i):
    split_scalar_high(act, n, s, which, i)
    split_scalar_middle(act, n, s, which, i)


def split_scalar_high(act, n, s, which, i):
    act.wait_ge(s.full_ready[which], i + 1)
    for at in HIGH_AT[which]:
        src = heads_of(n.full[which], i).unsqueeze(2).broadcast_to([P, 4 * H, at[1], HD])
        ins = act.activation(segments(n, which, i, at), src, ACT.Copy)
    ins.then_inc(s.high_ready[which], 1)


def split_scalar_middle(act, n, s, which, i):
    act.wait_ge(s.rest_ready[which], i + 1)
    for at in MIDDLE_AT[which]:
        src = heads_of(n.full[which], i).unsqueeze(2).broadcast_to([P, 4 * H, at[1], HD])
        ins = act.activation(segments(n, which, i, at), src, ACT.Copy)
    ins.then_inc(s.middle_ready[which], 1)


def split_vector(dve, n, s, which, i):
    full = heads_of(n.full[which], i)
    dve.wait_ge(s.high_ready[which], i + 1)
    dve.tensor_tensor(full, full, segments(n, which, i, (HIGH_AT[which][0][0], 1, 1))[:, :, 0, :], ALU.subtract)\
       .then_inc(s.rest_ready[which], 1)
    dve.wait_ge(s.middle_ready[which], i + 1)
    dve.tensor_tensor(segments(n, which, i, (LOW_AT[which], 1, 1))[:, :, 0, :], full,
                      segments(n, which, i, (MIDDLE_AT[which][0][0], 1, 1))[:, :, 0, :], ALU.subtract)\
       .then_inc(s.split_ready[which], 1)


def narrow_tensor(pe, k, n, s, kinds):
    for item in s.plan:
        kind, b = item[:2]
        ring = {"A": s.turned, "M": s.turned, "T": s.turned, "S": s.scores, "X": s.scoresT}.get(kind)
        if ring:
            bank = ring.place(item)
            ring.wait_free(pe, item)
        if kind == "A":
            t = KB * b + item[2]
            for which, to in (("q", bank), ("k", bank + 1)):
                pe.wait_ge(s.split_ready[which], t // 4 + 1)
                for j in range(PAIRS):
                    mm = pe.transpose(k.ps[:, to, :].bitcast(BF16)[:, tile(j)],
                                      n.parts[which][:, t, 2 * j:2 * j + 2, :], k.identb[:, :])
        elif kind == "S":
            t = KB * b + item[2]
            s.turned.wait_read(pe, ("A", b, 1))
            for h in (2 * item[3], 2 * item[3] + 1):
                mm = pe.matmul(k.ps[:, bank, h % 2 * S:h % 2 * S + S], n.q[:, h, tile(t)],
                               n.k[:, h // 2, b * S:b * S + S], start=True, stop=True)
        elif kind == "M":
            pe.wait_ge(s.top_ready, b + 1)
            for i in range(KB):
                mm = pe.transpose(k.ps[:, bank, :].bitcast(BF16)[:, tile(i)], n.top3[:, KB * b + i, :], k.identb[:, :])
        elif kind == "X":
            j, kb = item[2:4]
            s.turned.wait_read(pe, ("M", b))
            for i in range(2):
                h = G * j + 2 * item[4] + i
                at = k.ps[:, bank, i * S:i * S + S]
                pe.matmul(at, n.k[:, h // 2, tile(KB * b + kb)], n.q[:, h, b * S:b * S + S], start=True, stop=False,
                          skip_group_check=True)
                mm = pe.matmul(at, k.minus[:, kb * (kinds - 1) * H + h, :], n.topT[:, b * S:b * S + S], start=False,
                               stop=True, skip_group_check=True)
        elif kind == "P":
            j, kb = item[2:4]
            u = NG * b + j
            s.scoresT.wait_read(pe, ("X", b, j, kb, 1))
            if kb == 0 and u >= 2:
                pe.wait_ge(s.pv_copied, u - 1)
            at = kb * S if kinds == 2 else 0
            for g in range(G):
                mm = pe.matmul(k.ps[HS * g:HS * g + HS, 4 + u % 2, at:at + S], n.v[:, KB * b + kb, G * j + g, :],
                               n.e[:, (KB * u + kb) % 4, g, :], start=(kb == 0 or kinds == 2),
                               stop=(kb == 1 or kinds == 2), skip_group_check=True)
            mm.then_inc(s.pv_ready, 1)
        elif kind == "T":
            pe.wait_ge(s.pv_copied, NG * (b + 1))
            for j in range(NG):
                for kd in range(kinds):
                    to = (2 * j + kd) * P if kinds == 2 else j * P
                    mm = pe.transpose(k.ps[:, bank + to // 512, to % 512:to % 512 + P],
                                      n.oT[:, b % 2, j, kd, tile(item[2])], k.ident)
        if ring:
            mm.then_inc(ring.ready, 1)


def narrow_scalar(act, k, n, s, scale):
    for item in s.plan:
        kind, b = item[:2]
        if kind == "A":
            t = KB * b + item[2]
            s.turned.wait_ready(act, item)
            src = k.ps[:, s.turned.place(item), :].bitcast(BF16).rearrange("p (j c) -> p j c", c=P)
            act.activation(n.q[0:SEG, 0:H:2, tile(t)], src[0:SEG], ACT.Copy)
            act.activation(n.q[SEG:P, 1:H:2, tile(t)], src[SEG:P], ACT.Copy).then_inc(s.turned.freed["act"], 1)
        elif kind == "X":
            u = NG * b + item[2]
            r = KB * u + item[3]
            s.scoresT.wait_ready(act, item)
            if r >= 4:
                act.wait_ge(s.pv_ready, r - 3)
            act.activation(n.e[:, r % 4, 2 * item[4]:2 * item[4] + 2, :].rearrange("p g c -> p (g c)"),
                           k.ps[:, s.scoresT.place(item), :], ACT.Exp, scale=scale).then_inc(s.scoresT.freed["act"], 1)
            if kind == "X" and item[2:] == (0, 0, 0) and n.gaps:
                act.wait_ge(s.gap_ready, b + 1)
                gap = n.mw[:, KB * b:KB * b + KB, :, :]
                act.activation(gap, gap, ACT.Exp, scale=scale).then_inc(s.gap_exp, 1)


def narrow_vector(dve, k, n, s, kinds):
    top = Link(dve, s.top_step)
    step = Link(dve, s.mix_step)

    def split_top(b):
        m = n.top[:, KB * b:KB * b + KB, 0:kinds, :].rearrange("p t a h -> p t (a h)")
        rest = n.rest[:, :, 0:kinds * H]

        def part(i):
            return n.top3[:, KB * b:KB * b + KB, KB * H * i:KB * H * i + kinds * H]
        top(dve.tensor_copy(part(0), m))
        top(dve.tensor_tensor(rest, m, part(0), ALU.subtract))
        top(dve.tensor_copy(part(1), rest))
        dve.tensor_tensor(part(2), rest, part(1), ALU.subtract).then_inc(s.top_ready, 1)
        if kinds == 2:
            m, w = n.top[:, KB * b:KB * b + KB, :, :], n.mw[:, KB * b:KB * b + KB, :, :]
            top(dve.tensor_tensor(w[:, :, 0, :], m[:, :, 0, :], m[:, :, 1, :], ALU.subtract))
            top(dve.tensor_scalar(w[:, :, 1, :], w[:, :, 0, :], -1.0, 0.0, ALU.mult, ALU.min))
            dve.tensor_scalar(w[:, :, 0, :], w[:, :, 0, :], 0.0, None, ALU.min).then_inc(s.gap_ready, 1)

    def mix(b, i, bank):
        t = KB * b + i
        if kinds == 1:
            o = k.ps[:, bank, :].rearrange("p (a h c) -> p a h c", a=NG, h=G)
            f = n.mf[:, 0, :].rearrange("p (a h) -> p a h", h=G)
            step(dve.reciprocal(f, o[:, :, :, HD]))
            ins = dve.tensor_tensor(n.att[:, t, :].rearrange("p (a h c) -> p a h c", h=G, c=HD), o[:, :, :, 0:HD],
                                    f.unsqueeze(3).broadcast_to([P, NG, G, HD]), ALU.mult)
            ins.then_inc(s.turned.freed["dve"], 1)
            s.turned.wait_read(dve, ("T", b, i))
            return
        o = k.ps[:, bank:bank + 2, :].rearrange("p a (g j h c) -> p (a g) j h c", g=2, j=2, h=G)

        def grouped(a):
            return a.rearrange("p (a h) -> p a h", h=G)
        if i == 0:
            dve.wait_ge(s.gap_exp, b + 1)
        for kd in range(2):
            dve.tensor_tensor(grouped(n.mt[:, kd, :]), o[:, :, kd, :, HD], grouped(n.mw[:, t, kd, :]), ALU.mult)
        step(dve.reciprocal(grouped(n.mf[:, 0, :]), o[:, :, i, :, HD]))
        step(dve.tensor_tensor(n.ml[:, :], n.mt[:, 0, :], n.mt[:, 1, :], ALU.add))
        step(dve.reciprocal(n.ml[:, :], n.ml[:, :]))
        step(dve.tensor_tensor(n.mt[:, :, :], n.mw[:, t, :, :], n.ml[:, :].unsqueeze(1).broadcast_to([P, 2, H]), ALU.mult))
        step(dve.tensor_tensor(n.mt[:, i, :], n.mt[:, i, :], n.mf[:, 0, :], ALU.add))
        for kd in range(2):
            ins = dve.tensor_tensor(n.tmp[:, kd, :, :, :], o[:, :, kd, :, 0:HD],
                                    grouped(n.mt[:, kd, :]).unsqueeze(3).broadcast_to([P, NG, G, HD]), ALU.mult)
        step(ins)
        dve.tensor_tensor(n.att[:, t, :].rearrange("p (a h c) -> p a h c", h=G, c=HD), n.tmp[:, 0, :, :, :],
                          n.tmp[:, 1, :, :, :], ALU.add).then_inc(s.turned.freed["dve"], 1)
        s.turned.wait_read(dve, ("T", b, i))

    for item in s.plan:
        kind, b = item[:2]
        ring = {"A": s.turned, "M": s.turned, "T": s.turned, "S": s.scores}.get(kind)
        if ring:
            ring.wait_ready(dve, item)
            bank = ring.place(item)
        if kind == "A":
            t = KB * b + item[2]
            ins = dve.tensor_copy(n.k[:, :, tile(t)], k.ps[:, bank + 1, :].bitcast(BF16).rearrange("p (j c) -> p j c", c=P))
        elif kind == "S":
            t = KB * b + item[2]
            out = n.top[:, t, 0:kinds, 2 * item[3]:2 * item[3] + 2].rearrange("p a h -> p h a")
            ins = dve.tensor_reduce(out, k.ps[:, bank, :].rearrange("p (h a c) -> p h a c", h=2, a=kinds), AX_X, ALU.max)
        elif kind == "M":
            ins = dve.tensor_copy(n.topT[:, b * S:b * S + S], k.ps[:, bank, :].bitcast(BF16)[:, 0:S])
        elif kind == "T":
            mix(b, item[2], bank)
        if ring and kind != "T":
            ins.then_inc(ring.freed["dve"], 1)
        if kind == "S" and item[2:] == (KB - 1, PAIRS - 1):
            s.scores.wait_read(dve, item)
            if b >= 1:
                dve.wait_ge(s.top_ready, b)
            split_top(b)
        if kind == "P" and item[3] == KB - 1:
            u = NG * b + item[2]
            dve.wait_ge(s.pv_ready, KB * (u + 1))
            dve.tensor_copy(n.oT[:, b % 2, item[2], 0:kinds, :],
                            k.ps[:, 4 + u % 2, 0:kinds * S].rearrange("p (a c) -> p a c", c=S)).then_inc(s.pv_copied, 1)


def project_tensor(pe, k, s, att, w):
    for t in range(NT):
        s.turned.wait_read(pe, ("T", t // KB, t % KB))
        pe.transpose(k.ps[:, t // 4, tile(t % 4)], att[:, t, :], k.ident).then_inc(s.attT_ready, 1)
    pe.wait_ge(s.attT_lo, 1)
    for t in range(NT):
        if t == 4:
            pe.wait_ge(s.attT_hi, 1)
        pe.matmul(k.ps[:, 2 + t // 4, tile(t % 4)], k.zT[:, tile(t)], w, start=True, stop=True)\
          .then_inc(s.out_ready, 1)


def project_scalar(act, k, s):
    act.wait_ge(s.attT_ready, NT)
    act.activation(k.zT[:, half(1)], k.ps[:, 1, :], ACT.Copy).then_inc(s.attT_hi, 1)


def project_vector(dve, k, s):
    dve.wait_ge(s.attT_ready, NT // 2)
    dve.tensor_copy(k.zT[:, half(0)], k.ps[:, 0, :]).then_inc(s.attT_lo, 1)
    for i in range(2):
        dve.wait_ge(s.out_ready, 4 * (i + 1))
        dve.tensor_tensor(k.x[:, 4 * i:4 * i + 4, :], k.x[:, 4 * i:4 * i + 4, :],
                          k.ps[:, 2 + i, :].rearrange("p (t d) -> p t d", d=D), ALU.add)


def row_over_tiles(k, name, tiles):
    return k.rows[:, ROW_AT[name]].unsqueeze(1).broadcast_to([P, tiles, D])


def copy_values(dve, k, n, s, bank, before, bias):
    for i in range(2):
        dve.wait_ge(s.proj_ready, before + i + 1)
        src = k.ps[:, bank + i, :].rearrange("p (t h c) -> p t h c", t=4, c=HD)
        dst = n.v[:, 4 * i:4 * i + 4, :, 0:HD]
        if bias is None:
            ins = dve.tensor_copy(dst, src)
        else:
            ins = dve.tensor_tensor(dst, src, k.rows[:, ROW_AT[bias]].rearrange("p (h c) -> p h c", c=HD)
                                    .unsqueeze(1).broadcast_to([P, 4, H, HD]), ALU.add)
        ins.then_inc(s.v_copied, 1)


def project_in(pe, k, s, bank, lhsT, w):
    for i in range(2):
        for t in range(4):
            mm = pe.matmul(k.ps[:, bank + i, tile(t)], lhsT[:, tile(4 * i + t)], w, start=True, stop=True)
        mm.then_inc(s.proj_ready, 1)


def cross_phase(nc, k):
    s = narrow_sems(k, "cross")
    W = k.w
    with ExitStack() as ctx:
        n = narrow_buffers(nc, k, ctx, "cross")
        n.gaps = True
        block = ctx.enter_context(nc.Block())

        @block.gpsimd
        def _(pool):
            narrow_prepare(pool, n, s)

        @block.vector
        def _(dve):
            dve.wait_ge(k.rows_loaded, 16)

            def full(which, bank, before, i):
                dve.wait_ge(s.proj_ready, before + i + 1)
                dve.tensor_tensor(n.full[which][:, 4 * i:4 * i + 4, :], k.ps[:, bank + i, :].rearrange(
                    "p (t d) -> p t d", d=D), row_over_tiles(k, "b" + which + "0", 4), ALU.add)\
                   .then_inc(s.full_ready[which], 1)
            for i in range(2):
                full("k", 2, 0, i)
            norm_vector(dve, k, s)
            dve.wait_ge(s.prep, PREPARED)
            full("q", 6, 4, 0)
            split_vector(dve, n, s, "k", 0)
            split_vector(dve, n, s, "q", 0)
            full("q", 6, 4, 1)
            copy_values(dve, k, n, s, 4, 2, "bv0")
            dve.wait_ge(s.zT_hi, s.nth + 1)
            dve.tensor_tensor(k.x[:, :, :], k.x[:, :, :], row_over_tiles(k, "bo0", NT), ALU.add).then_inc(s.bias_added, 1)
            split_vector(dve, n, s, "k", 1)
            split_vector(dve, n, s, "q", 1)
            narrow_vector(dve, k, n, s, 2)
            dve.wait_ge(s.bias_added, 1)
            project_vector(dve, k, s)

        @block.scalar
        def _(act):
            act.wait_ge(s.prep, PREPARED)
            split_scalar_high(act, n, s, "k", 0)
            split_scalar_high(act, n, s, "k", 1)
            norm_scalar(act, k, s)
            split_scalar_middle(act, n, s, "k", 0)
            split_scalar(act, n, s, "q", 0)
            split_scalar_middle(act, n, s, "k", 1)
            split_scalar(act, n, s, "q", 1)
            narrow_scalar(act, k, n, s, HD ** -0.5)
            project_scalar(act, k, s)

        @block.tensor
        def _(pe):
            pe.wait_ge(k.ctx_loaded, 16)
            project_in(pe, k, s, 2, k.ctxT, W["wk0"])
            project_in(pe, k, s, 4, k.ctxT, W["wv0"])
            norm_tensor(pe, k, s)
            wait_zT(pe, s)
            project_in(pe, k, s, 6, k.zT, W["wq0"])
            pe.wait_ge(s.full_ready["q"], 2)
            pe.wait_ge(s.full_ready["k"], 2)
            pe.wait_ge(s.v_copied, 2)
            narrow_tensor(pe, k, n, s, 2)
            project_tensor(pe, k, s, n.att, W["wo0"])



def moe_phase(nc, k, ins):
    s = norm_sems(k, "moe")
    loaded = k.sem("moe_weights_loaded")
    logits_ready = k.sem("moe_logits_ready")
    gate_step = k.sem("moe_gate_step")
    gap_ready = k.sem("moe_gap_ready")
    gap_exp = k.sem("moe_gap_exp")
    hidden_ready = k.sem("moe_hidden_ready")
    gelu_done = k.sem("moe_gelu_done")
    expert_ready = k.sem("moe_expert_ready")
    added = k.sem("moe_added")
    with ExitStack() as ctx:
        def sb(name, shape):
            return ctx.enter_context(nc.sbuf_tensor(name, shape, F32))
        w1 = sb("w1", [P, E, F])
        w2 = sb("w2", [P, E, FC, D])
        h = sb("hidden", [P, 2, FC, T])
        lg = sb("logits", [P, NT, E])
        cand = sb("candidates", [P, NT, E])
        pick1 = sb("pick1", [P, NT, E])
        pick2 = sb("pick2", [P, NT, E])
        comb = sb("comb", [P, NT, E])
        c1, c2, c3, c4 = (sb(f"moe_c{i}", [P, NT]) for i in range(4))
        block = ctx.enter_context(nc.Block())

        @block.sync
        def _(sp):
            sp.dma_start(w1[:, :, :], ins["w1"].rearrange("e d f -> d e f")).then_inc(loaded, 16)
            sp.dma_start(w2[:, :, :, :], ins["w2"].rearrange("e (c p) d -> p e c d", p=P)).then_inc(loaded, 16)

        @block.vector
        def _(dve):
            norm_vector(dve, k, s)
            step = Link(dve, gate_step)

            def wide(a):
                return a[:, :].unsqueeze(2).broadcast_to([P, NT, E])
            rank = k.const[:, CONST_AT["rank"]].unsqueeze(1).broadcast_to([P, NT, E])
            dve.wait_ge(logits_ready, 1)
            step(dve.tensor_copy(lg[:, :, :], k.ps[:, 2, 0:NT * E].rearrange("p (t e) -> p t e", e=E)))

            def best(top, pick):
                step(dve.tensor_reduce(top[:, :], lg[:, :, :], AX_X, ALU.max))
                step(dve.tensor_tensor(cand[:, :, :], lg[:, :, :], wide(top), ALU.is_equal))
                step(dve.tensor_tensor(cand[:, :, :], cand[:, :, :], rank, ALU.mult))
                step(dve.tensor_reduce(c3[:, :], cand[:, :, :], AX_X, ALU.max))
                step(dve.tensor_tensor(pick[:, :, :], cand[:, :, :], wide(c3), ALU.is_equal))

            best(c1, pick1)
            step(dve.scalar_tensor_tensor(out=lg[:, :, :], in0=pick1[:, :, :], scalar=-3e38, in1=lg[:, :, :],
                                          op0=ALU.mult, op1=ALU.add))
            best(c2, pick2)
            dve.tensor_tensor(c3[:, :], c2[:, :], c1[:, :], ALU.subtract).then_inc(gap_ready, 1)
            dve.wait_ge(gap_exp, 1)
            step(dve.tensor_scalar(c1[:, :], c4[:, :], 1.0, None, ALU.add))
            step(dve.reciprocal(c1[:, :], c1[:, :]))
            step(dve.tensor_tensor(pick2[:, :, :], pick2[:, :, :], wide(c4), ALU.mult))
            step(dve.tensor_tensor(comb[:, :, :], pick1[:, :, :], pick2[:, :, :], ALU.add))
            step(dve.tensor_tensor(comb[:, :, :], comb[:, :, :], wide(c1), ALU.mult))
            for e in range(E):
                for t in range(NT):
                    dve.wait_ge(expert_ready, e * NT + 4 * (t // 4) + 4)
                    if e >= 1:
                        dve.wait_ge(added, (e - 1) * NT + t + 1)
                    dve.scalar_tensor_tensor(out=k.x[:, t, :], in0=k.ps[:, 2 * (e % 2) + t // 4, tile(t % 4)],
                                             scalar=comb[:, t, e:e + 1], in1=k.x[:, t, :], op0=ALU.mult,
                                             op1=ALU.add).then_inc(added, 1)

        @block.scalar
        def _(act):
            norm_scalar(act, k, s)
            act.wait_ge(gap_ready, 1)
            act.activation(c4[:, :], c3[:, :], ACT.Exp).then_inc(gap_exp, 1)
            for i in range(E * 2 * FC):
                e, c, part = i // (2 * FC), i // 2 % FC, i % 2
                act.wait_ge(hidden_ready, i + 1)
                if e >= 2:
                    act.wait_ge(expert_ready, (e - 1) * NT)
                act.activation(h[:, e % 2, c, half(part)], k.ps[:, 4 + i % 4, :], ACT.Gelu_apprx_tanh)\
                   .then_inc(gelu_done, 1)

        @block.tensor
        def _(pe):
            norm_tensor(pe, k, s)
            wait_zT(pe, s)
            for t in range(NT):
                mm = pe.matmul(k.ps[:, 2, t * E:t * E + E], k.zT[:, tile(t)], k.w["gate"], start=True, stop=True)
            mm.then_inc(logits_ready, 1)
            pe.wait_ge(loaded, 32)

            def hidden(i):
                e, c, part = i // (2 * FC), i // 2 % FC, i % 2
                if i >= 4:
                    pe.wait_ge(gelu_done, i - 3)
                pe.matmul(k.ps[:, 4 + i % 4, :], w1[:, e, tile(c)], k.zT[:, half(part)], start=True,
                          stop=True).then_inc(hidden_ready, 1)

            def expert(e, t):
                pe.wait_ge(gelu_done, (e + 1) * 2 * FC)
                if e == 1:
                    pe.wait_ge(gate_step, 1)
                if e >= 2:
                    pe.wait_ge(added, (e - 2) * NT + 4 * (t // 4) + 4)
                for c in range(FC):
                    mm = pe.matmul(k.ps[:, 2 * (e % 2) + t // 4, tile(t % 4)], h[:, e % 2, c, tile(t)],
                                   w2[:, e, c, :], start=(c == 0), stop=(c == FC - 1))
                mm.then_inc(expert_ready, 1)

            for e in range(E + 1):
                for i in range(NT):
                    if e < E:
                        hidden(e * NT + i)
                    if e >= 1:
                        expert(e - 1, i)



def rotary_phase(nc, k):
    s = narrow_sems(k, "rotary")
    rope_step = k.sem("rotary_rope_step")
    W = k.w
    with ExitStack() as ctx:
        n = narrow_buffers(nc, k, ctx, "rotary")
        n.gaps = False
        block = ctx.enter_context(nc.Block())

        @block.gpsimd
        def _(pool):
            narrow_prepare(pool, n, s)

        @block.vector
        def _(dve):
            step = Link(dve, rope_step)

            def rope(bank, i, which, before):
                dve.wait_ge(s.proj_ready, before + i + 1)
                src = k.ps[:, bank + i, :].rearrange("p (b c) -> p b c", b=2)
                pairs = k.ps[:, bank + i, :].rearrange("p (b c two) -> p b c two", b=2, two=2)
                by_cos = n.att[:, 0:4, :].rearrange("p t c -> p (t c)")
                by_sin = n.att[:, 4:8, :].rearrange("p t c -> p (t c)")
                sin = k.const[:, CONST_AT["sin"]].rearrange("p (c two) -> p c two", two=2)
                dve.tensor_tensor(by_cos.rearrange("p (b c) -> p b c", b=2), src,
                                  k.const[:, CONST_AT["cos"]].unsqueeze(1).broadcast_to([P, 2, KB * P]), ALU.mult)
                for even in range(2):
                    ins = dve.tensor_tensor(by_sin.rearrange("p (b c two) -> p b c two", b=2, two=2)[:, :, :, even],
                                            pairs[:, :, :, 1 - even],
                                            sin[:, :, even].unsqueeze(1).broadcast_to([P, 2, KB * P // 2]), ALU.mult)
                step(ins)
                dve.tensor_tensor(n.full[which][:, 4 * i:4 * i + 4, :].rearrange("p t c -> p (t c)"), by_cos, by_sin,
                                  ALU.add).then_inc(s.full_ready[which], 1)
                dve.wait_ge(s.full_ready[which], i + 1)

            norm_vector(dve, k, s)
            dve.wait_ge(s.prep, PREPARED)
            rope(2, 0, "q", 0)
            rope(4, 0, "k", 2)
            split_vector(dve, n, s, "q", 0)
            rope(2, 1, "q", 0)
            split_vector(dve, n, s, "k", 0)
            rope(4, 1, "k", 2)
            copy_values(dve, k, n, s, 6, 4, None)
            split_vector(dve, n, s, "q", 1)
            split_vector(dve, n, s, "k", 1)
            narrow_vector(dve, k, n, s, 1)
            project_vector(dve, k, s)

        @block.scalar
        def _(act):
            norm_scalar(act, k, s)
            act.wait_ge(s.prep, PREPARED)
            for i in range(2):
                split_scalar_high(act, n, s, "q", i)
                split_scalar_high(act, n, s, "k", i)
                split_scalar_middle(act, n, s, "q", i)
                split_scalar_middle(act, n, s, "k", i)
            narrow_scalar(act, k, n, s, HD ** -0.5)
            project_scalar(act, k, s)

        @block.tensor
        def _(pe):
            norm_tensor(pe, k, s)
            wait_zT(pe, s)
            project_in(pe, k, s, 2, k.zT, W["wq1"])
            project_in(pe, k, s, 4, k.zT, W["wk1"])
            project_in(pe, k, s, 6, k.zT, W["wv1"])
            pe.wait_ge(s.full_ready["q"], 2)
            pe.wait_ge(s.full_ready["k"], 2)
            pe.wait_ge(s.v_copied, 2)
            narrow_tensor(pe, k, n, s, 1)
            project_tensor(pe, k, s, n.att, W["wo1"])



QG = 16
NQ = S // QG
NPAIR = 4
RPAIR = NPAIR * QG
RSUM = 5
ROUND = 1.5 * 2.0 ** 23
TWO_PI_HI = 6.28125
TWO_PI_LO = float(2.0 * np.pi - 6.28125)
BELOW_PI = 3.1415925
U = DK + 1


def box_prep_phase(nc, k, ins):
    box_in = k.sem("box_inputs")
    centre_step = k.sem("box_centre_step")
    apart = k.sem("box_apart")
    absolute = k.sem("box_absolute")
    clipped = k.sem("box_clipped")
    logged = k.sem("box_logged")
    turns_ready = k.sem("box_turns")
    angle_step = k.sem("box_angle_step")
    angle_ready = k.sem("box_angle_ready")
    sine_done = k.sem("box_sine_done")
    half_sine_step = k.sem("box_half_sine_step")
    half_sine = k.sem("box_half_sine")
    features = k.sem("box_features")
    size_step = k.sem("box_size_step")
    size_ready = k.sem("box_size_ready")
    size_log = k.sem("box_size_log")
    size_angle = k.sem("box_size_angle")
    size_sine = k.sem("box_size_sine")
    with ExitStack() as ctx:
        def sb(name, shape):
            return ctx.enter_context(nc.sbuf_tensor(name, shape, F32))
        rows = sb("box_rows", [P, 4, T])
        own = sb("box_own", [P, NT, 4])
        ckey = sb("box_centre_key", [P, 2, T])
        cown = sb("box_centre_own", [P, NT, 2])
        size = sb("box_size_own", [P, NT, 2])
        d = sb("box_distance", [P, NT, 2, S])
        turns = sb("box_turns_of", [P, NT, 2, S])
        feat = sb("box_feat", [P, NT, NPAIR, S])
        ends = sb("box_ends", [P, 2, T])
        y5 = sb("box_y5", [P, 2, T])
        t5 = sb("box_t5", [P, 2, T])
        block = ctx.enter_context(nc.Block())
        r5 = slice(RPAIR, RPAIR + RSUM)

        @block.sync
        def _(sp):
            sp.dma_start(rows[:, :, :], ins["box_rows"].partition_broadcast(P)).then_inc(box_in, 16)
            sp.dma_start(own[:, :, :], ins["boxes"].rearrange("(t p) c -> p t c", p=P)).then_inc(box_in, 16)
            sp.dma_start(ends[r5, :, :], ins["box_ends"]).then_inc(box_in, 16)
            sp.dma_start(k.box5[r5, :], ins["box5"]).then_inc(box_in, 16)
            for t in range(NT):
                b, i = t // KB, t % KB
                sp.wait_ge(sine_done, b + 1)
                sp.wait_ge(features, b + 1)
                sp.dma_start(k.pairs[b, :, i * P:i * P + P, :].rearrange("f q m -> q f m"), feat[:, t, :, :])\
                  .then_inc(k.pairs_stored, 16)
            sp.wait_ge(k.pairs_stored, 16 * NT)

        @block.vector
        def _(dve):
            step = Link(dve, centre_step)
            dve.wait_ge(box_in, 64)
            step(dve.tensor_tensor(ckey[:, :, :], rows[:, 0:2, :], rows[:, 2:4, :], ALU.add))
            step(dve.tensor_scalar(ckey[:, :, :], ckey[:, :, :], 0.5, None, ALU.mult))
            step(dve.tensor_tensor(cown[:, :, :], own[:, :, 0:2], own[:, :, 2:4], ALU.add))
            step(dve.tensor_scalar(cown[:, :, :], cown[:, :, :], 0.5, None, ALU.mult))
            step(dve.tensor_tensor(size[:, :, :], own[:, :, 2:4], own[:, :, 0:2], ALU.subtract))
            step(dve.tensor_scalar(size[:, :, :], size[:, :, :], 1.0, None, ALU.add))
            step(dve.reciprocal(size[:, :, :], size[:, :, :]))
            for b in range(B):
                for t in range(KB * b, KB * b + KB):
                    for c in range(2):
                        ins_ = dve.tensor_scalar(d[:, t, c, :], ckey[:, c, b * S:b * S + S], cown[:, t, c:c + 1],
                                                 None, ALU.subtract)
                ins_.then_inc(apart, 1)
            five = Link(dve, size_step)
            five(dve.tensor_tensor(y5[r5, 0, :], ends[r5, 0, :], ends[r5, 1, :], ALU.subtract))
            dve.tensor_scalar(y5[r5, 0, :], y5[r5, 0, :], 1.0, None, ALU.add).then_inc(size_ready, 1)
            for b in range(B):
                dve.wait_ge(absolute, b + 1)
                dve.tensor_scalar(d[:, 2 * b:2 * b + 2, :, :], d[:, 2 * b:2 * b + 2, :, :], 1e-3, None, ALU.max)\
                   .then_inc(clipped, 1)
            dve.wait_ge(size_log, 1)
            five(dve.tensor_scalar(y5[r5, 0, :], y5[r5, 0, :], 100.0, None, ALU.mult))
            for form in range(2):
                quarter, phase = k.box5[r5, 2 * form:2 * form + 1], k.box5[r5, 2 * form + 1:2 * form + 2]
                five(dve.tensor_scalar(t5[r5, form, :], y5[r5, 0, :], float(1 / (2 * np.pi)), quarter, ALU.mult, ALU.add))
                five(dve.tensor_scalar(t5[r5, form, :], t5[r5, form, :], ROUND, None, ALU.add))
                five(dve.tensor_scalar(t5[r5, form, :], t5[r5, form, :], ROUND, None, ALU.subtract))
                five(dve.scalar_tensor_tensor(out=y5[r5, 1, :], in0=t5[r5, form, :], scalar=-TWO_PI_HI,
                                              in1=y5[r5, 0, :], op0=ALU.mult, op1=ALU.add))
                five(dve.scalar_tensor_tensor(out=t5[r5, form, :], in0=t5[r5, form, :], scalar=-TWO_PI_LO,
                                              in1=y5[r5, 1, :], op0=ALU.mult, op1=ALU.add))
                five(dve.tensor_scalar(t5[r5, form, :], t5[r5, form, :], phase, BELOW_PI, ALU.add, ALU.min))
                dve.tensor_scalar(t5[r5, form, :], t5[r5, form, :], -BELOW_PI, None, ALU.max).then_inc(size_angle, 1)
            angle = Link(dve, angle_step)
            for b in range(B):
                y, n = d[:, 2 * b:2 * b + 2, :, :], turns[:, 2 * b:2 * b + 2, :, :]
                y, n = (v.rearrange("p t c m -> p (t c m)") for v in (y, n))
                dve.wait_ge(turns_ready, b + 1)
                angle(dve.scalar_tensor_tensor(out=y, in0=n, scalar=-TWO_PI_HI, in1=y, op0=ALU.mult, op1=ALU.add))
                angle(dve.scalar_tensor_tensor(out=y, in0=n, scalar=-TWO_PI_LO, in1=y, op0=ALU.mult, op1=ALU.add))
                dve.tensor_scalar(y, y, BELOW_PI, -BELOW_PI, ALU.min, ALU.max).then_inc(angle_ready, 1)
            for b in range(B):
                dve.wait_ge(half_sine, b + 1)
                dve.tensor_scalar(feat[:, 2 * b:2 * b + 2, 2:4, :], turns[:, 2 * b:2 * b + 2, :, :], -2.0, 1.0,
                                  ALU.mult, ALU.add).then_inc(features, 1)

        @block.gpsimd
        def _(pool):
            step = Link(pool, k.sem("box_pool_step"))
            for b in range(B):
                pool.wait_ge(logged, b + 1)
                y, n = d[:, 2 * b:2 * b + 2, :, :], turns[:, 2 * b:2 * b + 2, :, :]
                step(pool.tensor_scalar(y, y, 100.0, None, ALU.mult))
                step(pool.tensor_scalar(n, y, float(1 / (2 * np.pi)), ROUND, ALU.mult, ALU.add))
                pool.tensor_scalar(n, n, ROUND, None, ALU.subtract).then_inc(turns_ready, 1)

        @block.scalar
        def _(act):
            for b in range(B):
                act.wait_ge(apart, b + 1)
                for t in range(KB * b, KB * b + KB):
                    for c in range(2):
                        ins_ = act.activation(d[:, t, c, :], d[:, t, c, :], ACT.Abs, scale=size[:, t, c:c + 1])
                ins_.then_inc(absolute, 1)
            act.wait_ge(size_ready, 1)
            act.activation(y5[r5, 0, :], y5[r5, 0, :], ACT.Ln).then_inc(size_log, 1)
            for b in range(B):
                act.wait_ge(clipped, b + 1)
                act.activation(d[:, 2 * b:2 * b + 2, :, :], d[:, 2 * b:2 * b + 2, :, :], ACT.Ln).then_inc(logged, 1)
            for form in range(2):
                act.wait_ge(size_angle, form + 1)
                act.activation(k.size_waves[r5, form, :], t5[r5, form, :], ACT.Sin).then_inc(size_sine, 1)
            for b in range(B):
                angle, n = d[:, 2 * b:2 * b + 2, :, :], turns[:, 2 * b:2 * b + 2, :, :]
                act.wait_ge(angle_ready, b + 1)
                act.activation(n, angle, ACT.Sin, scale=0.5).then_inc(half_sine_step, 1)
                act.activation(feat[:, 2 * b:2 * b + 2, 0:2, :], angle, ACT.Sin).then_inc(sine_done, 1)
                act.wait_ge(half_sine_step, b + 1)
                act.activation(n, n, ACT.Square).then_inc(half_sine, 1)


def box_plan():
    plan = []
    for b in range(B + 1):
        front = ([("K", b, j) for j in range(2)] + [("Q", b, j) for j in range(2)] + [("V", b, j) for j in range(2)]
                 if b < B else [])
        late = [("G", b - 1, 1, j) for j in range(NQ // 2)] if b else []
        while front or late:
            if front:
                plan.append(front.pop(0))
            if late:
                plan.append(late.pop(0))
        sc = [("S", b, i, j) for i in range(KB) for j in range(4)] if b < B else []
        pv = []
        if b:
            for i in range(KB):
                pv += [("P", b - 1, i, j) for j in range(3)] + [("T", b - 1, i), ("O", b - 1, i)]
        while sc or pv:
            if sc:
                plan.append(sc.pop(0))
            if pv:
                plan.append(pv.pop(0))
        if b < B:
            plan.append(("M", b))
            plan += [("X", b, 0, j) for j in range(4)]
            for j in range(4):
                plan += [("X", b, 1, j), ("G", b, 0, 2 * j), ("G", b, 0, 2 * j + 1)]
    return plan


PV_HEADS = [range(0, 6), range(6, 11), range(11, 16)]
SLOT_USERS = {"K": "act", "Q": "dve", "V": "dve", "S": "dve", "M": "dve", "X": "act", "T": "act", "O": "dve"}


def box_phase(nc, k, ins):
    s = norm_sems(k, "box")
    prep = k.sem("box_prep")
    sums_loaded = k.sem("box_weights_loaded")
    pairs_loaded = [k.sem(f"box_pairs_loaded_{i}") for i in range(2)]
    sums_step = k.sem("box_sums_step")
    sums_ready = k.sem("box_sums_ready")
    slot_ready = k.sem("box_slot_ready")
    slot_freed = {"act": k.sem("box_slot_freed_act"), "dve": k.sem("box_slot_freed_dve")}
    g_ready = k.sem("box_g_ready")
    g_used = k.sem("box_g_used")
    pv_ready = k.sem("box_pv_ready")
    pv_used = k.sem("box_pv_used")
    pv_step = k.sem("box_pv_step")
    split_step = k.sem("box_split_step")
    max_split = k.sem("box_max_split")
    x_step = k.sem("box_x_step")
    plan = box_plan()
    slots = [item for item in plan if item[0] in SLOT_USERS]
    slot_at = {item: n for n, item in enumerate(slots)}
    g_at = {item: n for n, item in enumerate(i for i in plan if i[0] == "G")}
    pv_at = {item: n for n, item in enumerate(i for i in plan if i[0] == "P")}

    def freed(item):
        user = SLOT_USERS[item[0]]
        return slot_freed[user], sum(SLOT_USERS[i[0]] == user for i in slots[:slot_at[item] + 1])

    with ExitStack() as ctx:
        def sb(name, shape, dt=F32):
            return ctx.enter_context(nc.sbuf_tensor(name, shape, dt))
        wide = sb("wide", [P, WIDE_COLS])
        q2 = sb("box_q", [P, NC, 2, S])
        k2 = sb("box_k", [P, NC, S])
        v2 = sb("box_v", [P, 2, KB, H, U])
        top = sb("box_top", [P, NT, H])
        rest = sb("box_top_rest", [P, 2, H])
        top3 = sb("box_top3", [P, KB, P], BF16)
        top3T = sb("box_top3T", [P, S], BF16)
        e = sb("box_e", [P, 3, S, H])
        pairs = sb("box_pairs", [P, 2, NQ, P])
        sums = sb("box_sums", [P, S, H])
        sums2 = sb("box_sums2", [P, P, H])
        att = sb("box_att", [P, 2, H, DK])
        rden = sb("box_rden", [P, 2, 8])
        attT = k.z
        block = ctx.enter_context(nc.Block())
        r5 = slice(RPAIR, RPAIR + RSUM)
        rows = RPAIR + RSUM

        def slot(item):
            return 2 * (slot_at[item] % 2)

        @block.sync
        def _(sp):
            sp.dma_start(wide[:, :], ins["wide"]).then_inc(k.wide_loaded, 16)
            sp.dma_start(sums[0:RPAIR, :, :].rearrange("p (n q) h -> p n (q h)", q=QG),
                         ins["wg_rows"].unsqueeze(1).broadcast_to([RPAIR, NQ, H * QG])).then_inc(sums_loaded, 16)
            sp.wait_ge(k.pairs_stored, 16 * NT)
            for u in range(B * KB):
                b, kb = u // KB, u % KB
                if u >= 2:
                    sp.wait_ge(g_ready, (u - 1) * NQ // 2)
                for f in range(NPAIR):
                    sp.dma_start(pairs[QG * f:QG * f + QG, u % 2, :, :],
                                 k.pairs[b, f, :, kb * P:kb * P + P].rearrange("(n q) m -> q n m", q=QG))\
                      .then_inc(pairs_loaded[u % 2], 16)
                sp.dma_start(pairs[r5, u % 2, :, :], k.size_waves[r5, 0, b * S + kb * P:b * S + kb * P + P].unsqueeze(1)
                             .broadcast_to([RSUM, NQ, P])).then_inc(pairs_loaded[u % 2], 16)

        @block.gpsimd
        def _(pool):
            pool.memset(v2[:, :, :, :, DK:U], 1.0).then_inc(prep, 1)
            pool.wait_ge(prep, 1)
            pool.memset(top3[:, :, :], 0.0).then_inc(prep, 1)
            pool.wait_ge(prep, 2)
            pool.memset(q2[DK:P, :, 0, :], 0.0).then_inc(prep, 1)
            pool.wait_ge(prep, 3)
            pool.memset(q2[0:DK, :, 1, :], 0.0).then_inc(prep, 1)
            pool.wait_ge(prep, 4)
            step = Link(pool, sums_step)
            full = [RSUM, P, H]
            for b in range(B):
                if b >= 1:
                    pool.wait_ge(g_ready, b * NQ)
                for i in range(KB):
                    for form, dst in ((0, sums[r5, tile(i), :]), (1, sums2[r5, :, :])):
                        step(pool.tensor_tensor(dst, k.size_waves[r5, form, b * S + i * P:b * S + i * P + P]
                                                .unsqueeze(2).broadcast_to(full),
                                                k.box5[r5, 4 + H * form:4 + H * form + H].unsqueeze(1)
                                                .broadcast_to(full), ALU.mult))
                    pool.tensor_tensor(sums[r5, tile(i), :], sums[r5, tile(i), :], sums2[r5, :, :], ALU.add)\
                        .then_inc(sums_ready, 1)
                    pool.wait_ge(sums_ready, KB * b + i + 1)

        @block.tensor
        def _(pe):
            norm_tensor(pe, k, s)
            wait_zT(pe, s)
            pe.wait_ge(k.wide_loaded, 16)
            pe.wait_ge(sums_loaded, 16)
            wq, wk, wv, wo = (wide[:, WIDE_AT[n]] for n in ("wq2", "wk2", "wv2", "wo2"))

            def wait_freed(item):
                pe.wait_ge(*freed(item))

            for item in plan:
                kind, b = item[:2]
                if kind in SLOT_USERS:
                    bank = slot(item)
                    if slot_at[item] >= 2:
                        wait_freed(slots[slot_at[item] - 2])
                if kind in "KQ":
                    w, src = (wk, k.ctxT) if kind == "K" else (wq, k.zT)
                    for j in range(4):
                        mm = pe.matmul(k.ps[:, bank + j // 2, j % 2 * S:j % 2 * S + S], w[:, tile(4 * item[2] + j)],
                                       src[:, b * S:b * S + S], start=True, stop=True)
                elif kind == "V":
                    for j in range(2):
                        mm = pe.matmul(k.ps[:, bank + j, :], k.ctxT[:, tile(KB * b + item[2])], wv[:, half(j)],
                                       start=True, stop=True)
                elif kind == "S":
                    wait_freed(("K", b, 1))
                    wait_freed(("Q", b, 1))
                    for j in range(4):
                        h = 4 * item[3] + j
                        mm = pe.matmul(k.ps[:, bank + j // 2, j % 2 * S:j % 2 * S + S], q2[:, h // 2, h % 2, tile(item[2])],
                                       k2[:, h // 2, :], start=True, stop=True)
                elif kind == "M":
                    pe.wait_ge(max_split, b + 1)
                    for i in range(KB):
                        mm = pe.transpose(k.ps[:, bank, :].bitcast(BF16)[:, tile(i)], top3[:, i, :], k.identb[:, :])
                elif kind == "X":
                    wait_freed(("M", b))
                    for j in range(4):
                        h = 4 * item[3] + j
                        at = k.ps[:, bank + j // 2, j % 2 * S:j % 2 * S + S]
                        pe.matmul(at, k2[:, h // 2, tile(item[2])], q2[:, h // 2, h % 2, :], start=True, stop=False,
                                  skip_group_check=True)
                        mm = pe.matmul(at, k.minus[:, h, :], top3T[:, :], start=False, stop=True, skip_group_check=True)
                elif kind == "G":
                    n = g_at[item]
                    u = KB * b + item[2]
                    pe.wait_ge(pairs_loaded[u % 2], 16 * (NPAIR + 1) * (u // 2 + 1))
                    pe.wait_ge(sums_ready, KB * (b + 1))
                    if n >= 2:
                        pe.wait_ge(g_used, n - 1)
                    for j in range(2):
                        qg = 2 * item[3] + j
                        mm = pe.matmul(k.ps[:, 4 + n % 2, j * H * QG:(j + 1) * H * QG], pairs[0:rows, u % 2, qg, :],
                                       sums[0:rows, QG * qg:QG * qg + QG, :], start=True, stop=True)
                    mm.then_inc(g_ready, 1)
                elif kind == "P":
                    n = pv_at[item]
                    pe.wait_ge(g_used, (b + 1) * NQ)
                    wait_freed(("V", b, 1))
                    if n >= 2:
                        pe.wait_ge(pv_used, n - 1)
                    for j, h in enumerate(PV_HEADS[item[3]]):
                        for kb in range(KB):
                            mm = pe.matmul(k.ps[:, 6 + n % 2, j * U:j * U + U],
                                           e[:, (KB * b + kb) % 3, tile(item[2]), h],
                                           v2[:, b % 2, kb, h, :], start=(kb == 0), stop=(kb == KB - 1))
                    mm.then_inc(pv_ready, 1)
                elif kind == "T":
                    pe.wait_ge(pv_used, pv_at[("P", b, item[2], 2)] + 1)
                    for c in range(NC):
                        mm = pe.transpose(k.ps[:, bank + c // 4, tile(c % 4)], att[:, item[2], 2 * c:2 * c + 2, :],
                                          k.ident)
                elif kind == "O":
                    wait_freed(("T", b, item[2]))
                    for c in range(NC):
                        mm = pe.matmul(k.ps[:, bank, 0:D], attT[:, c, :], wo[:, tile(c)], start=(c == 0),
                                       stop=(c == NC - 1))
                if kind in SLOT_USERS:
                    mm.then_inc(slot_ready, 1)

        @block.scalar
        def _(act):
            norm_scalar(act, k, s)
            for item in plan:
                kind, b = item[:2]
                if SLOT_USERS.get(kind) != "act":
                    continue
                act.wait_ge(slot_ready, slot_at[item] + 1)
                bank = slot(item)
                if kind == "K":
                    for j in range(4):
                        c = 4 * item[2] + j
                        ins_ = act.activation(k2[:, c, :], k.ps[:, bank + j // 2, j % 2 * S:j % 2 * S + S], ACT.Identity,
                                              bias=k.w["bk2"][:, c:c + 1])
                elif kind == "X":
                    ins_ = act.activation(
                        e[:, (KB * b + item[2]) % 3, :, 4 * item[3]:4 * item[3] + 4].rearrange("p q h -> p h q"),
                        k.ps[:, bank:bank + 2, :].rearrange("p a (h q) -> p (a h) q", h=2), ACT.Exp, scale=DK ** -0.5)
                else:
                    ins_ = act.activation(attT[:, :, :].rearrange("p (a c) t -> p a (c t)", a=2),
                                          k.ps[:, bank:bank + 2, :], ACT.Copy)
                ins_.then_inc(slot_freed["act"], 1)

        @block.vector
        def _(dve):
            norm_vector(dve, k, s)
            dve.wait_ge(prep, 4)
            split = Link(dve, split_step)
            pvl = Link(dve, pv_step)
            dve.wait_ge(s.zT_hi, s.nth + 1)
            dve.tensor_tensor(k.x[:, :, :], k.x[:, :, :], row_over_tiles(k, "bo2", NT), ALU.add).then_inc(x_step, 1)
            dve.wait_ge(x_step, 1)
            for item in plan:
                kind, b = item[:2]
                bank = 0
                if SLOT_USERS.get(kind) == "dve":
                    dve.wait_ge(slot_ready, slot_at[item] + 1)
                    bank = slot(item)
                if kind == "Q":
                    for j in range(4):
                        c = 4 * item[2] + j
                        for side in range(2):
                            r = slice(DK * side, DK * side + DK)
                            ins_ = dve.tensor_scalar(q2[r, c, side, :], k.ps[r, bank + j // 2, j % 2 * S:j % 2 * S + S],
                                                     k.w["bq2"][r, c:c + 1], None, ALU.add)
                elif kind == "V":
                    ins_ = dve.tensor_tensor(v2[:, b % 2, item[2], :, 0:DK],
                                             k.ps[:, bank:bank + 2, :].rearrange("p a (h c) -> p (a h) c", c=DK),
                                             k.rows[:, ROW_AT["bv2"]].rearrange("p (h c) -> p h c", c=DK), ALU.add)
                elif kind == "S":
                    t = KB * b + item[2]
                    ins_ = dve.tensor_reduce(top[:, t, 4 * item[3]:4 * item[3] + 4],
                                             k.ps[:, bank:bank + 2, :].rearrange("p a (h c) -> p (a h) c", c=S), AX_X,
                                             ALU.max)
                elif kind == "M":
                    ins_ = dve.tensor_copy(top3T[:, :], k.ps[:, bank, :].bitcast(BF16)[:, 0:S])
                elif kind == "O":
                    t = KB * b + item[2]
                    ins_ = dve.tensor_tensor(k.x[:, t, :], k.x[:, t, :], k.ps[:, bank, 0:D], ALU.add)
                elif kind == "G":
                    n = g_at[item]
                    part = e[:, (KB * b + item[2]) % 3, 2 * QG * item[3]:2 * QG * (item[3] + 1), :].rearrange("p q h -> p (q h)")
                    dve.wait_ge(g_ready, n + 1)
                    dve.wait_ge(*freed(("X", b, item[2], 3)))
                    dve.scalar_tensor_tensor(out=part, in0=k.ps[:, 4 + n % 2, :], scalar=1e-6, in1=part, op0=ALU.max,
                                             op1=ALU.mult).then_inc(g_used, 1)
                elif kind == "P":
                    n = pv_at[item]
                    heads = PV_HEADS[item[3]]
                    m = len(heads)
                    dve.wait_ge(pv_ready, n + 1)
                    o = k.ps[:, 6 + n % 2, 0:m * U].rearrange("p (h c) -> p h c", c=U)
                    if n >= 2:
                        dve.wait_ge(pv_used, n - 1)
                    pvl(dve.reciprocal(rden[:, n % 2, 0:m], o[:, :, DK]))
                    dve.tensor_tensor(att[:, item[2], heads[0]:heads[0] + m, :], o[:, :, 0:DK],
                                      rden[:, n % 2, 0:m].unsqueeze(2).broadcast_to([P, m, DK]), ALU.mult).then_inc(pv_used, 1)
                if SLOT_USERS.get(kind) == "dve":
                    ins_.then_inc(slot_freed["dve"], 1)
                if kind == "S" and item[2:] == (KB - 1, 3):
                    dve.wait_ge(*freed(item))
                    m2 = top[:, KB * b:KB * b + KB, :]

                    if b >= 1:
                        dve.wait_ge(*freed(("M", b - 1)))

                    def part(j):
                        return top3[:, :, KB * H * j:KB * H * j + H]
                    split(dve.tensor_copy(part(0), m2))
                    split(dve.tensor_tensor(rest[:, :, :], m2, part(0), ALU.subtract))
                    split(dve.tensor_copy(part(1), rest[:, :, :]))
                    dve.tensor_tensor(part(2), rest[:, :, :], part(1), ALU.subtract).then_inc(max_split, 1)
                    dve.wait_ge(max_split, b + 1)


def box_arrays(a):
    boxes = a["fside_BxSx4_0"].reshape(T, 4)
    lo_x, lo_y, hi_x, hi_y = boxes.T
    zero = np.zeros(T, np.float32)
    wg, bg = a["L1_xattn_Wg"], a["L1_xattn_bg"]
    quarters = np.array([[0.25, 0.0, 0.25, 0.0, 0.25], [0.0, -0.25, 0.0, -0.25, 0.25]], np.float32)
    box5 = np.zeros((RSUM, 4 + 2 * H), np.float32)
    for form in range(2):
        box5[:, 2 * form] = quarters[form]
        box5[:, 2 * form + 1] = quarters[form] * np.float32(2 * np.pi)
    box5[0:2, 4:4 + H], box5[2:4, 4:4 + H] = wg[:, 6], wg[:, 7]
    box5[0:2, 4 + H:], box5[2:4, 4 + H:], box5[4, 4 + H:] = wg[:, 2], wg[:, 3], bg
    wg_rows = np.zeros((NPAIR, QG, QG, H), np.float32)
    for f, col in enumerate((0, 1, 4, 5)):
        for q in range(QG):
            wg_rows[f, q, q, :] = wg[:, col]
    return {
        "boxes": boxes, "box_rows": np.ascontiguousarray(boxes.T), "box5": box5,
        "box_ends": np.ascontiguousarray(np.stack([np.stack([hi_x, hi_x, hi_y, hi_y, zero]),
                                                   np.stack([lo_x, lo_x, lo_y, lo_y, zero])], 1)),
        "wg_rows": wg_rows.reshape(RPAIR, H * QG),
    }



def chain_phase(nc, k):
    s = norm_sems(k, "chain")
    turned = [k.sem(f"chain_product_{i}") for i in range(2)]
    copied_lo = k.sem("chain_copied_lo")
    copied_hi = k.sem("chain_copied_hi")
    last_ready = k.sem("chain_last_ready")
    biased = k.sem("chain_biased")
    tanh_done = k.sem("chain_tanh_done")
    W = k.w
    with ExitStack() as ctx:
        a = ctx.enter_context(nc.sbuf_tensor("chain_a", [P, T], F32))
        b = ctx.enter_context(nc.sbuf_tensor("chain_b", [P, T], F32))
        block = ctx.enter_context(nc.Block())
        bufs = (a, b)

        @block.vector
        def _(dve):
            norm_vector(dve, k, s)
            for j in range(2):
                dve.wait_ge(turned[0], j + 1)
                dve.tensor_copy(bufs[j][:, half(0)], k.ps[:, 2 + 2 * j, :]).then_inc(copied_lo, 1)
            for i in range(2):
                dve.wait_ge(last_ready, i + 1)
                dve.tensor_tensor(k.z[:, 4 * i:4 * i + 4, :], k.ps[:, 6 + i, :].rearrange("p (t d) -> p t d", d=D),
                                  row_over_tiles(k, "ffn_b", 4), ALU.add).then_inc(biased, 1)
            for i in range(2):
                dve.wait_ge(tanh_done, i + 1)
                dve.tensor_tensor(k.x[:, 4 * i:4 * i + 4, :], k.x[:, 4 * i:4 * i + 4, :],
                                  k.z[:, 4 * i:4 * i + 4, :], ALU.add).then_inc(k.x_final, 1)

        @block.scalar
        def _(act):
            norm_scalar(act, k, s)
            for j in range(2):
                act.wait_ge(turned[1], j + 1)
                act.activation(bufs[j][:, half(1)], k.ps[:, 3 + 2 * j, :], ACT.Copy).then_inc(copied_hi, 1)
            for i in range(2):
                act.wait_ge(biased, i + 1)
                act.activation(k.z[:, 4 * i:4 * i + 4, :], k.z[:, 4 * i:4 * i + 4, :], ACT.Tanh).then_inc(tanh_done, 1)

        @block.tensor
        def _(pe):
            norm_tensor(pe, k, s)
            wait_zT(pe, s)
            for i in range(2):
                pe.matmul(k.ps[:, 2 + i, :], W["ffn1"], k.zT[:, half(i)], start=True, stop=True).then_inc(turned[i], 1)
            for i in range(2):
                pe.wait_ge((copied_lo, copied_hi)[i], 1)
                pe.matmul(k.ps[:, 4 + i, :], W["ffn2"], a[:, half(i)], start=True, stop=True).then_inc(turned[i], 1)
            for i in range(2):
                pe.wait_ge((copied_lo, copied_hi)[i], 2)
                for t in range(4):
                    mm = pe.matmul(k.ps[:, 6 + i, tile(t)], b[:, tile(4 * i + t)], W["ffn3"], start=True, stop=True)
                mm.then_inc(last_ready, 1)


def store_phase(nc, k, out):
    stored = k.sem("stored")
    with nc.Block() as block:
        @block.sync
        def _(sp):
            sp.dma_start(out.rearrange("(t p) d -> p t d", p=P), k.x[:, :, :]).then_inc(stored, 16)
            sp.wait_ge(stored, 16)


def decoder(nc, ins, out):
    with ExitStack() as ctx:
        def sb(name, shape, dt=F32):
            return ctx.enter_context(nc.sbuf_tensor(name, shape, dt))
        k = Parts()
        k.sem = lambda name: ctx.enter_context(nc.semaphore(name))
        k.ps = ctx.enter_context(nc.psum_tensor("ps", [P, 8, 512], F32))
        k.norms = 0
        k.norm_sems = [k.sem(f"norm_{n}") for n in ("step", "z_ready", "zT_in_psum", "zT_lo", "zT_hi")]
        k.x = sb("x", [P, NT, D])
        k.z = sb("z", [P, NT, D])
        k.zT = sb("zT", [P, T])
        k.ctxT = sb("ctxT", [P, T])
        k.stats = sb("stats", [P, NT, 6])
        k.mv = sb("mv", [P, NT, 2])
        k.var = sb("var", [P, NT])
        k.rstd = sb("rstd", [P, NT])
        k.newton = sb("newton", [P, NT])
        k.const = sb("const", [P, CONST_COLS])
        k.ident = k.const[:, CONST_AT["ident"]]
        k.identb = sb("identb", [P, P], BF16)
        k.minus = sb("minus", [P, KB * H, P], BF16)
        k.weights = sb("weights", [P, W_COLS])
        k.w = {n: k.weights[:, c] for n, c in W_AT.items()}
        k.rows = sb("rows", [P, ROW_COLS])
        k.box5 = sb("box5", [P, 4 + 2 * H])
        k.size_waves = sb("size_waves", [P, 2, T])
        k.pairs = nc.dram_tensor("pair_features", (B, NPAIR, S, S), F32).ap()
        k.pairs_stored = k.sem("box_pairs_stored")
        k.x_loaded = k.sem("x_loaded")
        k.const_loaded = k.sem("const_loaded")
        k.weights_loaded = k.sem("weights_loaded")
        k.ctx_loaded = k.sem("ctx_loaded")
        k.rows_loaded = k.sem("rows_loaded")
        k.wide_loaded = k.sem("wide_loaded")
        k.x_final = k.sem("x_final")
        load_phase(nc, k, ins)
        box_prep_phase(nc, k, ins)
        scan_phase(nc, k)
        cross_phase(nc, k)
        moe_phase(nc, k, ins)
        rotary_phase(nc, k)
        box_phase(nc, k, ins)
        chain_phase(nc, k)
        store_phase(nc, k, out)







def kernel(**inputs):
    import concourse.bacc as _bacc
    from concourse.bass_utils import run_bass_kernel_spmd as _run

    a = {n: np.asarray(v) for n, v in inputs.items()}
    pos = np.arange(S, dtype=np.float32)[:, None] * np.power(np.float32(10000.0), np.float32(2.0) * np.arange(
        HD // 2, dtype=np.float32) / np.float32(HD))[None, :]
    cos = np.tile(np.repeat(np.cos(pos), 2, 1), (1, H)).astype(np.float32)
    sin = np.tile(np.stack([-np.sin(pos), np.sin(pos)], -1).reshape(S, HD), (1, H)).astype(np.float32)
    minus = np.zeros((P, KB * H), np.float32)
    for part in range(3):
        minus[KB * H * part:KB * H * (part + 1)] = -np.eye(KB * H, dtype=np.float32)
    parts = {
        "A": a["L0_attn_A"], "A_T": a["L0_attn_A"].T, "Bm": a["L0_attn_Bm"], "W_ctx_T": a["L0_attn_W_ctx"].T,
        "wq0": a["L0_xattn_Wq"].T, "wk0": a["L0_xattn_Wk"].T, "wv0": a["L0_xattn_Wv"].T,
        "wo0": a["L0_xattn_Wo"].T, "gate": a["L0_ffn_gate_w"], "wq1": a["L1_attn_w_q"].T, "wk1": a["L1_attn_w_k"].T,
        "wv1": a["L1_attn_w_v"].T, "wo1": a["L1_attn_w_o"].T, "ffn1": a["L1_ffn_weight"],
        "ffn2": a["L1_ffn_aux_weight1"], "ffn3": a["L1_ffn_aux_weight2"],
        "bq0": a["L0_xattn_bq"], "bk0": a["L0_xattn_bk"], "minus": minus,
        "bq2": a["L1_xattn_bq"].reshape(NC, P).T, "bk2": a["L1_xattn_bk"].reshape(NC, P).T,
        "wq2": a["L1_xattn_Wq"].T, "wk2": a["L1_xattn_Wk"].T, "wv2": a["L1_xattn_Wv"].T,
        "wo2": a["L1_xattn_Wo"].T.reshape(NC, P, D).transpose(1, 0, 2).reshape(P, NC * D),
        "bv0": a["L0_xattn_bv"], "bo0": a["L0_xattn_bo"], "bo2": a["L1_xattn_bo"], "ffn_b": a["L1_ffn_bias"],
        "bv2": a["L1_xattn_bv"],
        "ident": np.eye(P, dtype=np.float32), "cos": cos.reshape(KB, P, D).transpose(1, 0, 2).reshape(P, KB * D),
        "sin": sin.reshape(KB, P, D).transpose(1, 0, 2).reshape(P, KB * D),
        "rank": np.tile(np.arange(E, 0, -1, dtype=np.float32), (P, 1)),
    }

    def pack(names, axis=1):
        return np.ascontiguousarray(np.concatenate([parts[n] for n, _ in names], axis))

    arrays = {
        "x": a["x"].reshape(T, D), "ctx_T": np.ascontiguousarray(a["ctx_1024"].reshape(T, D).T),
        "const": pack(CONSTS), "weights": pack(WEIGHTS), "wide": pack(WIDE), "rows": pack(ROWS, 0),
        "w1": a["L0_ffn_w1"], "w2": a["L0_ffn_w2"],
    }
    arrays.update(box_arrays(a))
    nc = _bacc.Bacc("TRN2", target_bir_lowering=False, num_devices=1)
    ins = {n: nc.dram_tensor(f"in_{n}", v.shape, mybir.dt.from_np(v.dtype), kind="ExternalInput").ap()
           for n, v in arrays.items()}
    out = nc.dram_tensor("out", (T, D), F32, kind="ExternalOutput").ap()
    decoder(nc, ins, out)
    r = _run(nc, [{f"in_{n}": v for n, v in arrays.items()}], core_ids=[0])
    return np.asarray(r.results[0]["out"]).reshape(B, S, D)
```

```python
from contextlib import ExitStack

import concourse.bass as bass
import numpy as np
from concourse import mybir

F32 = mybir.dt.float32
BF16 = mybir.dt.bfloat16
I32 = mybir.dt.int32
ALU = mybir.AluOpType
ACT = mybir.ActivationFunctionType
AX_X = mybir.AxisListType.X

B, S, D = 4, 256, 128
T = B * S
P = 128
NT = T // P
KB = S // P
H = 16
HD = D // H
G = 4
NG = H // G
HS = P // G
E, F = 8, 512
FC = F // P
DK = 64
NC = H * DK // P
EPS = 1e-5
RSQRT_GUESS = float(0x5F3759DF)

WEIGHTS = [("A", P), ("A_T", P), ("Bm", P), ("W_ctx_T", P), ("wq0", P), ("wk0", P),
           ("wv0", P), ("wo0", P), ("gate", E), ("wq1", P), ("wk1", P), ("wv1", P), ("wo1", P),
           ("ffn1_T", P), ("ffn2", P), ("ffn3", P), ("bq2", NC), ("bk2", NC)]
WIDE = [("wq2", H * DK), ("wk2", H * DK), ("wv2", H * DK), ("wo2", H * DK)]
ROWS = [("bq0", D), ("bk0", D), ("bv0", D), ("bo0", D), ("bo2", D), ("ffn_b", D), ("bv2", H * DK)]
CONSTS = [("ident", P), ("cos", KB * P), ("sin", KB * P), ("rank", E), ("minus", KB * H)]


def columns(parts):
    at, out = 0, {}
    for name, n in parts:
        out[name] = slice(at, at + n)
        at += n
    return out, at


W_AT, W_COLS = columns(WEIGHTS)
WIDE_AT, WIDE_COLS = columns(WIDE)
ROW_AT, ROW_COLS = columns(ROWS)
CONST_AT, CONST_COLS = columns(CONSTS)


class Parts:
    pass


class Link:

    def __init__(self, eng, sem, before=0):
        self.eng, self.sem, self.n = eng, sem, before

    def __call__(self, ins):
        self.n += 1
        ins.then_inc(self.sem, 1)
        self.eng.wait_ge(self.sem, self.n)


def half(t4):
    return slice(t4 * 512, t4 * 512 + 512)


def tile(t):
    return slice(t * P, t * P + P)



STATS_STEPS = 2
NORM_STEPS = 14


SUBLAYERS = ("scan", "cross", "moe", "rotary", "box", "chain")


def norm_sems(k, name):
    s = Parts()
    s.nth = SUBLAYERS.index(name)
    s.norm_step, s.z_vector, s.z_scalar, s.zT_in_psum, s.zT_lo, s.zT_hi = k.norm_sems
    return s


BOTH = 2


def norm_tiles(i):
    return slice(0, NT) if i == BOTH else slice(4 * i, 4 * i + 4)


def steps_before(s, i):
    return 0 if i == BOTH else (2 * s.nth + i - 1) * NORM_STEPS


def norm_stats(dve, k, s, i):
    step = Link(dve, s.norm_step, steps_before(s, i))
    at = norm_tiles(i)
    for t in range(at.start, at.stop):
        ins = dve.bn_stats(k.stats[:, t, :], k.x[:, t, :])
    step(ins)
    for t in range(at.start, at.stop):
        ins = dve.bn_aggr(k.mv[:, t, :], k.stats[:, t, :])
    step(ins)


def norm_root(dve, k, s, i):
    step = Link(dve, s.norm_step, steps_before(s, i) + STATS_STEPS)
    at = norm_tiles(i)
    var, rstd, newton = k.var[:, at], k.rstd[:, at], k.newton[:, at]
    step(dve.tensor_scalar(var, k.mv[:, at, 1], EPS, None, ALU.add))
    step(dve.tensor_scalar(rstd.bitcast(I32), var.bitcast(I32), -0.5, RSQRT_GUESS, ALU.mult, ALU.add))
    for _ in range(3):
        step(dve.tensor_tensor(newton, rstd, rstd, ALU.mult))
        step(dve.scalar_tensor_tensor(out=newton, in0=newton, scalar=-0.5, in1=var, op0=ALU.mult, op1=ALU.mult))
        step(dve.scalar_tensor_tensor(out=rstd, in0=newton, scalar=1.5, in1=rstd, op0=ALU.add, op1=ALU.mult))
    step(dve.scalar_tensor_tensor(out=k.shift[:, at], in0=k.mv[:, at, 0], scalar=-1.0, in1=rstd, op0=ALU.mult,
                                  op1=ALU.mult))


def norm_z_vector(dve, k, s, i):
    for t in (4 * i, 4 * i + 1):
        dve.tensor_scalar(k.z[:, t, :], k.x[:, t, :], k.mv[:, t, 0:1], k.rstd[:, t:t + 1],
                          ALU.subtract, ALU.mult).then_inc(s.z_vector, 1)


def norm_z_scalar(act, k, s, i):
    act.wait_ge(s.norm_step, steps_before(s, i if s.nth else BOTH) + NORM_STEPS)
    for t in (4 * i + 2, 4 * i + 3):
        act.activation(k.z[:, t, :], k.x[:, t, :], ACT.Identity, bias=k.shift[:, t:t + 1],
                       scale=k.rstd[:, t:t + 1]).then_inc(s.z_scalar, 1)


def norm_vector_half(dve, k, s, i):
    norm_stats(dve, k, s, i)
    norm_root(dve, k, s, i)
    norm_z_vector(dve, k, s, i)


def norm_ahead(dve, k, name):
    s = norm_sems(k, name)
    norm_stats(dve, k, s, 0)
    norm_root(dve, k, s, 0)


def norm_vector(dve, k, s):
    norm_z_vector(dve, k, s, 0)
    norm_zT_vector(dve, k, s)
    norm_vector_half(dve, k, s, 1)


def norm_scalar(act, k, s):
    norm_z_scalar(act, k, s, 0)
    norm_z_scalar(act, k, s, 1)
    norm_zT_scalar(act, k, s)


def norm_zT_vector(dve, k, s, bank=0):
    dve.wait_ge(s.zT_in_psum, s.nth * NT + NT // 2)
    dve.tensor_copy(k.zT[:, half(0)], k.ps[:, bank, :]).then_inc(s.zT_lo, 1)


def norm_zT_scalar(act, k, s, bank=1):
    act.wait_ge(s.zT_in_psum, s.nth * NT + NT)
    act.activation(k.zT[:, half(1)], k.ps[:, bank, :], ACT.Copy).then_inc(s.zT_hi, 1)


def norm_tensor(pe, k, s, i, bank=None):
    for j in range(4):
        t = 4 * i + j
        pe.wait_ge((s.z_vector, s.z_scalar)[j // 2], 4 * s.nth + 2 * i + j % 2 + 1)
        pe.transpose(k.ps[:, i if bank is None else bank, tile(j)], k.z[:, t, :], k.ident).then_inc(s.zT_in_psum, 1)


def wait_zT(eng, s, i):
    eng.wait_ge((s.zT_lo, s.zT_hi)[i], s.nth + 1)


def keep_warm(pe, k, products, bank=7):
    for _ in range(products):
        pe.matmul(k.ps[:, bank, :], k.identb[:, :], k.minus[:, 0:4, :], start=True, stop=True)



def load_sync(sp, k, ins):
    sp.dma_start(k.x[:, :, :], ins["x"].rearrange("(t p) d -> p t d", p=P)).then_inc(k.x_loaded, 16)
    sp.dma_start(k.const[:, :], ins["const"]).then_inc(k.const_loaded, 16)


def load_rest_sync(sp, k, ins):
    sp.dma_start(k.weights[:, :], ins["weights"]).then_inc(k.weights_loaded, 16)
    sp.dma_start(k.ctxT[:, :], ins["ctx_T"]).then_inc(k.ctx_loaded, 16)
    sp.dma_start(k.box5[R5, :, :], ins["box5"]).then_inc(k.rows_loaded, 16)
    sp.dma_start(k.rows[:, :], ins["rows"].partition_broadcast(P)).then_inc(k.rows_loaded, 16)


def bf16_constants_scalar(act, k):
    act.wait_ge(k.const_loaded, 16)
    act.activation(k.identb[:, :], k.ident, ACT.Copy)
    act.activation(k.minus[:, :, :], k.const[:, CONST_AT["minus"]].unsqueeze(2).broadcast_to([P, KB * H, P]),
                   ACT.Copy)



NORM_BANK = 6
G_BANK = 4
QG = 16
NQ = S // QG
NPAIR = 4
RPAIR = NPAIR * QG
RSUM = 5
ROUND = 1.5 * 2.0 ** 23
TWO_PI_HI = 6.28125
TWO_PI_LO = float(2.0 * np.pi - 6.28125)
BELOW_PI = 3.1415925
SIZE_CUT = 8
SIZE_ROWS = RSUM * SIZE_CUT
FORMS = 2
U = DK + 1


def box_prep_buffers(nc, k, ctx):
    def sb(name, shape):
        return ctx.enter_context(nc.sbuf_tensor(name, shape, F32))
    p = Parts()
    p.feat = sb("box_feat", [P, NT, NPAIR, S]) 
    p.rows = sb("box_rows", [P, 4, T])
    p.own = sb("box_own", [P, NT, 4])
    p.ckey = sb("box_centre_key", [P, 2, T])
    p.cown = sb("box_centre_own", [P, NT, 2])
    p.size = sb("box_size_own", [P, NT, 2])
    p.d = sb("box_distance", [P, NT, 2, S])
    p.turns = sb("box_turns_of", [P, NT, 2, S])
    p.ends = sb("box_ends", [P, 2, T // SIZE_CUT])
    p.angle5 = sb("box_size_angles", [P, T // SIZE_CUT])
    p.turns5 = sb("box_size_turns", [P, T // SIZE_CUT])
    p.phase5 = sb("box_size_phase", [P, 2])
    p.inputs = k.sem("box_inputs")
    p.own_input = k.sem("box_own_input")
    p.own_step = k.sem("box_own_step")
    p.own_size = k.sem("box_own_size")
    p.size_inputs = k.sem("box_size_inputs")
    p.centre_step = k.sem("box_centre_step")
    p.apart = k.sem("box_apart")
    p.absolute = k.sem("box_absolute")
    p.clipped = k.sem("box_clipped")
    p.logged = k.sem("box_logged")
    p.angle_step = k.sem("box_angle_step")
    p.angle_ready = k.sem("box_angle_ready")
    p.sine_done = k.sem("box_sine_done")
    p.half_sine_step = k.sem("box_half_sine_step")
    p.half_sine = k.sem("box_half_sine")
    p.features = k.sem("box_features")
    p.size_step = k.sem("box_size_step")
    p.size_log = k.sem("box_size_log")
    p.size_sine = k.sem("box_size_sine")
    return p


def box_tiles(a, b):
    return a[:, KB * b:KB * b + KB, :, :].rearrange("p t c m -> p (t c m)")


def box_sizes_own_vector(dve, p):
    step = Link(dve, p.own_step)
    dve.wait_ge(p.own_input, 16)
    step(dve.tensor_tensor(p.size[:, :, :], p.own[:, :, 2:4], p.own[:, :, 0:2], ALU.subtract))
    step(dve.tensor_scalar(p.size[:, :, :], p.size[:, :, :], 1.0, None, ALU.add))
    dve.reciprocal(p.size[:, :, :], p.size[:, :, :]).then_inc(p.own_size, 1)


def box_centres_vector(dve, p):
    step = Link(dve, p.centre_step)
    step(dve.tensor_tensor(p.cown[:, :, :], p.own[:, :, 0:2], p.own[:, :, 2:4], ALU.add))
    step(dve.tensor_scalar(p.cown[:, :, :], p.cown[:, :, :], 0.5, None, ALU.mult))
    dve.wait_ge(p.inputs, 16)
    step(dve.tensor_tensor(p.ckey[:, :, :], p.rows[:, 0:2, :], p.rows[:, 2:4, :], ALU.add))
    step(dve.tensor_scalar(p.ckey[:, :, :], p.ckey[:, :, :], 0.5, None, ALU.mult))


def box_apart_vector(dve, p, b):
    for t in range(KB * b, KB * b + KB):
        for c in range(2):
            ins = dve.tensor_scalar(p.d[:, t, c, :], p.ckey[:, c, b * S:b * S + S], p.cown[:, t, c:c + 1], None,
                                    ALU.subtract)
    ins.then_inc(p.apart, 1)


def box_clip_vector(dve, p, b):
    dve.wait_ge(p.absolute, b + 1)
    dve.tensor_scalar(box_tiles(p.d, b), box_tiles(p.d, b), 1e-3, None, ALU.max).then_inc(p.clipped, 1)


def box_angle_vector(dve, p, b):
    angle = Link(dve, p.angle_step, 5 * b)
    y, n = box_tiles(p.d, b), box_tiles(p.turns, b)
    dve.wait_ge(p.logged, b + 1)
    angle(dve.tensor_scalar(y, y, 100.0, None, ALU.mult))
    angle(dve.tensor_scalar(n, y, float(1 / (2 * np.pi)), ROUND, ALU.mult, ALU.add))
    angle(dve.tensor_scalar(n, n, ROUND, None, ALU.subtract))
    angle(dve.scalar_tensor_tensor(out=y, in0=n, scalar=-TWO_PI_HI, in1=y, op0=ALU.mult, op1=ALU.add))
    angle(dve.scalar_tensor_tensor(out=y, in0=n, scalar=-TWO_PI_LO, in1=y, op0=ALU.mult, op1=ALU.add))
    dve.tensor_scalar(y, y, BELOW_PI, -BELOW_PI, ALU.min, ALU.max).then_inc(p.angle_ready, 1)


def box_cosine_vector(dve, p, b):
    dve.wait_ge(p.half_sine, b + 1)
    dve.tensor_scalar(p.feat[:, KB * b:KB * b + KB, 2:4, :], p.turns[:, KB * b:KB * b + KB, :, :], -2.0, 1.0,
                      ALU.mult, ALU.add).then_inc(p.features, 1)


SIZE_STEPS = 2
R5 = slice(RPAIR, RPAIR + RSUM)
ALL5 = slice(0, FORMS * SIZE_ROWS)


def box_sizes_vector(dve, p):
    dve.wait_ge(p.size_inputs, 32)
    five = Link(dve, p.size_step)
    y = p.angle5[ALL5, :]
    five(dve.tensor_tensor(y, p.ends[ALL5, 0, :], p.ends[ALL5, 1, :], ALU.subtract))
    five(dve.tensor_scalar(y, y, 1.0, None, ALU.add))


def box_size_angles_vector(dve, p):
    dve.wait_ge(p.size_log, 1)
    five = Link(dve, p.size_step, SIZE_STEPS)
    y, n = p.angle5[ALL5, :], p.turns5[ALL5, :]
    quarter, phase = p.phase5[ALL5, 0:1], p.phase5[ALL5, 1:2]
    five(dve.tensor_scalar(y, y, 100.0, None, ALU.mult))
    five(dve.tensor_scalar(n, y, float(1 / (2 * np.pi)), quarter, ALU.mult, ALU.add))
    five(dve.tensor_scalar(n, n, ROUND, None, ALU.add))
    five(dve.tensor_scalar(n, n, ROUND, None, ALU.subtract))
    five(dve.scalar_tensor_tensor(out=y, in0=n, scalar=-TWO_PI_HI, in1=y, op0=ALU.mult, op1=ALU.add))
    five(dve.scalar_tensor_tensor(out=y, in0=n, scalar=-TWO_PI_LO, in1=y, op0=ALU.mult, op1=ALU.add))
    five(dve.tensor_scalar(y, y, phase, BELOW_PI, ALU.add, ALU.min))
    five(dve.tensor_scalar(y, y, -BELOW_PI, None, ALU.max))


SIZE_ANGLE_STEPS = 8


def box_absolute_scalar(act, p, b):
    act.wait_ge(p.own_size, 1)
    act.wait_ge(p.apart, b + 1)
    for t in range(KB * b, KB * b + KB):
        for c in range(2):
            ins = act.activation(p.d[:, t, c, :], p.d[:, t, c, :], ACT.Abs, scale=p.size[:, t, c:c + 1])
    ins.then_inc(p.absolute, 1)


def box_size_log_scalar(act, p):
    act.wait_ge(p.size_step, SIZE_STEPS)
    act.activation(p.angle5[ALL5, :], p.angle5[ALL5, :], ACT.Ln).then_inc(p.size_log, 1)


def box_log_scalar(act, p, b):
    act.wait_ge(p.clipped, b + 1)
    act.activation(box_tiles(p.d, b), box_tiles(p.d, b), ACT.Ln).then_inc(p.logged, 1)


def box_size_sine_scalar(act, p):
    act.wait_ge(p.size_step, SIZE_STEPS + SIZE_ANGLE_STEPS)
    act.activation(p.turns5[ALL5, :], p.angle5[ALL5, :], ACT.Sin).then_inc(p.size_sine, 1)


def box_sine_scalar(act, p, b):
    act.wait_ge(p.angle_ready, b + 1)
    act.activation(box_tiles(p.turns, b), box_tiles(p.d, b), ACT.Sin, scale=0.5).then_inc(p.half_sine_step, 1)
    act.activation(p.feat[:, KB * b:KB * b + KB, 0:2, :], p.d[:, KB * b:KB * b + KB, :, :], ACT.Sin)\
       .then_inc(p.sine_done, 1)


def box_square_scalar(act, p, b):
    act.wait_ge(p.half_sine_step, b + 1)
    act.activation(box_tiles(p.turns, b), box_tiles(p.turns, b), ACT.Square).then_inc(p.half_sine, 1)


def box_load_sync(sp, k, p, ins):
    sp.dma_start(p.rows[:, :, :], ins["box_rows"].partition_broadcast(P)).then_inc(p.inputs, 16)
    sp.dma_start(p.own[:, :, :], ins["boxes"].rearrange("(t p) c -> p t c", p=P)).then_inc(p.own_input, 16)
    sp.dma_start(p.ends[ALL5, :, :], ins["box_ends"]).then_inc(p.size_inputs, 16)
    sp.dma_start(p.phase5[ALL5, :], ins["box_phase"]).then_inc(p.size_inputs, 16)


def box_store_sync(sp, k, p):
    for b in range(B):
        if b == 1:
            sp.wait_ge(p.size_sine, 1)
            for form in range(FORMS):
                at = SIZE_ROWS * form
                for r in range(RSUM):
                    sp.dma_start(k.size_waves[RPAIR + r:RPAIR + r + 1, form, :],
                                 p.turns5[at + SIZE_CUT * r:at + SIZE_CUT * (r + 1), :]).then_inc(k.waves_stored, 16)
        sp.wait_ge(p.sine_done, b + 1)
        sp.wait_ge(p.features, b + 1)
        sp.dma_start(k.pairs[b].rearrange("(t q) f m -> q t (f m)", q=P),
                     p.feat[:, KB * b:KB * b + KB, :, :].rearrange("q t f m -> q t (f m)"))\
          .then_inc(k.pairs_stored, 16)
    sp.wait_ge(k.waves_stored, 16 * FORMS * RSUM)
    sp.wait_ge(k.pairs_stored, 16 * B)



LEVELS = S.bit_length() - 1


def scan_phase(nc, k, ins):
    s = norm_sems(k, "scan")
    power_step = k.sem("scan_power_in_psum")
    power_dve = k.sem("scan_power_copied")
    power_act = k.sem("scan_power_T_copied")
    level_done = [k.sem(f"scan_level_done_{i}") for i in range(2)]
    copied = [k.sem(f"scan_copied_{i}") for i in range(2)]
    out_ready = k.sem("scan_out_ready")
    W = k.w
    with ExitStack() as ctx:
        powers = ctx.enter_context(nc.sbuf_tensor("powers", [P, LEVELS, 2, P], F32))
        hs = ctx.enter_context(nc.sbuf_tensor("scan_h", [P, T], F32))
        block = ctx.enter_context(nc.Block())

        def power(level, transposed):
            if level == 0:
                return W["A_T" if transposed else "A"]
            return powers[:, level, transposed, :]

        @block.sync
        def _(sp):
            load_sync(sp, k, ins)
            load_rest_sync(sp, k, ins)

        @block.vector
        def _(dve):
            dve.wait_ge(k.x_loaded, 16)
            norm_stats(dve, k, s, BOTH)
            norm_root(dve, k, s, BOTH)
            norm_z_vector(dve, k, s, 0)
            norm_z_vector(dve, k, s, 1)
            norm_zT_vector(dve, k, s)
            for level in range(1, LEVELS):
                dve.wait_ge(power_step, level)
                dve.tensor_copy(powers[:, level, 0, :], k.ps[:, 6, 0:P]).then_inc(power_dve, 1)
            for level in range(LEVELS + 1):
                dve.wait_ge(level_done[0], level + 1)
                dve.tensor_copy(hs[:, half(0)], k.ps[:, 2, :]).then_inc(copied[0], 1)
            dve.wait_ge(out_ready, 1)
            dve.tensor_tensor(k.x[:, 0:4, :], k.x[:, 0:4, :], k.ps[:, 4, :].rearrange("p (t d) -> p t d", d=D), ALU.add)
            dve.wait_ge(out_ready, 2)
            dve.tensor_tensor(k.x[:, 4:8, :], k.x[:, 4:8, :], k.ps[:, 5, :].rearrange("p (t d) -> p t d", d=D), ALU.add)

        @block.scalar
        def _(act):
            bf16_constants_scalar(act, k)
            norm_scalar(act, k, s)
            for level in range(1, LEVELS):
                act.wait_ge(power_step, level)
                act.activation(powers[:, level, 1, :], k.ps[:, 7, 0:P], ACT.Copy).then_inc(power_act, 1)
            for level in range(LEVELS + 1):
                act.wait_ge(level_done[1], level + 1)
                act.activation(hs[:, half(1)], k.ps[:, 3, :], ACT.Copy).then_inc(copied[1], 1)

        @block.tensor
        def _(pe):
            pe.wait_ge(k.const_loaded, 16)
            norm_tensor(pe, k, s, 0)
            norm_tensor(pe, k, s, 1)
            pe.wait_ge(k.weights_loaded, 16)

            def square(level):
                if level > 1:
                    pe.wait_ge(power_dve, level - 1)
                    pe.wait_ge(power_act, level - 1)
                pe.matmul(k.ps[:, 6, 0:P], power(level - 1, 1), power(level - 1, 0), start=True, stop=True)
                pe.matmul(k.ps[:, 7, 0:P], power(level - 1, 0), power(level - 1, 1), start=True,
                          stop=True).then_inc(power_step, 1)

            for level in range(1, LEVELS):
                square(level)
            for i in range(2):
                wait_zT(pe, s, i)
                pe.matmul(k.ps[:, 2 + i, :], W["Bm"], k.zT[:, half(i)], start=True, stop=True,
                          skip_group_check=True).then_inc(level_done[i], 1)
            pe.wait_ge(power_dve, LEVELS - 1)
            for level in range(LEVELS):
                shift = 1 << level
                for i in range(2):
                    pe.wait_ge(copied[i], level + 1)
                    for b in range(2):
                        at = b * S
                        mm = pe.matmul(k.ps[:, 2 + i, at + shift:at + S], power(level, 0),
                                       hs[:, i * 512 + at:i * 512 + at + S - shift], start=False, stop=True,
                                       skip_group_check=True)
                    mm.then_inc(level_done[i], 1)
            for i in range(2):
                pe.wait_ge(copied[i], LEVELS + 1)
                for t in range(4):
                    mm = pe.matmul(k.ps[:, 4 + i, tile(t)], hs[:, tile(4 * i + t)], W["W_ctx_T"],
                                   start=True, stop=True)
                mm.then_inc(out_ready, 1)



SEG = 64
NSEG = 6
PAIRS = H // 2
FIRST_GROUPS = NG // 2
SECOND_BANK = 3


class Ring:

    def __init__(self, k, name, plan, users, places, last=None):
        self.users, self.places, self.last = users, places, last
        self.steps = [item for item in plan if item[0] in users]
        self.at = {item: n for n, item in enumerate(self.steps)}
        self.ready = k.sem(f"{name}_ready")
        self.freed = {e: k.sem(f"{name}_freed_{e}") for e in ("act", "dve") if any(e in u for u in users.values())}

    def own_place(self, item):
        return self.last is not None and item == self.steps[-1]

    def place(self, item):
        return self.last if self.own_place(item) else self.places[self.at[item] % len(self.places)]

    def wait_free(self, pe, item):
        n = self.at[item] - len(self.places)
        if n >= 0 and not self.own_place(item):
            self.wait_read(pe, self.steps[n])

    def wait_read(self, eng, item, of=None):
        for user in self.users[item[0]]:
            if of in (None, user):
                count = sum(user in self.users[i[0]] for i in self.steps[:self.at[item] + 1])
                eng.wait_ge(self.freed[user], count)

    def wait_ready(self, eng, item):
        eng.wait_ge(self.ready, self.at[item] + 1)


def narrow_plan():
    def scores(b):
        return [("S", b, i, j) for j in range(PAIRS) for i in range(KB)] if b < B else []

    first = scores(0)
    plan = [("A", 0, 0), ("A", 0, 1)] + first[:PAIRS] + [("M", 0, 0)]
    late = []
    for b in range(B):
        sc = scores(b + 1)
        for n in range(NG * KB):
            j, kb = n // KB, n % KB
            if b == 0 and n < FIRST_GROUPS * KB:
                take = [[first[PAIRS + 2 * n]], [first[PAIRS + 2 * n + 1]]]
            else:
                per = 4 if b == 0 else 3
                take, sc = [sc[:per // 2], sc[per // 2:per]], sc[per:]
            plan += [("X", b, j, kb, 0)] + take[0] + [("X", b, j, kb, 1)] + take[1]
            plan += late
            late = [("P", b, j, kb)]
            if b == 0 and n in (1, 2):
                plan.append(("A", 1, n - 1))
            if b == 0 and n == FIRST_GROUPS * KB - 1:
                plan.append(("M", 0, 1))
            if b >= 1 and n in (1, 3):
                plan.append(("T", b - 1, n // 2))
            if b == B // 2 and n in (4, 6):
                plan.append(("Y" if n == 4 else "O", b - 1, KB - 1))
            if b + 2 < B and n in (5, 6):
                plan.append(("A", b + 2, n - 5))
            if b + 1 < B and n == NG * KB - 1:
                plan.append(("M", b + 1, 1))
    plan += late
    return plan + [("T", B - 1, 0), ("T", B - 1, 1)]


def narrow_sems(k, name):
    s = norm_sems(k, name)
    s.bias_added = k.sem(f"{name}_bias_added")
    s.prep = k.sem(f"{name}_prep")
    s.proj_ready = k.sem(f"{name}_proj_ready")
    s.v_copied = k.sem(f"{name}_v_copied")
    s.full_ready = {"q": k.sem(f"{name}_q_full"), "k": k.sem(f"{name}_k_full")}
    s.high_ready = {"q": k.sem(f"{name}_q_high"), "k": k.sem(f"{name}_k_high")}
    s.rest_ready = {"q": k.sem(f"{name}_q_rest"), "k": k.sem(f"{name}_k_rest")}
    s.middle_ready = {"q": k.sem(f"{name}_q_middle"), "k": k.sem(f"{name}_k_middle")}
    s.split_ready = {"q": k.sem(f"{name}_q_split"), "k": k.sem(f"{name}_k_split")}
    s.top_step = k.sem(f"{name}_top_step")
    s.top_ready = k.sem(f"{name}_top_ready")
    s.gap_ready = k.sem(f"{name}_gap_ready")
    s.gap_exp = k.sem(f"{name}_gap_exp")
    s.mix_step = k.sem(f"{name}_mix_step")
    s.attT_ready = k.sem(f"{name}_attT_ready")
    s.attT_hi = k.sem(f"{name}_attT_hi")
    s.out_ready = k.sem(f"{name}_out_ready")
    plan = narrow_plan()
    s.plan = plan
    s.turned = Ring(k, f"{name}_turned", plan, {"A": ("act", "dve"), "M": ("dve",), "T": ("dve",),
                                                   "Y": ("act",), "O": ("dve",)}, [6], last=2)
    s.scores = Ring(k, f"{name}_scores", plan, {"S": ("dve",)}, [0, 1])
    s.scoresT = Ring(k, f"{name}_scoresT", plan, {"X": ("act",)}, [2, 3])
    s.rings = {kind: ring for ring in (s.turned, s.scores, s.scoresT) for kind in ring.users}
    s.pv_ready = k.sem(f"{name}_pv_ready")
    s.pv_copied = k.sem(f"{name}_pv_copied")
    return s


def narrow_buffers(nc, k, ctx, sublayer):
    def sb(name, shape, dt=F32):
        return ctx.enter_context(nc.sbuf_tensor(f"{sublayer}_{name}", shape, dt))
    n = Parts()
    n.e = sb("e", [P, 4, G, S])
    n.oT = sb("oT", [P, 2, NG, KB, S])
    n.full = {"q": sb("q_full", [P, NT, D]), "k": sb("k_full", [P, NT, D])}
    n.parts = {"q": sb("q_parts", [P, NT, H, SEG], BF16), "k": sb("k_parts", [P, NT, H, SEG], BF16)}
    n.q = sb("q", [P, H, T], BF16)
    n.k = sb("k", [P, PAIRS, T], BF16)
    n.v = sb("v", [P, NT, H, HS])
    n.top = sb("top", [P, NT, KB, H])
    n.rest = sb("top_rest", [P, KB, KB * H])
    n.top3 = sb("top3", [P, NT, P], BF16)
    n.topT = sb("topT", [P, T], BF16)
    n.topT_first = sb("topT_first", [P, S], BF16)
    n.att = k.z
    n.tmp = sb("products", [P, 2, NG, G, HD])
    n.mw = sb("block_weights", [P, NT, KB, H])
    n.mf = sb("factors", [P, 2, H])
    n.mt = sb("mix_tmp", [P, 2, H])
    n.ml = sb("mix_sum", [P, H])
    return n


HIGH_AT = {"q": [(0, 3, 1)], "k": [(0, 2, 3), (5, 1, 1)]}
MIDDLE_AT = {"q": [(3, 2, 1)], "k": [(1, 2, 3)]}
LOW_AT = {"q": 5, "k": 2}


def narrow_prepare(pool, n, s):
    step = Link(pool, s.prep)
    step(pool.memset(n.parts["q"][:, :, :, NSEG * HD:SEG], 0.0))
    step(pool.memset(n.parts["k"][:, :, :, NSEG * HD:SEG], 0.0))
    step(pool.memset(n.q[SEG:P, 0:H:2, :], 0.0))
    step(pool.memset(n.q[0:SEG, 1:H:2, :], 0.0))
    step(pool.memset(n.top3[:, :, :], 0.0))
    step(pool.memset(n.v[:, :, :, HD + 1:HS], 0.0))
    step(pool.memset(n.v[:, :, :, HD:HD + 1], 1.0))


PREPARED = {"parts": 2, "q": 4, "top3": 5, "v": 7}


def segments(n, which, i, at):
    first, count, by = at
    v = n.parts[which][:, 4 * i:4 * i + 4, :, 0:NSEG * HD].rearrange("p t h (g c) -> p (t h) g c", c=HD)
    return v[:, :, first:first + (count - 1) * by + 1:by, :]


def heads_of(a, i):
    return a[:, 4 * i:4 * i + 4, :].rearrange("p t (h c) -> p (t h) c", c=HD)


def split_scalar_high(act, n, s, which, i):
    act.wait_ge(s.full_ready[which], i + 1)
    for at in HIGH_AT[which]:
        src = heads_of(n.full[which], i).unsqueeze(2).broadcast_to([P, 4 * H, at[1], HD])
        ins = act.activation(segments(n, which, i, at), src, ACT.Copy)
    ins.then_inc(s.high_ready[which], 1)


def split_scalar_middle(act, n, s, which, i):
    act.wait_ge(s.rest_ready[which], i + 1)
    for at in MIDDLE_AT[which]:
        src = heads_of(n.full[which], i).unsqueeze(2).broadcast_to([P, 4 * H, at[1], HD])
        ins = act.activation(segments(n, which, i, at), src, ACT.Copy)
    ins.then_inc(s.middle_ready[which], 1)


def split_vector_rest(dve, n, s, which, i):
    full = heads_of(n.full[which], i)
    dve.wait_ge(s.high_ready[which], i + 1)
    dve.tensor_tensor(full, full, segments(n, which, i, (HIGH_AT[which][0][0], 1, 1))[:, :, 0, :], ALU.subtract)\
       .then_inc(s.rest_ready[which], 1)


def split_vector_low(dve, n, s, which, i):
    dve.wait_ge(s.middle_ready[which], i + 1)
    dve.tensor_tensor(segments(n, which, i, (LOW_AT[which], 1, 1))[:, :, 0, :], heads_of(n.full[which], i),
                      segments(n, which, i, (MIDDLE_AT[which][0][0], 1, 1))[:, :, 0, :], ALU.subtract)\
       .then_inc(s.split_ready[which], 1)


SECOND_HALF_AFTER = [("S", 0, 1, 0), ("S", 0, 1, 2), ("S", 0, 1, 3), ("M", 0, 0)]


def narrow_tensor(pe, k, n, s, kinds, second_half, wo):
    for item in s.plan:
        kind, b = item[:2]
        ring = s.rings.get(kind)
        if ring:
            bank = ring.place(item)
            ring.wait_free(pe, item)
        if item == ("A", 0, 0):
            pe.wait_ge(s.prep, PREPARED["parts"])
        elif item == ("S", 0, 0, 0):
            pe.wait_ge(s.prep, PREPARED["q"])
        if kind == "A":
            t = KB * b + item[2]
            for which, to in (("q", bank), ("k", bank + 1)):
                pe.wait_ge(s.split_ready[which], t // 4 + 1)
                for j in range(PAIRS):
                    mm = pe.transpose(k.ps[:, to, :].bitcast(BF16)[:, tile(j)],
                                      n.parts[which][:, t, 2 * j:2 * j + 2, :], k.identb[:, :])
        elif kind == "S":
            t = KB * b + item[2]
            s.turned.wait_read(pe, ("A", b, 1))
            for h in (2 * item[3], 2 * item[3] + 1):
                mm = pe.matmul(k.ps[:, bank, h % 2 * S:h % 2 * S + S], n.q[:, h, tile(t)],
                               n.k[:, h // 2, b * S:b * S + S], start=True, stop=True)
        elif kind == "M":
            pe.wait_ge(s.top_ready, b + item[2] + 1)
            for i in range(KB):
                mm = pe.transpose(k.ps[:, bank, :].bitcast(BF16)[:, tile(i)], n.top3[:, KB * b + i, :], k.identb[:, :])
        elif kind == "X":
            j, kb = item[2:4]
            early = b == 0 and j < FIRST_GROUPS
            s.turned.wait_read(pe, ("M", b, 0 if early else 1))
            maxima = n.topT_first[:, :] if early else n.topT[:, b * S:b * S + S]
            if item[1:] == (0, 0, 0, 1):
                pe.wait_ge(s.full_ready["q"], 2)
            for i in range(2):
                h = G * j + 2 * item[4] + i
                at = k.ps[:, bank, i * S:i * S + S]
                pe.matmul(at, n.k[:, h // 2, tile(KB * b + kb)], n.q[:, h, b * S:b * S + S], start=True, stop=False,
                          skip_group_check=True)
                mm = pe.matmul(at, k.minus[:, kb * (kinds - 1) * H + h, :], maxima, start=False,
                               stop=True, skip_group_check=True)
        elif kind == "P":
            j, kb = item[2:4]
            u = NG * b + j
            s.scoresT.wait_read(pe, ("X", b, j, kb, 1))
            if kb == 0 and u >= 2:
                pe.wait_ge(s.pv_copied, u - 1)
            if item[1:] == (0, 0, 0):
                pe.wait_ge(s.v_copied, 2)
                pe.wait_ge(s.prep, PREPARED["v"])
                if kinds == 1:
                    pe.wait_ge(s.full_ready["k"], 2)
            at = kb * S if kinds == 2 else 0
            for g in range(G):
                mm = pe.matmul(k.ps[HS * g:HS * g + HS, 4 + u % 2, at:at + S], n.v[:, KB * b + kb, G * j + g, :],
                               n.e[:, (KB * u + kb) % 4, g, :], start=(kb == 0 or kinds == 2),
                               stop=(kb == 1 or kinds == 2), skip_group_check=True)
            mm.then_inc(s.pv_ready, 1)
        elif kind == "T":
            pe.wait_ge(s.pv_copied, NG * (b + 1))
            for j in range(NG):
                for kd in range(kinds):
                    to = (2 * j + kd) * P if kinds == 2 else j * P
                    mm = pe.transpose(k.ps[:, bank + to // 512, to % 512:to % 512 + P],
                                      n.oT[:, b % 2, j, kd, tile(item[2])], k.ident)
        elif kind == "Y":
            s.turned.wait_read(pe, ("T", b, KB - 1))
            for t in range(NT // 2):
                mm = pe.transpose(k.ps[:, bank, tile(t)], n.att[:, t, :], k.ident)
        elif kind == "O":
            s.turned.wait_read(pe, ("Y",) + item[1:])
            for t in range(NT // 2):
                mm = pe.matmul(k.ps[:, bank, tile(t)], k.zT[:, tile(t)], wo, start=True, stop=True)
        if ring:
            mm.then_inc(ring.ready, 1)
        if item in SECOND_HALF_AFTER:
            second_half(SECOND_HALF_AFTER.index(item))


def narrow_scalar(act, k, n, s, kinds, scale, values):
    for item in s.plan:
        kind, b = item[:2]
        if kind == "A":
            t = KB * b + item[2]
            s.turned.wait_ready(act, item)
            src = k.ps[:, s.turned.place(item), :].bitcast(BF16).rearrange("p (j c) -> p j c", c=P)
            act.activation(n.q[0:SEG, 0:H:2, tile(t)], src[0:SEG], ACT.Copy).then_inc(s.turned.freed["act"], 1)
            if t == 1:
                norm_z_scalar(act, k, s, 1)
                norm_zT_scalar(act, k, s, SECOND_BANK)
        elif kind == "Y":
            s.turned.wait_ready(act, item)
            act.activation(k.zT[:, half(0)], k.ps[:, s.turned.place(item), :], ACT.Copy)\
               .then_inc(s.turned.freed["act"], 1)
        elif kind == "P" and item[3] == KB - 1:
            u = NG * b + item[2]
            act.wait_ge(s.pv_ready, KB * (u + 1))
            if u >= 2 * NG:
                s.turned.wait_read(act, ("T", b - 2, 1))
            act.activation(n.oT[:, b % 2, item[2], 0:kinds, :],
                           k.ps[:, 4 + u % 2, 0:kinds * S].rearrange("p (a c) -> p a c", c=S), ACT.Copy)\
               .then_inc(s.pv_copied, 1)
        elif kind == "X":
            u = NG * b + item[2]
            r = KB * u + item[3]
            s.scoresT.wait_ready(act, item)
            if r >= 4:
                act.wait_ge(s.pv_ready, r - 3)
            if item == ("X", 0, 0, 0, 1):
                values(1)
                split_scalar_high(act, n, s, "q", 1)
            elif item == ("X", 0, 0, 1, 1):
                split_scalar_high(act, n, s, "k", 1)
            elif item[:4] == ("X", 0, 1, 0):
                split_scalar_middle(act, n, s, "qk"[item[4]], 1)
            act.activation(n.e[:, r % 4, 2 * item[4]:2 * item[4] + 2, :].rearrange("p g c -> p (g c)"),
                           k.ps[:, s.scoresT.place(item), :], ACT.Exp, scale=scale).then_inc(s.scoresT.freed["act"], 1)
            if item[2:] == (FIRST_GROUPS, 0, 0) and n.gaps:
                act.wait_ge(s.gap_ready, b + 1)
                gap = n.mw[:, KB * b:KB * b + KB, :, :]
                act.activation(gap, gap, ACT.Exp, scale=scale).then_inc(s.gap_exp, 1)


def narrow_vector(dve, k, n, s, kinds, second_half, values, next_sublayer):
    top = Link(dve, s.top_step)
    step = Link(dve, s.mix_step)

    def split_top(b, heads, last):
        m = n.top[:, KB * b:KB * b + KB, 0:kinds, heads]
        rest = n.rest[:, :, 0:kinds * H].rearrange("p t (a h) -> p t a h", h=H)[:, :, :, heads]

        def part(i):
            return n.top3[:, KB * b:KB * b + KB, KB * H * i:KB * H * i + kinds * H]\
                    .rearrange("p t (a h) -> p t a h", h=H)[:, :, :, heads]
        top(dve.tensor_copy(part(0), m))
        top(dve.tensor_tensor(rest, m, part(0), ALU.subtract))
        top(dve.tensor_copy(part(1), rest))
        dve.tensor_tensor(part(2), rest, part(1), ALU.subtract).then_inc(s.top_ready, 1)
        if kinds == 2 and last:
            m, w = n.top[:, KB * b:KB * b + KB, :, :], n.mw[:, KB * b:KB * b + KB, :, :]
            top(dve.tensor_tensor(w[:, :, 0, :], m[:, :, 0, :], m[:, :, 1, :], ALU.subtract))
            top(dve.tensor_scalar(w[:, :, 1, :], w[:, :, 0, :], -1.0, 0.0, ALU.mult, ALU.min))
            dve.tensor_scalar(w[:, :, 0, :], w[:, :, 0, :], 0.0, None, ALU.min).then_inc(s.gap_ready, 1)

    def mix(b, i, bank):
        t = KB * b + i
        if kinds == 1:
            o = k.ps[:, bank, :].rearrange("p (a h c) -> p a h c", a=NG, h=G)
            f = n.mf[:, 0, :].rearrange("p (a h) -> p a h", h=G)
            step(dve.reciprocal(f, o[:, :, :, HD]))
            ins = dve.tensor_tensor(n.att[:, t, :].rearrange("p (a h c) -> p a h c", h=G, c=HD), o[:, :, :, 0:HD],
                                    f.unsqueeze(3).broadcast_to([P, NG, G, HD]), ALU.mult)
            ins.then_inc(s.turned.freed["dve"], 1)
            s.turned.wait_read(dve, ("T", b, i))
            return
        o = k.ps[:, bank:bank + 2, :].rearrange("p a (g j h c) -> p (a g) j h c", g=2, j=2, h=G)

        def grouped(a):
            return a.rearrange("p (a h) -> p a h", h=G)
        if i == 0:
            dve.wait_ge(s.gap_exp, b + 1)
        for kd in range(2):
            dve.tensor_tensor(grouped(n.mt[:, kd, :]), o[:, :, kd, :, HD], grouped(n.mw[:, t, kd, :]), ALU.mult)
        step(dve.reciprocal(grouped(n.mf[:, 0, :]), o[:, :, i, :, HD]))
        step(dve.tensor_tensor(n.ml[:, :], n.mt[:, 0, :], n.mt[:, 1, :], ALU.add))
        step(dve.reciprocal(n.ml[:, :], n.ml[:, :]))
        step(dve.tensor_tensor(n.mt[:, :, :], n.mw[:, t, :, :], n.ml[:, :].unsqueeze(1).broadcast_to([P, 2, H]), ALU.mult))
        step(dve.tensor_tensor(n.mt[:, i, :], n.mt[:, i, :], n.mf[:, 0, :], ALU.add))
        for kd in range(2):
            ins = dve.tensor_tensor(n.tmp[:, kd, :, :, :], o[:, :, kd, :, 0:HD],
                                    grouped(n.mt[:, kd, :]).unsqueeze(3).broadcast_to([P, NG, G, HD]), ALU.mult)
        step(ins)
        dve.tensor_tensor(n.att[:, t, :].rearrange("p (a h c) -> p a h c", h=G, c=HD), n.tmp[:, 0, :, :, :],
                          n.tmp[:, 1, :, :, :], ALU.add).then_inc(s.turned.freed["dve"], 1)
        s.turned.wait_read(dve, ("T", b, i))

    for item in s.plan:
        kind, b = item[:2]
        ring = s.rings.get(kind)
        if ring and "dve" in ring.users[kind]:
            ring.wait_ready(dve, item)
            bank = ring.place(item)
        if kind == "A":
            t = KB * b + item[2]
            q_turned, k_turned = (k.ps[:, bank + i, :].bitcast(BF16).rearrange("p (j c) -> p j c", c=P) for i in range(2))
            dve.tensor_copy(n.k[:, :, tile(t)], k_turned)
            ins = dve.tensor_copy(n.q[SEG:P, 1:H:2, tile(t)], q_turned[SEG:P])
        elif kind == "S":
            t = KB * b + item[2]
            out = n.top[:, t, 0:kinds, 2 * item[3]:2 * item[3] + 2].rearrange("p a h -> p h a")
            ins = dve.tensor_reduce(out, k.ps[:, bank, :].rearrange("p (h a c) -> p h a c", h=2, a=kinds), AX_X, ALU.max)
        elif kind == "M":
            to = n.topT[:, b * S:b * S + S] if item[2] else n.topT_first[:, :]
            ins = dve.tensor_copy(to, k.ps[:, bank, :].bitcast(BF16)[:, 0:S])
        elif kind == "T":
            mix(b, item[2], bank)
        elif kind == "O":
            if kinds == 2:
                dve.wait_ge(s.bias_added, 1)
            ins = dve.tensor_tensor(k.x[:, 0:4, :], k.x[:, 0:4, :],
                                    k.ps[:, bank, :].rearrange("p (t d) -> p t d", d=D), ALU.add)
        if ring and "dve" in ring.users[kind] and kind != "T":
            ins.then_inc(ring.freed["dve"], 1)
        if item == ("A", 0, 0):
            norm_root(dve, k, s, 1)
        elif item == ("A", 0, 1):
            norm_z_vector(dve, k, s, 1)
        if kind == "S" and item[2:] == (KB - 1, PAIRS - 1):
            s.scores.wait_read(dve, item)
            dve.wait_ge(s.top_ready, b + 1)
            split_top(b, slice(G * FIRST_GROUPS if b == 0 else 0, H), True)
        elif item == ("S", 0, KB - 1, PAIRS // 2 - 1):
            s.scores.wait_read(dve, item)
            dve.wait_ge(s.prep, PREPARED["top3"])
            split_top(b, slice(0, G * FIRST_GROUPS), False)
        if item == ("M", 0, 0):
            second_half("q")
        elif item == ("S", 0, 0, PAIRS // 2):
            values()
        elif item == ("S", 0, 1, PAIRS // 2):
            second_half("k")
        elif item == ("S", 0, 0, PAIRS // 2 + 1):
            split_vector_rest(dve, n, s, "q", 1)
        elif item == ("S", 0, 1, PAIRS // 2 + 2):
            split_vector_rest(dve, n, s, "k", 1)
        elif item == ("M", 0, 1):
            for which in "qk":
                split_vector_low(dve, n, s, which, 1)
        elif item == ("T", B - 2, KB - 1):
            s.turned.wait_read(dve, ("O", B // 2 - 1, KB - 1))
            norm_ahead(dve, k, next_sublayer)


def project_tensor(pe, k, s, att, w):
    for t in range(NT // 2, NT):
        s.turned.wait_read(pe, ("T", t // KB, t % KB))
        pe.transpose(k.ps[:, 1, tile(t % 4)], att[:, t, :], k.ident).then_inc(s.attT_ready, 1)
    pe.wait_ge(s.attT_hi, 1)
    for t in range(NT // 2, NT):
        pe.matmul(k.ps[:, 3, tile(t % 4)], k.zT[:, tile(t)], w, start=True, stop=True).then_inc(s.out_ready, 1)


def project_scalar(act, k, s):
    act.wait_ge(s.attT_ready, NT // 2)
    act.activation(k.zT[:, half(1)], k.ps[:, 1, :], ACT.Copy).then_inc(s.attT_hi, 1)


def project_vector(dve, k, s):
    dve.wait_ge(s.out_ready, NT // 2)
    dve.tensor_tensor(k.x[:, 4:8, :], k.x[:, 4:8, :], k.ps[:, 3, :].rearrange("p (t d) -> p t d", d=D), ALU.add)


def row_over_tiles(k, name, tiles):
    return k.rows[:, ROW_AT[name]].unsqueeze(1).broadcast_to([P, tiles, D])


def copy_values(dve, k, n, s, bank, before, bias):
    for i in range(2):
        dve.wait_ge(s.proj_ready, before + i + 1)
        dve.tensor_tensor(n.v[:, 4 * i:4 * i + 4, :, 0:HD],
                          k.ps[:, bank + i, :].rearrange("p (t h c) -> p t h c", t=4, c=HD),
                          k.rows[:, ROW_AT[bias]].rearrange("p (h c) -> p h c", c=HD).unsqueeze(1)
                          .broadcast_to([P, 4, H, HD]), ALU.add).then_inc(s.v_copied, 1)


def project_half(pe, k, s, bank, lhsT, w, i):
    for t in range(4):
        mm = pe.matmul(k.ps[:, bank + i, tile(t)], lhsT[:, tile(4 * i + t)], w, start=True, stop=True)
    mm.then_inc(s.proj_ready, 1)


def project_in(pe, k, s, bank, lhsT, w):
    for i in range(2):
        project_half(pe, k, s, bank, lhsT, w, i)


def cross_phase(nc, k):
    s = narrow_sems(k, "cross")
    W = k.w
    with ExitStack() as ctx:
        n = narrow_buffers(nc, k, ctx, "cross")
        n.gaps = True
        block = ctx.enter_context(nc.Block())

        @block.gpsimd
        def _(pool):
            narrow_prepare(pool, n, s)

        @block.vector
        def _(dve):
            dve.wait_ge(k.rows_loaded, 32)

            def full(which, before, i):
                dve.wait_ge(s.proj_ready, before + i + 1)
                dve.tensor_tensor(n.full[which][:, 4 * i:4 * i + 4, :], k.ps[:, 2 + i, :].rearrange(
                    "p (t d) -> p t d", d=D), row_over_tiles(k, "b" + which + "0", 4), ALU.add)\
                   .then_inc(s.full_ready[which], 1)

            def second_half(which):
                if which == "q":
                    full("q", 4, 1)

            def values():
                copy_values(dve, k, n, s, 4, 2, "bv0")
                dve.wait_ge(s.zT_hi, s.nth + 1)
                dve.tensor_tensor(k.x[:, :, :], k.x[:, :, :], row_over_tiles(k, "bo0", NT), ALU.add)\
                   .then_inc(s.bias_added, 1)

            for i in range(2):
                full("k", 0, i)
            norm_vector_half(dve, k, s, 0)
            split_vector_rest(dve, n, s, "k", 0)
            norm_zT_vector(dve, k, s)
            norm_stats(dve, k, s, 1)
            full("q", 4, 0)
            split_vector_low(dve, n, s, "k", 0)
            split_vector_rest(dve, n, s, "q", 0)
            split_vector_low(dve, n, s, "q", 0)
            narrow_vector(dve, k, n, s, 2, second_half, values, "moe")
            dve.wait_ge(s.bias_added, 1)
            project_vector(dve, k, s)

        @block.scalar
        def _(act):
            split_scalar_high(act, n, s, "k", 0)
            norm_z_scalar(act, k, s, 0)
            split_scalar_middle(act, n, s, "k", 0)
            split_scalar_high(act, n, s, "q", 0)
            split_scalar_middle(act, n, s, "q", 0)
            narrow_scalar(act, k, n, s, 2, HD ** -0.5, lambda i: None)
            project_scalar(act, k, s)

        @block.tensor
        def _(pe):
            pe.wait_ge(k.ctx_loaded, 16)
            project_in(pe, k, s, 2, k.ctxT, W["wk0"])
            project_in(pe, k, s, 4, k.ctxT, W["wv0"])
            keep_warm(pe, k, 3)
            norm_tensor(pe, k, s, 0)
            keep_warm(pe, k, 3)
            wait_zT(pe, s, 0)
            pe.wait_ge(s.full_ready["k"], 2)
            project_half(pe, k, s, 2, k.zT, W["wq0"], 0)
            keep_warm(pe, k, 4)

            def second_half(place):
                if place == 0:
                    norm_tensor(pe, k, s, 1, SECOND_BANK)
                elif place == 1:
                    wait_zT(pe, s, 1)
                    project_half(pe, k, s, 2, k.zT, W["wq0"], 1)
            narrow_tensor(pe, k, n, s, 2, second_half, W["wo0"])
            project_tensor(pe, k, s, n.att, W["wo0"])



ABSOLUTE_AT = (14, 17, 20, 23)
LOG_AT = (28, 32)
SINE_AT = (40, 44, 48, 52)
SQUARE_AT = (42, 46, 50, 54)
PART_BATCHES = ((0, 1), (2, 3))
FIRST_EXPERTS = 2


def hidden_part(i):
    e, r = i // (2 * FC), i % (2 * FC)
    return (e, r % FC, r // FC) if e == 0 else (e, r // 2, r % 2)


def moe_phase(nc, k, ins):
    s = norm_sems(k, "moe")
    w1_loaded = [k.sem(f"moe_w1_loaded_{i}") for i in range(2)]
    w2_loaded = [k.sem(f"moe_w2_loaded_{i}") for i in range(2)]
    logits_ready = k.sem("moe_logits_ready")
    gate_step = k.sem("moe_gate_step")
    gap_ready = k.sem("moe_gap_ready")
    gap_exp = k.sem("moe_gap_exp")
    hidden_ready = k.sem("moe_hidden_ready")
    gelu_done = k.sem("moe_gelu_done")
    expert_ready = k.sem("moe_expert_ready")
    added = k.sem("moe_added")
    with ExitStack() as ctx:
        def sb(name, shape):
            return ctx.enter_context(nc.sbuf_tensor(name, shape, F32))
        w1 = sb("w1", [P, E, F])
        w2 = sb("w2", [P, E, FC, D])
        h = sb("hidden", [P, 2, FC, T])
        lg = sb("logits", [P, NT, E])
        cand = sb("candidates", [P, NT, E])
        pick1 = sb("pick1", [P, NT, E])
        pick2 = sb("pick2", [P, NT, E])
        comb = sb("comb", [P, NT, E])
        c1, c2, c3, c4 = (sb(f"moe_c{i}", [P, NT]) for i in range(4))
        box = box_prep_buffers(nc, k, ctx)
        block = ctx.enter_context(nc.Block())

        @block.sync
        def _(sp):
            for i, of in enumerate((slice(0, FIRST_EXPERTS), slice(FIRST_EXPERTS, E))):
                sp.dma_start(w1[:, of, :], ins["w1"][of].rearrange("e d f -> d e f")).then_inc(w1_loaded[i], 16)
                for e in range(of.start, of.stop):
                    sp.dma_start(w2[:, e, :, :], ins["w2"][e].rearrange("(c p) d -> p c d", p=P))\
                      .then_inc(w2_loaded[i], 16)
            box_load_sync(sp, k, box, ins)
            box_store_sync(sp, k, box)

        @block.vector
        def _(dve):
            norm_vector(dve, k, s)
            step = Link(dve, gate_step)

            def wide(a):
                return a[:, :].unsqueeze(2).broadcast_to([P, NT, E])
            rank = k.const[:, CONST_AT["rank"]].unsqueeze(1).broadcast_to([P, NT, E])
            dve.wait_ge(logits_ready, 1)
            step(dve.tensor_copy(lg[:, :, :], k.ps[:, 2, 0:NT * E].rearrange("p (t e) -> p t e", e=E)))

            def best(top, pick):
                step(dve.tensor_reduce(top[:, :], lg[:, :, :], AX_X, ALU.max))
                step(dve.tensor_tensor(cand[:, :, :], lg[:, :, :], wide(top), ALU.is_equal))
                step(dve.tensor_tensor(cand[:, :, :], cand[:, :, :], rank, ALU.mult))
                step(dve.tensor_reduce(c3[:, :], cand[:, :, :], AX_X, ALU.max))
                step(dve.tensor_tensor(pick[:, :, :], cand[:, :, :], wide(c3), ALU.is_equal))

            best(c1, pick1)
            step(dve.scalar_tensor_tensor(out=lg[:, :, :], in0=pick1[:, :, :], scalar=-3e38, in1=lg[:, :, :],
                                          op0=ALU.mult, op1=ALU.add))
            best(c2, pick2)
            dve.tensor_tensor(c3[:, :], c2[:, :], c1[:, :], ALU.subtract).then_inc(gap_ready, 1)
            dve.wait_ge(gap_exp, 1)
            step(dve.tensor_scalar(c1[:, :], c4[:, :], 1.0, None, ALU.add))
            step(dve.reciprocal(c1[:, :], c1[:, :]))
            step(dve.tensor_tensor(pick2[:, :, :], pick2[:, :, :], wide(c4), ALU.mult))
            step(dve.tensor_tensor(comb[:, :, :], pick1[:, :, :], pick2[:, :, :], ALU.add))
            step(dve.tensor_tensor(comb[:, :, :], comb[:, :, :], wide(c1), ALU.mult))
            box_sizes_own_vector(dve, box)
            box_centres_vector(dve, box)
            for b in range(B):
                box_apart_vector(dve, box, b)
            box_sizes_vector(dve, box)
            for e in range(E):
                if e == 2:
                    for b in range(B):
                        box_clip_vector(dve, box, b)
                elif e == 3:
                    box_size_angles_vector(dve, box)
                if e in (3, 4):
                    for b in PART_BATCHES[e - 3]:
                        box_angle_vector(dve, box, b)
                if e in (5, 6):
                    for b in PART_BATCHES[e - 5]:
                        box_cosine_vector(dve, box, b)
                for t in range(NT):
                    if (e, t) == (E - 1, NT // 2):
                        dve.wait_ge(added, e * NT + t)
                        norm_ahead(dve, k, "rotary")
                    dve.wait_ge(expert_ready, e * NT + 4 * (t // 4) + 4)
                    if e >= 1:
                        dve.wait_ge(added, (e - 1) * NT + t + 1)
                    dve.scalar_tensor_tensor(out=k.x[:, t, :], in0=k.ps[:, 2 * (e % 2) + t // 4, tile(t % 4)],
                                             scalar=comb[:, t, e:e + 1], in1=k.x[:, t, :], op0=ALU.mult,
                                             op1=ALU.add).then_inc(added, 1)

        @block.scalar
        def _(act):
            norm_z_scalar(act, k, s, 0)
            for i in range(E * 2 * FC):
                if i == 2 * FC:
                    act.wait_ge(gap_ready, 1)
                    act.activation(c4[:, :], c3[:, :], ACT.Exp).then_inc(gap_exp, 1)
                e, c, part = hidden_part(i)
                if i == NT // 2:
                    norm_z_scalar(act, k, s, 1)
                    norm_zT_scalar(act, k, s)
                if i in ABSOLUTE_AT:
                    box_absolute_scalar(act, box, ABSOLUTE_AT.index(i))
                elif i in LOG_AT:
                    for b in PART_BATCHES[LOG_AT.index(i)]:
                        box_log_scalar(act, box, b)
                elif i in SINE_AT:
                    box_sine_scalar(act, box, SINE_AT.index(i))
                elif i in SQUARE_AT:
                    box_square_scalar(act, box, SQUARE_AT.index(i))
                if i == LOG_AT[0]:
                    box_size_log_scalar(act, box)
                elif i == SINE_AT[0]:
                    box_size_sine_scalar(act, box)
                act.wait_ge(hidden_ready, i + 1)
                if e >= 2:
                    act.wait_ge(expert_ready, (e - 1) * NT)
                act.activation(h[:, e % 2, c, half(part)], k.ps[:, 4 + i % 4, :], ACT.Gelu_apprx_tanh)\
                   .then_inc(gelu_done, 1)

        @block.tensor
        def _(pe):
            norm_tensor(pe, k, s, 0)
            keep_warm(pe, k, 4)
            wait_zT(pe, s, 0)

            def logits():
                for t in range(NT):
                    mm = pe.matmul(k.ps[:, 2, t * E:t * E + E], k.zT[:, tile(t)], k.w["gate"], start=True, stop=True)
                mm.then_inc(logits_ready, 1)

            def hidden(i):
                e, c, part = hidden_part(i)
                if i == 0:
                    pe.wait_ge(w1_loaded[0], 16)
                elif i == NT // 2:
                    keep_warm(pe, k, 10, 3)
                    norm_tensor(pe, k, s, 1)
                    keep_warm(pe, k, 4, 3)
                    wait_zT(pe, s, 1)
                elif e == FIRST_EXPERTS:
                    pe.wait_ge(w1_loaded[1], 16)
                if i >= 4:
                    pe.wait_ge(gelu_done, i - 3)
                pe.matmul(k.ps[:, 4 + i % 4, :], w1[:, e, tile(c)], k.zT[:, half(part)], start=True,
                          stop=True).then_inc(hidden_ready, 1)

            def expert(e, t):
                pe.wait_ge(gelu_done, (e + 1) * 2 * FC)
                pe.wait_ge(w2_loaded[e >= FIRST_EXPERTS], 16 * (E - FIRST_EXPERTS if e >= FIRST_EXPERTS else FIRST_EXPERTS))
                if e == 1:
                    pe.wait_ge(gate_step, 1)
                if e >= 2:
                    pe.wait_ge(added, (e - 2) * NT + 4 * (t // 4) + 4)
                for c in range(FC):
                    mm = pe.matmul(k.ps[:, 2 * (e % 2) + t // 4, tile(t % 4)], h[:, e % 2, c, tile(t)],
                                   w2[:, e, c, :], start=(c == 0), stop=(c == FC - 1))
                mm.then_inc(expert_ready, 1)

            for e in range(E + 1):
                for i in range(NT):
                    if e < E:
                        hidden(e * NT + i)
                    if e >= 1:
                        expert(e - 1, i)
                if e == 0:
                    logits()



def rotary_phase(nc, k):
    s = narrow_sems(k, "rotary")
    rope_step = k.sem("rotary_rope_step")
    W = k.w
    with ExitStack() as ctx:
        n = narrow_buffers(nc, k, ctx, "rotary")
        n.gaps = False
        block = ctx.enter_context(nc.Block())

        @block.gpsimd
        def _(pool):
            narrow_prepare(pool, n, s)

        @block.vector
        def _(dve):
            step = Link(dve, rope_step)

            def rope(bank, i, which):
                dve.wait_ge(s.proj_ready, 3 * i + (2 if which == "k" else 1))
                src = k.ps[:, bank + i, :].rearrange("p (b c) -> p b c", b=2)
                pairs = k.ps[:, bank + i, :].rearrange("p (b c two) -> p b c two", b=2, two=2)
                by_cos = n.att[:, 0:4, :].rearrange("p t c -> p (t c)")
                by_sin = n.att[:, 4:8, :].rearrange("p t c -> p (t c)")
                sin = k.const[:, CONST_AT["sin"]].rearrange("p (c two) -> p c two", two=2)
                dve.tensor_tensor(by_cos.rearrange("p (b c) -> p b c", b=2), src,
                                  k.const[:, CONST_AT["cos"]].unsqueeze(1).broadcast_to([P, 2, KB * P]), ALU.mult)
                for even in range(2):
                    ins = dve.tensor_tensor(by_sin.rearrange("p (b c two) -> p b c two", b=2, two=2)[:, :, :, even],
                                            pairs[:, :, :, 1 - even],
                                            sin[:, :, even].unsqueeze(1).broadcast_to([P, 2, KB * P // 2]), ALU.mult)
                step(ins)
                dve.tensor_tensor(n.full[which][:, 4 * i:4 * i + 4, :].rearrange("p t c -> p (t c)"), by_cos, by_sin,
                                  ALU.add).then_inc(s.full_ready[which], 1)
                dve.wait_ge(s.full_ready[which], i + 1)

            def second_half(which):
                rope({"q": 2, "k": 4}[which], 1, which)

            norm_z_vector(dve, k, s, 0)
            norm_zT_vector(dve, k, s)
            norm_stats(dve, k, s, 1)
            rope(2, 0, "q")
            rope(4, 0, "k")
            for which in "qk":
                split_vector_rest(dve, n, s, which, 0)
            for which in "qk":
                split_vector_low(dve, n, s, which, 0)
            narrow_vector(dve, k, n, s, 1, second_half, lambda: None, "box")
            project_vector(dve, k, s)

        @block.scalar
        def _(act):
            def values(i):
                act.wait_ge(s.proj_ready, 3 * i + 3)
                act.activation(n.v[:, 4 * i:4 * i + 4, :, 0:HD],
                               k.ps[:, 4 * i, :].rearrange("p (t h c) -> p t h c", t=4, c=HD), ACT.Copy)\
                   .then_inc(s.v_copied, 1)

            norm_z_scalar(act, k, s, 0)
            for which in "qk":
                split_scalar_high(act, n, s, which, 0)
            for which in "qk":
                split_scalar_middle(act, n, s, which, 0)
            values(0)
            narrow_scalar(act, k, n, s, 1, HD ** -0.5, values)
            project_scalar(act, k, s)

        @block.tensor
        def _(pe):
            norm_tensor(pe, k, s, 0)
            keep_warm(pe, k, 3)
            wait_zT(pe, s, 0)
            project_half(pe, k, s, 2, k.zT, W["wq1"], 0)
            project_half(pe, k, s, 4, k.zT, W["wk1"], 0)
            project_half(pe, k, s, 0, k.zT, W["wv1"], 0)
            keep_warm(pe, k, 18)

            def second_half(place):
                if place == 0:
                    norm_tensor(pe, k, s, 1, SECOND_BANK)
                elif place == 1:
                    wait_zT(pe, s, 1)
                    project_half(pe, k, s, 2, k.zT, W["wq1"], 1)
                elif place == 2:
                    project_half(pe, k, s, 4, k.zT, W["wk1"], 1)
                else:
                    pe.wait_ge(s.full_ready["k"], 1)
                    project_half(pe, k, s, 3, k.zT, W["wv1"], 1)

            pe.wait_ge(s.v_copied, 1)
            narrow_tensor(pe, k, n, s, 1, second_half, W["wo1"])
            project_tensor(pe, k, s, n.att, W["wo1"])



def box_plan():
    plan = []
    for b in range(B + 1):
        front = [(kind, b, j) for kind in "KQV" for j in range(2)] if b < B else []
        late = [("G", b - 1, 1, j) for j in range(NQ // 2)] if b else []
        if b == B:
            plan += late[:NQ // 4]
            sc, late = late[NQ // 4:], []
        while front or late:
            if front:
                plan.append(front.pop(0))
            if late:
                plan.append(late.pop(0))
        if b < B:
            sc = [("S", b, i, j) for i in range(KB) for j in range(4)]
        pv = []
        if b:
            pv = [("P", b - 1, 0, j) for j in range(3)]
            pv += [("P", b - 1, 1, 0), ("T", b - 1, 0), ("P", b - 1, 1, 1), ("O", b - 1, 0), ("P", b - 1, 1, 2),
                   ("T", b - 1, 1), ("O", b - 1, 1)]
        last = []
        while sc or pv:
            if sc:
                plan.append(sc.pop(0))
            elif b < B:
                last, pv = pv, []
            if pv:
                plan.append(pv.pop(0))
        if b < B:
            plan.append(("M", b))
            for j in range(4):
                plan += last[:1] + [("X", b, 0, j)]
                last = last[1:]
            for j in range(4):
                plan += [("X", b, 1, j), ("G", b, 0, 2 * j), ("G", b, 0, 2 * j + 1)]
    return plan


PV_HEADS = [range(0, 6), range(6, 11), range(11, 16)]
SLOT_USERS = {"K": "act", "Q": "dve", "V": "dve", "S": "dve", "M": "dve", "X": "act", "T": "act", "O": "dve"}


def box_phase(nc, k, ins):
    s = norm_sems(k, "box")
    prep = k.sem("box_prep")
    wk_loaded, wv_loaded, wq_loaded, wo_loaded = (k.sem(f"box_{n}_loaded") for n in ("wk", "wv", "wq", "wo"))
    sums_loaded = k.sem("box_weights_loaded")
    pairs_loaded = [k.sem(f"box_pairs_loaded_{i}") for i in range(2)]
    sums_step = k.sem("box_sums_step")
    sums_ready = k.sem("box_sums_ready")
    slot_ready = k.sem("box_slot_ready")
    slot_freed = {"act": k.sem("box_slot_freed_act"), "dve": k.sem("box_slot_freed_dve")}
    g_ready = k.sem("box_g_ready")
    g_used = k.sem("box_g_used")
    pv_ready = k.sem("box_pv_ready")
    pv_used = k.sem("box_pv_used")
    pv_step = k.sem("box_pv_step")
    split_step = k.sem("box_split_step")
    max_split = k.sem("box_max_split")
    x_step = k.sem("box_x_step")
    plan = box_plan()
    slots = [item for item in plan if item[0] in SLOT_USERS]
    slot_at = {item: n for n, item in enumerate(slots)}
    g_at = {item: n for n, item in enumerate(i for i in plan if i[0] == "G")}
    pv_at = {item: n for n, item in enumerate(i for i in plan if i[0] == "P")}

    def freed(item):
        user = SLOT_USERS[item[0]]
        return slot_freed[user], sum(SLOT_USERS[i[0]] == user for i in slots[:slot_at[item] + 1])

    with ExitStack() as ctx:
        def sb(name, shape, dt=F32):
            return ctx.enter_context(nc.sbuf_tensor(name, shape, dt))
        wide = sb("wide", [P, WIDE_COLS])
        q2 = sb("box_q", [P, NC, 2, S])
        k2 = sb("box_k", [P, NC, S])
        v2 = sb("box_v", [P, 2, KB, H, U])
        top = sb("box_top", [P, NT, H])
        rest = sb("box_top_rest", [P, 2, H])
        top3 = sb("box_top3", [P, KB, P], BF16)
        top3T = sb("box_top3T", [P, S], BF16)
        e = sb("box_e", [P, 3, S, H])
        pairs = sb("box_pairs", [P, 2, NQ, P])
        sums = sb("box_sums", [P, S, H])
        sums2 = sb("box_sums2", [P, P, H])
        att = sb("box_att", [P, 2, H, DK])
        rden = sb("box_rden", [P, 2, 8])
        attT = k.z
        block = ctx.enter_context(nc.Block())
        r5 = slice(RPAIR, RPAIR + RSUM)
        rows = RPAIR + RSUM

        def slot(item):
            return 2 * (slot_at[item] % 2)

        @block.sync
        def _(sp):
            for name, ready in (("wk2", wk_loaded), ("wq2", wq_loaded), ("wv2", wv_loaded), ("wo2", wo_loaded)):
                sp.dma_start(wide[:, WIDE_AT[name]], ins["wide"][:, WIDE_AT[name]]).then_inc(ready, 16)
            sp.dma_start(sums[0:RPAIR, :, :].rearrange("p (n q) h -> p n (q h)", q=QG),
                         ins["wg_rows"].unsqueeze(1).broadcast_to([RPAIR, NQ, H * QG])).then_inc(sums_loaded, 16)
            sp.wait_ge(k.pairs_stored, 16 * B)
            for u in range(B * KB):
                b, kb = u // KB, u % KB
                if u >= 2:
                    sp.wait_ge(g_ready, (u - 1) * NQ // 2)
                for f in range(NPAIR):
                    sp.dma_start(pairs[QG * f:QG * f + QG, u % 2, :, :],
                                 k.pairs[b, :, f, kb * P:kb * P + P].rearrange("(n q) m -> q n m", q=QG))\
                      .then_inc(pairs_loaded[u % 2], 16)
                sp.dma_start(pairs[r5, u % 2, :, :], k.size_waves[r5, 0, b * S + kb * P:b * S + kb * P + P].unsqueeze(1)
                             .broadcast_to([RSUM, NQ, P])).then_inc(pairs_loaded[u % 2], 16)

        @block.gpsimd
        def _(pool):
            pool.memset(v2[:, :, :, :, DK:U], 1.0).then_inc(prep, 1)
            pool.wait_ge(prep, 1)
            pool.memset(top3[:, :, :], 0.0).then_inc(prep, 1)
            pool.wait_ge(prep, 2)
            pool.memset(q2[DK:P, :, 0, :], 0.0).then_inc(prep, 1)
            pool.wait_ge(prep, 3)
            pool.memset(q2[0:DK, :, 1, :], 0.0).then_inc(prep, 1)
            pool.wait_ge(prep, 4)
            step = Link(pool, sums_step)
            full = [RSUM, P, H]
            pool.wait_ge(k.rows_loaded, 32)
            for b in range(B):
                if b >= 1:
                    pool.wait_ge(g_ready, b * NQ)
                for i in range(KB):
                    for form, dst in ((0, sums[r5, tile(i), :]), (1, sums2[r5, :, :])):
                        step(pool.tensor_tensor(dst, k.size_waves[r5, form, b * S + i * P:b * S + i * P + P]
                                                .unsqueeze(2).broadcast_to(full),
                                                k.box5[r5, form, :].unsqueeze(1)
                                                .broadcast_to(full), ALU.mult))
                    pool.tensor_tensor(sums[r5, tile(i), :], sums[r5, tile(i), :], sums2[r5, :, :], ALU.add)\
                        .then_inc(sums_ready, 1)
                    pool.wait_ge(sums_ready, KB * b + i + 1)

        @block.tensor
        def _(pe):
            wq, wk, wv, wo = (wide[:, WIDE_AT[n]] for n in ("wq2", "wk2", "wv2", "wo2"))

            def wait_freed(item):
                pe.wait_ge(*freed(item))

            for item in plan:
                kind, b = item[:2]
                if item == ("K", 0, 0):
                    pe.wait_ge(wk_loaded, 16)
                elif item == ("V", 0, 0):
                    norm_tensor(pe, k, s, 1, NORM_BANK + 1)
                    pe.wait_ge(wv_loaded, 16)
                elif item == ("Q", B // 2, 0):
                    wait_zT(pe, s, 1)
                elif item == ("Q", 0, 0):
                    norm_tensor(pe, k, s, 0, NORM_BANK)
                    keep_warm(pe, k, 4)
                    wait_zT(pe, s, 0)
                    pe.wait_ge(wq_loaded, 16)
                elif item == ("G", 0, 0, 0):
                    pe.wait_ge(sums_loaded, 16)
                elif item == ("O", 0, 0):
                    pe.wait_ge(wo_loaded, 16)
                if kind in SLOT_USERS:
                    bank = slot(item)
                    if slot_at[item] >= 2:
                        wait_freed(slots[slot_at[item] - 2])
                if kind in "KQ":
                    w, src = (wk, k.ctxT) if kind == "K" else (wq, k.zT)
                    for j in range(4):
                        mm = pe.matmul(k.ps[:, bank + j // 2, j % 2 * S:j % 2 * S + S], w[:, tile(4 * item[2] + j)],
                                       src[:, b * S:b * S + S], start=True, stop=True)
                elif kind == "V":
                    for j in range(2):
                        mm = pe.matmul(k.ps[:, bank + j, :], k.ctxT[:, tile(KB * b + item[2])], wv[:, half(j)],
                                       start=True, stop=True)
                elif kind == "S":
                    wait_freed(("K", b, 1))
                    wait_freed(("Q", b, 1))
                    for j in range(4):
                        h = 4 * item[3] + j
                        mm = pe.matmul(k.ps[:, bank + j // 2, j % 2 * S:j % 2 * S + S], q2[:, h // 2, h % 2, tile(item[2])],
                                       k2[:, h // 2, :], start=True, stop=True)
                elif kind == "M":
                    pe.wait_ge(max_split, b + 1)
                    for i in range(KB):
                        mm = pe.transpose(k.ps[:, bank, :].bitcast(BF16)[:, tile(i)], top3[:, i, :], k.identb[:, :])
                elif kind == "X":
                    wait_freed(("M", b))
                    for j in range(4):
                        h = 4 * item[3] + j
                        at = k.ps[:, bank + j // 2, j % 2 * S:j % 2 * S + S]
                        pe.matmul(at, k2[:, h // 2, tile(item[2])], q2[:, h // 2, h % 2, :], start=True, stop=False,
                                  skip_group_check=True)
                        mm = pe.matmul(at, k.minus[:, h, :], top3T[:, :], start=False, stop=True, skip_group_check=True)
                elif kind == "G":
                    n = g_at[item]
                    u = KB * b + item[2]
                    pe.wait_ge(pairs_loaded[u % 2], 16 * (NPAIR + 1) * (u // 2 + 1))
                    pe.wait_ge(sums_ready, KB * (b + 1))
                    if n >= 2:
                        pe.wait_ge(g_used, n - 1)
                    for j in range(2):
                        qg = 2 * item[3] + j
                        mm = pe.matmul(k.ps[:, G_BANK + n % 2, j * H * QG:(j + 1) * H * QG], pairs[0:rows, u % 2, qg, :],
                                       sums[0:rows, QG * qg:QG * qg + QG, :], start=True, stop=True)
                    mm.then_inc(g_ready, 1)
                elif kind == "P":
                    n = pv_at[item]
                    pe.wait_ge(g_used, g_at[("G", b, 1, (item[2] + 1) * NQ // 4 - 1)] + 1)
                    wait_freed(("V", b, 1))
                    if n >= 2:
                        pe.wait_ge(pv_used, n - 1)
                    for j, h in enumerate(PV_HEADS[item[3]]):
                        for kb in range(KB):
                            mm = pe.matmul(k.ps[:, 6 + n % 2, j * U:j * U + U],
                                           e[:, (KB * b + kb) % 3, tile(item[2]), h],
                                           v2[:, b % 2, kb, h, :], start=(kb == 0), stop=(kb == KB - 1))
                    mm.then_inc(pv_ready, 1)
                elif kind == "T":
                    if (b, item[2]) == (B - 1, KB - 1):
                        keep_warm(pe, k, 4, G_BANK)
                    pe.wait_ge(pv_used, pv_at[("P", b, item[2], 2)] + 1)
                    for c in range(NC):
                        mm = pe.transpose(k.ps[:, bank + c // 4, tile(c % 4)], att[:, item[2], 2 * c:2 * c + 2, :],
                                          k.ident)
                elif kind == "O":
                    wait_freed(("T", b, item[2]))
                    for c in range(NC):
                        mm = pe.matmul(k.ps[:, bank, 0:D], attT[:, c, :], wo[:, tile(c)], start=(c == 0),
                                       stop=(c == NC - 1))
                if kind in SLOT_USERS:
                    mm.then_inc(slot_ready, 1)

        @block.scalar
        def _(act):
            norm_z_scalar(act, k, s, 0)
            for item in plan:
                kind, b = item[:2]
                if item == ("Q", 0, 0):
                    norm_z_scalar(act, k, s, 1)
                elif item == ("V", 0, 0):
                    norm_zT_scalar(act, k, s, NORM_BANK + 1)
                if SLOT_USERS.get(kind) != "act":
                    continue
                act.wait_ge(slot_ready, slot_at[item] + 1)
                bank = slot(item)
                if kind == "K":
                    for j in range(4):
                        c = 4 * item[2] + j
                        ins_ = act.activation(k2[:, c, :], k.ps[:, bank + j // 2, j % 2 * S:j % 2 * S + S], ACT.Identity,
                                              bias=k.w["bk2"][:, c:c + 1])
                elif kind == "X":
                    ins_ = act.activation(
                        e[:, (KB * b + item[2]) % 3, :, 4 * item[3]:4 * item[3] + 4].rearrange("p q h -> p h q"),
                        k.ps[:, bank:bank + 2, :].rearrange("p a (h q) -> p (a h) q", h=2), ACT.Exp, scale=DK ** -0.5)
                else:
                    ins_ = act.activation(attT[:, :, :].rearrange("p (a c) t -> p a (c t)", a=2),
                                          k.ps[:, bank:bank + 2, :], ACT.Copy)
                ins_.then_inc(slot_freed["act"], 1)

        @block.vector
        def _(dve):
            norm_z_vector(dve, k, s, 0)
            norm_vector_half(dve, k, s, 1)
            split = Link(dve, split_step)
            pvl = Link(dve, pv_step)
            for item in plan:
                kind, b = item[:2]
                bank = 0
                if item == ("T", B - 1, 0):
                    dve.wait_ge(*freed(("O", B // 2 - 1, KB - 1)))
                    norm_ahead(dve, k, "chain")
                if item == ("Q", 0, 0):
                    norm_zT_vector(dve, k, s, NORM_BANK)
                    dve.wait_ge(prep, 4)
                elif item == ("S", 0, 0, 2):
                    dve.wait_ge(s.zT_hi, s.nth + 1)
                    dve.tensor_tensor(k.x[:, :, :], k.x[:, :, :], row_over_tiles(k, "bo2", NT), ALU.add)\
                       .then_inc(x_step, 1)
                    dve.wait_ge(x_step, 1)
                if SLOT_USERS.get(kind) == "dve":
                    dve.wait_ge(slot_ready, slot_at[item] + 1)
                    bank = slot(item)
                if kind == "Q":
                    c = slice(4 * item[2], 4 * item[2] + 4)
                    for side in range(2):
                        r = slice(DK * side, DK * side + DK)
                        ins_ = dve.tensor_tensor(q2[r, c, side, :],
                                                 k.ps[r, bank:bank + 2, :].rearrange("p a (c q) -> p (a c) q", q=S),
                                                 k.w["bq2"][r, c].unsqueeze(2).broadcast_to([DK, 4, S]), ALU.add)
                elif kind == "V":
                    ins_ = dve.tensor_tensor(v2[:, b % 2, item[2], :, 0:DK],
                                             k.ps[:, bank:bank + 2, :].rearrange("p a (h c) -> p (a h) c", c=DK),
                                             k.rows[:, ROW_AT["bv2"]].rearrange("p (h c) -> p h c", c=DK), ALU.add)
                elif kind == "S":
                    t = KB * b + item[2]
                    ins_ = dve.tensor_reduce(top[:, t, 4 * item[3]:4 * item[3] + 4],
                                             k.ps[:, bank:bank + 2, :].rearrange("p a (h c) -> p (a h) c", c=S), AX_X,
                                             ALU.max)
                elif kind == "M":
                    ins_ = dve.tensor_copy(top3T[:, :], k.ps[:, bank, :].bitcast(BF16)[:, 0:S])
                elif kind == "O":
                    t = KB * b + item[2]
                    ins_ = dve.tensor_tensor(k.x[:, t, :], k.x[:, t, :], k.ps[:, bank, 0:D], ALU.add)
                elif kind == "G":
                    n = g_at[item]
                    part = e[:, (KB * b + item[2]) % 3, 2 * QG * item[3]:2 * QG * (item[3] + 1), :].rearrange("p q h -> p (q h)")
                    dve.wait_ge(g_ready, n + 1)
                    dve.wait_ge(*freed(("X", b, item[2], 3)))
                    dve.scalar_tensor_tensor(out=part, in0=k.ps[:, G_BANK + n % 2, :], scalar=1e-6, in1=part, op0=ALU.max,
                                             op1=ALU.mult).then_inc(g_used, 1)
                elif kind == "P":
                    n = pv_at[item]
                    heads = PV_HEADS[item[3]]
                    m = len(heads)
                    dve.wait_ge(pv_ready, n + 1)
                    o = k.ps[:, 6 + n % 2, 0:m * U].rearrange("p (h c) -> p h c", c=U)
                    if n >= 2:
                        dve.wait_ge(pv_used, n - 1)
                    pvl(dve.reciprocal(rden[:, n % 2, 0:m], o[:, :, DK]))
                    dve.tensor_tensor(att[:, item[2], heads[0]:heads[0] + m, :], o[:, :, 0:DK],
                                      rden[:, n % 2, 0:m].unsqueeze(2).broadcast_to([P, m, DK]), ALU.mult).then_inc(pv_used, 1)
                if SLOT_USERS.get(kind) == "dve":
                    ins_.then_inc(slot_freed["dve"], 1)
                if kind == "S" and item[2:] == (KB - 1, 3):
                    dve.wait_ge(*freed(item))
                    m2 = top[:, KB * b:KB * b + KB, :]

                    if b >= 1:
                        dve.wait_ge(*freed(("M", b - 1)))

                    def part(j):
                        return top3[:, :, KB * H * j:KB * H * j + H]
                    split(dve.tensor_copy(part(0), m2))
                    split(dve.tensor_tensor(rest[:, :, :], m2, part(0), ALU.subtract))
                    split(dve.tensor_copy(part(1), rest[:, :, :]))
                    dve.tensor_tensor(part(2), rest[:, :, :], part(1), ALU.subtract).then_inc(max_split, 1)
                    dve.wait_ge(max_split, b + 1)


def box_arrays(a):
    boxes = a["fside_BxSx4_0"].reshape(T, 4)
    lo_x, lo_y, hi_x, hi_y = boxes.T
    zero = np.zeros(T, np.float32)
    wg, bg = a["L1_xattn_Wg"], a["L1_xattn_bg"]
    quarters = np.array([[0.25, 0.0, 0.25, 0.0, 0.25], [0.0, -0.25, 0.0, -0.25, 0.25]], np.float32)
    box_phase = np.repeat(np.stack([quarters, quarters * np.float32(2 * np.pi)], -1).reshape(FORMS * RSUM, 2),
                          SIZE_CUT, 0)
    box5 = np.zeros((RSUM, FORMS, H), np.float32)
    box5[0:2, 0], box5[2:4, 0] = wg[:, 6], wg[:, 7]
    box5[0:2, 1], box5[2:4, 1], box5[4, 1] = wg[:, 2], wg[:, 3], bg
    ends = np.stack([np.stack([hi_x, hi_x, hi_y, hi_y, zero]), np.stack([lo_x, lo_x, lo_y, lo_y, zero])], 1)
    ends = ends.reshape(RSUM, 2, SIZE_CUT, T // SIZE_CUT).transpose(0, 2, 1, 3).reshape(SIZE_ROWS, 2, T // SIZE_CUT)
    wg_rows = np.zeros((NPAIR, QG, QG, H), np.float32)
    for f, col in enumerate((0, 1, 4, 5)):
        for q in range(QG):
            wg_rows[f, q, q, :] = wg[:, col]
    return {
        "boxes": boxes, "box_rows": np.ascontiguousarray(boxes.T), "box5": box5,
        "box_ends": np.ascontiguousarray(np.tile(ends, (FORMS, 1, 1))), "box_phase": box_phase,
        "wg_rows": wg_rows.reshape(RPAIR, H * QG),
    }



def chain_phase(nc, k, out):
    s = norm_sems(k, "chain")
    stored = k.sem("stored")
    product_ready = k.sem("chain_product_ready")
    product_copied = k.sem("chain_product_copied")
    last_ready = k.sem("chain_last_ready")
    biased = k.sem("chain_biased")
    tanh_done = k.sem("chain_tanh_done")
    W = k.w
    with ExitStack() as ctx:
        products = ctx.enter_context(nc.sbuf_tensor("chain_products", [P, 2, D], F32))
        block = ctx.enter_context(nc.Block())

        @block.sync
        def _(sp):
            tokens = out.rearrange("(t p) d -> p t d", p=P)
            for i in range(2):
                sp.wait_ge(k.x_final, i + 1)
                sp.dma_start(tokens[:, 4 * i:4 * i + 4, :], k.x[:, 4 * i:4 * i + 4, :]).then_inc(stored, 16)
            sp.wait_ge(stored, 32)

        @block.vector
        def _(dve):
            norm_vector(dve, k, s)
            for i in range(2):
                dve.wait_ge(last_ready, i + 1)
                dve.tensor_tensor(k.z[:, 4 * i:4 * i + 4, :], k.ps[:, 6 + i, :].rearrange("p (t d) -> p t d", d=D),
                                  row_over_tiles(k, "ffn_b", 4), ALU.add).then_inc(biased, 1)
            for i in range(2):
                dve.wait_ge(tanh_done, i + 1)
                dve.tensor_tensor(k.x[:, 4 * i:4 * i + 4, :], k.x[:, 4 * i:4 * i + 4, :],
                                  k.z[:, 4 * i:4 * i + 4, :], ALU.add).then_inc(k.x_final, 1)

        @block.scalar
        def _(act):
            for j in range(2):
                act.wait_ge(product_ready, j + 1)
                act.activation(products[:, j, :], k.ps[:, 2 + j, 0:D], ACT.Copy).then_inc(product_copied, 1)
            norm_scalar(act, k, s)
            for i in range(2):
                act.wait_ge(biased, i + 1)
                act.activation(k.z[:, 4 * i:4 * i + 4, :], k.z[:, 4 * i:4 * i + 4, :], ACT.Tanh).then_inc(tanh_done, 1)

        @block.tensor
        def _(pe):
            pe.matmul(k.ps[:, 2, 0:D], W["ffn2"], W["ffn1_T"], start=True, stop=True).then_inc(product_ready, 1)
            pe.wait_ge(product_copied, 1)
            pe.matmul(k.ps[:, 3, 0:D], products[:, 0, :], W["ffn3"], start=True, stop=True).then_inc(product_ready, 1)
            norm_tensor(pe, k, s, 0)
            keep_warm(pe, k, 8)
            wait_zT(pe, s, 0)
            pe.wait_ge(product_copied, 2)
            for i in range(2):
                if i == 1:
                    norm_tensor(pe, k, s, 1)
                    wait_zT(pe, s, 1)
                for t in range(4):
                    mm = pe.matmul(k.ps[:, 6 + i, tile(t)], k.zT[:, tile(4 * i + t)], products[:, 1, :], start=True,
                                   stop=True)
                mm.then_inc(last_ready, 1)


def decoder(nc, ins, out):
    with ExitStack() as ctx:
        def sb(name, shape, dt=F32):
            return ctx.enter_context(nc.sbuf_tensor(name, shape, dt))
        k = Parts()
        k.sem = lambda name: ctx.enter_context(nc.semaphore(name))
        k.ps = ctx.enter_context(nc.psum_tensor("ps", [P, 8, 512], F32))
        k.norm_sems = [k.sem(f"norm_{n}") for n in ("step", "z_vector", "z_scalar", "zT_in_psum", "zT_lo", "zT_hi")]
        k.x = sb("x", [P, NT, D])
        k.z = sb("z", [P, NT, D])
        k.zT = sb("zT", [P, T])
        k.ctxT = sb("ctxT", [P, T])
        k.stats = sb("stats", [P, NT, 6])
        k.mv = sb("mv", [P, NT, 2])
        k.var = sb("var", [P, NT])
        k.rstd = sb("rstd", [P, NT])
        k.newton = sb("newton", [P, NT])
        k.shift = sb("shift", [P, NT])
        k.const = sb("const", [P, CONST_COLS])
        k.ident = k.const[:, CONST_AT["ident"]]
        k.identb = sb("identb", [P, P], BF16)
        k.minus = sb("minus", [P, KB * H, P], BF16)
        k.weights = sb("weights", [P, W_COLS])
        k.w = {n: k.weights[:, c] for n, c in W_AT.items()}
        k.rows = sb("rows", [P, ROW_COLS])
        k.box5 = sb("box5", [P, FORMS, H])
        k.size_waves = sb("size_waves", [P, 2, T])
        k.pairs = nc.dram_tensor("pair_features", (B, S, NPAIR, S), F32).ap()
        k.pairs_stored = k.sem("box_pairs_stored")
        k.waves_stored = k.sem("box_waves_stored")
        k.x_loaded = k.sem("x_loaded")
        k.const_loaded = k.sem("const_loaded")
        k.weights_loaded = k.sem("weights_loaded")
        k.ctx_loaded = k.sem("ctx_loaded")
        k.rows_loaded = k.sem("rows_loaded")
        k.x_final = k.sem("x_final")
        scan_phase(nc, k, ins)
        cross_phase(nc, k)
        moe_phase(nc, k, ins)
        rotary_phase(nc, k)
        box_phase(nc, k, ins)
        chain_phase(nc, k, out)





def kernel(**inputs):
    import concourse.bacc as _bacc
    from concourse.bass_utils import run_bass_kernel_spmd as _run

    a = {n: np.asarray(v) for n, v in inputs.items()}
    pos = np.arange(S, dtype=np.float32)[:, None] * np.power(np.float32(10000.0), np.float32(2.0) * np.arange(
        HD // 2, dtype=np.float32) / np.float32(HD))[None, :]
    cos = np.tile(np.repeat(np.cos(pos), 2, 1), (1, H)).astype(np.float32)
    sin = np.tile(np.stack([-np.sin(pos), np.sin(pos)], -1).reshape(S, HD), (1, H)).astype(np.float32)
    minus = np.zeros((P, KB * H), np.float32)
    for part in range(3):
        minus[KB * H * part:KB * H * (part + 1)] = -np.eye(KB * H, dtype=np.float32)
    parts = {
        "A": a["L0_attn_A"], "A_T": a["L0_attn_A"].T, "Bm": a["L0_attn_Bm"], "W_ctx_T": a["L0_attn_W_ctx"].T,
        "wq0": a["L0_xattn_Wq"].T, "wk0": a["L0_xattn_Wk"].T, "wv0": a["L0_xattn_Wv"].T,
        "wo0": a["L0_xattn_Wo"].T, "gate": a["L0_ffn_gate_w"], "wq1": a["L1_attn_w_q"].T, "wk1": a["L1_attn_w_k"].T,
        "wv1": a["L1_attn_w_v"].T, "wo1": a["L1_attn_w_o"].T, "ffn1_T": a["L1_ffn_weight"].T,
        "ffn2": a["L1_ffn_aux_weight1"], "ffn3": a["L1_ffn_aux_weight2"],
        "bq0": a["L0_xattn_bq"], "bk0": a["L0_xattn_bk"], "minus": minus,
        "bq2": a["L1_xattn_bq"].reshape(NC, P).T, "bk2": a["L1_xattn_bk"].reshape(NC, P).T,
        "wq2": a["L1_xattn_Wq"].T, "wk2": a["L1_xattn_Wk"].T, "wv2": a["L1_xattn_Wv"].T,
        "wo2": a["L1_xattn_Wo"].T.reshape(NC, P, D).transpose(1, 0, 2).reshape(P, NC * D),
        "bv0": a["L0_xattn_bv"], "bo0": a["L0_xattn_bo"], "bo2": a["L1_xattn_bo"], "ffn_b": a["L1_ffn_bias"],
        "bv2": a["L1_xattn_bv"],
        "ident": np.eye(P, dtype=np.float32), "cos": cos.reshape(KB, P, D).transpose(1, 0, 2).reshape(P, KB * D),
        "sin": sin.reshape(KB, P, D).transpose(1, 0, 2).reshape(P, KB * D),
        "rank": np.tile(np.arange(E, 0, -1, dtype=np.float32), (P, 1)),
    }

    def pack(names, axis=1):
        return np.ascontiguousarray(np.concatenate([parts[n] for n, _ in names], axis))

    arrays = {
        "x": a["x"].reshape(T, D), "ctx_T": np.ascontiguousarray(a["ctx_1024"].reshape(T, D).T),
        "const": pack(CONSTS), "weights": pack(WEIGHTS), "wide": pack(WIDE), "rows": pack(ROWS, 0),
        "w1": a["L0_ffn_w1"], "w2": a["L0_ffn_w2"],
    }
    arrays.update(box_arrays(a))
    nc = _bacc.Bacc("TRN2", target_bir_lowering=False, num_devices=1)
    ins = {n: nc.dram_tensor(f"in_{n}", v.shape, mybir.dt.from_np(v.dtype), kind="ExternalInput").ap()
           for n, v in arrays.items()}
    out = nc.dram_tensor("out", (T, D), F32, kind="ExternalOutput").ap()
    decoder(nc, ins, out)
    r = _run(nc, [{f"in_{n}": v for n, v in arrays.items()}], core_ids=[0])
    return np.asarray(r.results[0]["out"]).reshape(B, S, D)
```
